# Optimizing a Trainium2 kernel written in Bass

```python
import numpy as np
import jax
import jax.numpy as jnp

def _softmax(x, axis=-1):
    return jax.nn.softmax(x, axis=axis)

def _gelu(x):
    return jax.nn.gelu(x, approximate=True)

def _silu(x):
    return jax.nn.silu(x)

def _sigmoid(x):
    return jax.nn.sigmoid(x)

def _layernorm(x, axis=-1, eps=1e-05):
    m = jnp.mean(x, axis=axis, keepdims=True)
    v = jnp.var(x, axis=axis, keepdims=True)
    return (x - m) / jnp.sqrt(v + eps)

def _scatter_add(tgt, idx, src, axis=0):
    return tgt.at[idx].add(src)

def _segment_sum(src, seg, n):
    return jax.ops.segment_sum(src, seg, n)
kernel_name = 'mk_seq_postln_d1_jaxref_r4_d61c99'

def setup_inputs(seed: int=0):
    np.random.seed(seed)
    _w = jnp.asarray

    def _L0_attn_setup():
        import jax, jax.numpy as jnp
        import numpy as np
        EMBED_DIM = 512
        HEAD_DIM = 128
        HALF = HEAD_DIM // 2
        NH2 = EMBED_DIM // HALF
        H = NH2 // 2
        DEPTH = 12
        LAMBDA_INIT = 0.8 - 0.6 * float(np.exp(-0.3 * DEPTH))
        SCALING = HEAD_DIM ** (-0.5)
        BATCH, SEQ = (1, 512)
        EPS = 1e-05

        def _rope_tables(t, dim):
            inv = 1.0 / 10000.0 ** (np.arange(0, dim, 2)[:dim // 2].astype(np.float64) / dim)
            ang = np.outer(np.arange(t), inv)
            return (jnp.asarray(np.cos(ang), jnp.float32), jnp.asarray(np.sin(ang), jnp.float32))

        def _apply_rope(x, cos, sin):
            xr, xi = (x[..., 0::2], x[..., 1::2])
            c = cos[None, :, None, :]
            s = sin[None, :, None, :]
            out = jnp.stack([xr * c - xi * s, xr * s + xi * c], axis=-1)
            return out.reshape(x.shape)
        key = jax.random.key(seed)
        ks = jax.random.split(key, 10)
        wstd = 0.25 / float(np.sqrt(EMBED_DIM))
        return {'x': jax.random.normal(ks[0], (BATCH, SEQ, EMBED_DIM), jnp.float32), 'wq': jax.random.normal(ks[1], (EMBED_DIM, EMBED_DIM), jnp.float32) * wstd, 'wk': jax.random.normal(ks[2], (EMBED_DIM, EMBED_DIM), jnp.float32) * wstd, 'wv': jax.random.normal(ks[3], (EMBED_DIM, EMBED_DIM), jnp.float32) * wstd, 'wout': jax.random.normal(ks[4], (EMBED_DIM, EMBED_DIM), jnp.float32) * wstd, 'lambda_q1': jax.random.normal(ks[5], (HALF,), jnp.float32) * 0.1, 'lambda_q2': jax.random.normal(ks[6], (HALF,), jnp.float32) * 0.1, 'lambda_k1': jax.random.normal(ks[7], (HALF,), jnp.float32) * 0.1, 'lambda_k2': jax.random.normal(ks[8], (HALF,), jnp.float32) * 0.1, 'subln_weight': jnp.ones((2 * HALF,), jnp.float32)}
    _L0_attn_in = _L0_attn_setup()

    def _L0_ffn_setup():
        import jax, jax.numpy as jnp
        import numpy as np
        B, T = (1, 128)
        DIM = 512
        MOE_INTER = 352
        N_EXPERTS = 64
        TOPK = 6
        N_SHARED = 2
        SHARED_INTER = N_SHARED * MOE_INTER
        CAPACITY = 128
        ROUTE_SCALE = 1.0
        key = jax.random.key(seed)
        ks = jax.random.split(key, 8)

        def w(k, shape, fan_in):
            return jax.random.normal(k, shape, jnp.float32) * fan_in ** (-0.5)
        return {'x': jax.random.normal(ks[0], (B, T, DIM), jnp.float32), 'gate_w': w(ks[1], (N_EXPERTS, DIM), DIM), 'w1': w(ks[2], (N_EXPERTS, MOE_INTER, DIM), DIM), 'w2': w(ks[3], (N_EXPERTS, DIM, MOE_INTER), MOE_INTER), 'w3': w(ks[4], (N_EXPERTS, MOE_INTER, DIM), DIM), 'sw1': w(ks[5], (SHARED_INTER, DIM), DIM), 'sw2': w(ks[6], (DIM, SHARED_INTER), SHARED_INTER), 'sw3': w(ks[7], (SHARED_INTER, DIM), DIM)}
    _L0_ffn_in = _L0_ffn_setup()
    _d = {'L0_attn_x': _L0_attn_in['x'], 'L0_attn_wq': _L0_attn_in['wq'], 'L0_attn_wk': _L0_attn_in['wk'], 'L0_attn_wv': _L0_attn_in['wv'], 'L0_attn_wout': _L0_attn_in['wout'], 'L0_attn_lambda_q1': _L0_attn_in['lambda_q1'], 'L0_attn_lambda_q2': _L0_attn_in['lambda_q2'], 'L0_attn_lambda_k1': _L0_attn_in['lambda_k1'], 'L0_attn_lambda_k2': _L0_attn_in['lambda_k2'], 'L0_attn_subln_weight': _L0_attn_in['subln_weight'], 'L0_ffn_gate_w': _L0_ffn_in['gate_w'], 'L0_ffn_w1': _L0_ffn_in['w1'], 'L0_ffn_w2': _L0_ffn_in['w2'], 'L0_ffn_w3': _L0_ffn_in['w3'], 'L0_ffn_sw1': _L0_ffn_in['sw1'], 'L0_ffn_sw2': _L0_ffn_in['sw2'], 'L0_ffn_sw3': _L0_ffn_in['sw3']}
    _x0 = _d['L0_attn_x']
    _d['L0_attn_x'] = jax.random.normal(jax.random.fold_in(jax.random.key(seed), 1), (8, 1024, 512), dtype=_x0.dtype)
    del _x0
    return _d

def reference(L0_attn_x, L0_attn_wq, L0_attn_wk, L0_attn_wv, L0_attn_wout, L0_attn_lambda_q1, L0_attn_lambda_q2, L0_attn_lambda_k1, L0_attn_lambda_k2, L0_attn_subln_weight, L0_ffn_gate_w, L0_ffn_w1, L0_ffn_w2, L0_ffn_w3, L0_ffn_sw1, L0_ffn_sw2, L0_ffn_sw3):

    def _L0_attn_ref(x, wq, wk, wv, wout, lambda_q1, lambda_q2, lambda_k1, lambda_k2, subln_weight):
        import jax, jax.numpy as jnp
        import numpy as np
        EMBED_DIM = 512
        HEAD_DIM = 128
        HALF = HEAD_DIM // 2
        NH2 = EMBED_DIM // HALF
        H = NH2 // 2
        DEPTH = 12
        LAMBDA_INIT = 0.8 - 0.6 * float(np.exp(-0.3 * DEPTH))
        SCALING = HEAD_DIM ** (-0.5)
        BATCH, SEQ = (1, 512)
        EPS = 1e-05

        def _rope_tables(t, dim):
            inv = 1.0 / 10000.0 ** (np.arange(0, dim, 2)[:dim // 2].astype(np.float64) / dim)
            ang = np.outer(np.arange(t), inv)
            return (jnp.asarray(np.cos(ang), jnp.float32), jnp.asarray(np.sin(ang), jnp.float32))

        def _apply_rope(x, cos, sin):
            xr, xi = (x[..., 0::2], x[..., 1::2])
            c = cos[None, :, None, :]
            s = sin[None, :, None, :]
            out = jnp.stack([xr * c - xi * s, xr * s + xi * c], axis=-1)
            return out.reshape(x.shape)
        b, t, e = x.shape
        q = (x @ wq.T).reshape(b, t, NH2, HALF)
        k = (x @ wk.T).reshape(b, t, NH2, HALF)
        v = (x @ wv.T).reshape(b, t, H, 2 * HALF)
        cos, sin = _rope_tables(t, HALF)
        q = _apply_rope(q, cos, sin)
        k = _apply_rope(k, cos, sin)
        q = q.transpose(0, 2, 1, 3)
        k = k.transpose(0, 2, 1, 3)
        v = v.transpose(0, 2, 1, 3)
        scores = jnp.einsum('bhtd,bhsd->bhts', q, k) / SCALING
        probs = jax.nn.softmax(scores, axis=-1)
        lam1 = jnp.exp(jnp.sum(lambda_q1 * lambda_k1))
        lam2 = jnp.exp(jnp.sum(lambda_q2 * lambda_k2))
        lam = lam1 - lam2 + LAMBDA_INIT
        probs = probs.reshape(b, H, 2, t, t)
        diff = probs[:, :, 0] - lam * probs[:, :, 1]
        attn = jnp.einsum('bhts,bhsd->bhtd', diff, v)
        attn = attn * jax.lax.rsqrt(jnp.mean(attn * attn, axis=-1, keepdims=True) + EPS)
        attn = attn * subln_weight
        attn = attn.transpose(0, 2, 1, 3).reshape(b, t, e)
        return attn @ wout.T

    def _L0_ffn_ref(x, gate_w, w1, w2, w3, sw1, sw2, sw3):
        import jax, jax.numpy as jnp
        import numpy as np
        B, T = (1, 128)
        DIM = 512
        MOE_INTER = 352
        N_EXPERTS = 64
        TOPK = 6
        N_SHARED = 2
        SHARED_INTER = N_SHARED * MOE_INTER
        CAPACITY = 128
        ROUTE_SCALE = 1.0
        Bb, Tt, D = x.shape
        xf = x.reshape(-1, D)
        N = xf.shape[0]
        logits = xf @ gate_w.T
        scores = jax.nn.softmax(logits, axis=-1)
        gate_vals, idx = jax.lax.top_k(scores, TOPK)
        gate_vals = gate_vals * ROUTE_SCALE
        E = gate_w.shape[0]
        fe = idx.reshape(-1)
        ft = jnp.repeat(jnp.arange(N), TOPK)
        onehot = (fe[:, None] == jnp.arange(E)[None, :]).astype(jnp.int32)
        pos = jnp.take_along_axis(jnp.cumsum(onehot, axis=0) - 1, fe[:, None], axis=1)[:, 0]
        keep = pos < CAPACITY
        buf = jnp.full((E, CAPACITY), N, dtype=jnp.int32)
        buf = buf.at[fe, pos].set(ft.astype(jnp.int32), mode='drop')
        xpad = jnp.concatenate([xf, jnp.zeros((1, D), xf.dtype)], axis=0)
        xe = xpad[buf]
        h = jax.nn.silu(jnp.einsum('ecd,eid->eci', xe, w1)) * jnp.einsum('ecd,eid->eci', xe, w3)
        ye = jnp.einsum('eci,edi->ecd', h, w2)
        pc = jnp.minimum(pos, CAPACITY - 1)
        op = ye[fe, pc] * keep[:, None].astype(ye.dtype)
        routed = (op * gate_vals.reshape(-1)[:, None]).reshape(N, TOPK, D).sum(axis=1)
        z = jax.nn.silu(xf @ sw1.T) * (xf @ sw3.T) @ sw2.T
        return (routed + z).reshape(Bb, Tt, D)
    x = L0_attn_x
    x = _layernorm(x + _L0_attn_ref(x, L0_attn_wq, L0_attn_wk, L0_attn_wv, L0_attn_wout, L0_attn_lambda_q1, L0_attn_lambda_q2, L0_attn_lambda_k1, L0_attn_lambda_k2, L0_attn_subln_weight), axis=-1)
    x = _layernorm(x + _L0_ffn_ref(x, L0_ffn_gate_w, L0_ffn_w1, L0_ffn_w2, L0_ffn_w3, L0_ffn_sw1, L0_ffn_sw2, L0_ffn_sw3), axis=-1)
    return x

_drawn_inputs = setup_inputs


def setup_inputs(seed=0):
    import zlib

    import numpy as np

    out = dict(_drawn_inputs(seed))
    spreads = {'L0_attn_subln_weight': (1.0, 0.2)}
    factors = {}
    for name, (base, spread) in spreads.items():
        noise = np.random.default_rng([zlib.crc32(name.encode()), seed]).standard_normal(out[name].shape)
        drawn = base * np.exp(spread * noise) if base else spread * noise
        out[name] = jnp.asarray(drawn.astype(out[name].dtype))
    for name, factor in factors.items():
        out[name] = (out[name] * factor).astype(out[name].dtype)
    return out
```

```python
from contextlib import ExitStack

import numpy as np

import concourse.bass as bass
from concourse import mybir

F32 = mybir.dt.float32
F32R = mybir.dt.float32r
BF16 = mybir.dt.bfloat16
I32 = mybir.dt.int32
U32 = mybir.dt.uint32
ALU = mybir.AluOpType
ACT = mybir.ActivationFunctionType
AX = mybir.AxisListType

P = 128
BATCH, SEQ, DIM = 8, 1024, 512
TOKENS = BATCH * SEQ
KD = DIM // P
HALF = 64
SUBS = DIM // HALF
HEADS = SUBS // 2
VD = 2 * HALF
FREQ = HALF // 2
GROUP = P // FREQ
LAMBDA_INIT = 0.8 - 0.6 * float(np.exp(-0.3 * 12))
SCALE = 1.0 / (128**-0.5)
EPS = 1e-5
EXPERTS, TOPK, CAP, INTER = 64, 6, 128, 352
SHARED = 704
CHUNK = 512
DMA = 16


class Stage:

    def __init__(self, nc, name):
        self.nc, self.name, self.stack = nc, name, ExitStack()

    def __enter__(self):
        return self

    def __exit__(self, *error):
        return self.stack.__exit__(*error)

    def sbuf(self, name, shape, dt=F32):
        return self.stack.enter_context(self.nc.sbuf_tensor(f"{self.name}_{name}", shape, dt))

    def psum(self, name, shape, dt=F32):
        return self.stack.enter_context(self.nc.psum_tensor(f"{self.name}_{name}", shape, dt))

    def sem(self, name):
        return self.stack.enter_context(self.nc.semaphore(f"{self.name}_{name}"))


def split_product(nc, out, lhs, rhs, first, last):
    nc.tensor.matmul(out, lhs[0], rhs[0], start=first, stop=False)
    nc.tensor.matmul(out, lhs[0], rhs[1], start=False, stop=False)
    return nc.tensor.matmul(out, lhs[1], rhs[0], start=False, stop=last)


def project(nc, x_t, w_qk, w_v, rope_plain, rope_cross, q_parts, k_parts, v_parts):
    x_view = x_t.rearrange("(k p) t -> p k t", p=P)
    with Stage(nc, "proj") as st:
        raw_w = st.sbuf("raw_w", [P, KD, 2 * DIM])
        wqk = [st.sbuf(f"wqk_{part}", [P, KD, 2 * DIM], F32R) for part in ("hi", "lo")]
        wv = [st.sbuf(f"wv_{part}", [P, KD, DIM], F32R) for part in ("hi", "lo")]
        plain = [st.sbuf(f"plain{i}", [P, 2, SEQ]) for i in range(2)]
        cross = [st.sbuf(f"cross{i}", [P, 2, SEQ]) for i in range(2)]
        x_raw = [st.sbuf(f"x_raw{i}", [P, KD, CHUNK]) for i in range(2)]
        x_hi = [st.sbuf(f"x_hi{i}", [P, KD, CHUNK], F32R) for i in range(2)]
        x_lo = [st.sbuf(f"x_lo{i}", [P, KD, CHUNK], F32R) for i in range(2)]
        by_real = [st.sbuf(f"by_real{i}", [P, 2, CHUNK]) for i in range(2)]
        by_imag = [st.sbuf(f"by_imag{i}", [P, 2, CHUNK]) for i in range(2)]
        turned = [st.sbuf(f"turned{i}", [P, 2, CHUNK]) for i in range(2)]
        out_hi = [st.sbuf(f"out_hi{i}", [P, 2, CHUNK], F32R) for i in range(2)]
        out_lo = [st.sbuf(f"out_lo{i}", [P, 2, CHUNK], F32R) for i in range(2)]
        v_out = [st.sbuf(f"v_out{i}", [P, HEADS, 2, VD], F32R) for i in range(2)]
        ps_qk = [st.psum(f"ps_qk{i}", [P, 2, CHUNK]) for i in range(2)]
        ps_v = [st.psum(f"ps_v{i}", [P, HEADS, VD]) for i in range(2)]

        w_qk_in, w_v_in, tables_in = st.sem("w_qk_in"), st.sem("w_v_in"), st.sem("tables_in")
        w_hi, w_lo = st.sem("w_hi"), st.sem("w_lo")
        x_in = [st.sem(f"x_in{i}") for i in range(2)]
        x_hi_done, x_lo_done = st.sem("x_hi_done"), st.sem("x_lo_done")
        qk_done, qk_read = st.sem("qk_done"), st.sem("qk_read")
        real_done, imag_done, turned_done = st.sem("real_done"), st.sem("imag_done"), st.sem("turned_done")
        hi_done, lo_done = st.sem("hi_done"), st.sem("lo_done")
        v_done, v_hi_done, v_lo_done = st.sem("v_done"), st.sem("v_hi_done"), st.sem("v_lo_done")
        qk_stored = [st.sem(f"qk_stored{i}") for i in range(2)]
        v_stored = [st.sem(f"v_stored{i}") for i in range(2)]

        PAIRS = 2 * SUBS // GROUP
        VT = CHUNK // P
        chunks = 2 * BATCH

        with nc.Block() as block:

            @block.sync
            def _(sp):
                sp.dma_start(raw_w[:], w_qk.rearrange("(k p) n -> p k n", p=P)).then_inc(w_qk_in, DMA)
                sp.dma_start(x_raw[0][:], x_view[:, :, 0:CHUNK]).then_inc(x_in[0], DMA)
                for i in range(2):
                    sp.dma_start(plain[i][:], rope_plain[i]).then_inc(tables_in, DMA)
                    sp.dma_start(cross[i][:], rope_cross[i]).then_inc(tables_in, DMA)
                sp.wait_ge(w_lo, 1)
                sp.dma_start(raw_w[:, :, 0:DIM], w_v.rearrange("(k p) n -> p k n", p=P)).then_inc(w_v_in, DMA)
                with sp.Fori(0, BATCH) as b:
                    for half in range(2):
                        c = 2 * b + half
                        nxt = 1 - half
                        sp.wait_ge(x_lo_done, c + 1)
                        at = ((c + 1) % chunks) * CHUNK
                        sp.dma_start(x_raw[nxt][:], x_view[:, :, bass.ds(at, CHUNK)]).then_inc(x_in[nxt], DMA)
                        for m in range(PAIRS):
                            parts = (q_parts, k_parts)[m // 2]
                            rows = slice(P * (m % 2), P * (m % 2) + P)
                            cols = slice(half * CHUNK, half * CHUNK + CHUNK)
                            sp.wait_ge(hi_done, PAIRS * c + m + 1)
                            for ri in range(2):
                                sp.dma_start(parts[b, 0, ri, rows, cols], out_hi[m % 2][:, ri, :].bitcast(F32)).then_inc(qk_stored[m % 2], DMA)
                            sp.wait_ge(lo_done, PAIRS * c + m + 1)
                            for ri in range(2):
                                sp.dma_start(parts[b, 1, ri, rows, cols], out_lo[m % 2][:, ri, :].bitcast(F32)).then_inc(qk_stored[m % 2], DMA)
                            sp.wait_ge(v_lo_done, VT * c + m + 1 + 2)
                            s0 = half * CHUNK + m * P
                            sp.dma_start(
                                v_parts[b, :, s0 : s0 + P, :].rearrange("h s c -> s h c"),
                                v_out[m % 2][:].rearrange("p h l c -> p h (l c)").bitcast(F32),
                            ).then_inc(v_stored[m % 2], DMA)
                for i in range(2):
                    sp.wait_ge(qk_stored[i], 4 * DMA * (PAIRS // 2 * chunks + 1))
                    sp.wait_ge(v_stored[i], DMA * (VT // 2 * chunks + 1))
                sp.wait_ge(x_in[0], DMA * (BATCH + 1))

            @block.scalar
            def _(act):
                act.sem_inc(qk_stored[0], 4 * DMA)
                act.sem_inc(qk_stored[1], 4 * DMA)
                act.sem_inc(v_stored[0], DMA)
                act.sem_inc(v_stored[1], DMA)
                act.wait_ge(w_qk_in, DMA)
                nc.scalar.copy(wqk[0][:], raw_w[:]).then_inc(w_hi, 1)
                act.wait_ge(x_in[0], DMA)
                nc.scalar.copy(x_hi[0][:], x_raw[0][:]).then_inc(x_hi_done, 1)
                act.wait_ge(w_v_in, DMA)
                nc.scalar.copy(wv[0][:], raw_w[:, :, 0:DIM]).then_inc(w_hi, 1)
                with act.Fori(0, BATCH) as b:
                    for half in range(2):
                        c = 2 * b + half
                        nxt = 1 - half
                        act.wait_ge(v_done, VT * (c + 2))
                        act.wait_ge(x_in[nxt], DMA * (b + 1 + half))
                        nc.scalar.copy(x_hi[nxt][:], x_raw[nxt][:]).then_inc(x_hi_done, 1)
                        for m in range(PAIRS):
                            n = PAIRS * c + m
                            act.wait_ge(turned_done, n + 1)
                            act.wait_ge(qk_stored[m % 2], 4 * DMA * (2 * c + m // 2 + 1))
                            nc.scalar.copy(out_hi[m % 2][:], turned[m % 2][:]).then_inc(hi_done, 1)
                            act.wait_ge(v_done, VT * (c + 2) + m + 1)
                            act.wait_ge(v_stored[m % 2], DMA * (2 * c + m // 2 + 1))
                            nc.scalar.copy(v_out[m % 2][:, :, 0, :], ps_v[m % 2][:]).then_inc(v_hi_done, 1)

            @block.vector
            def _(dve):
                dve.sem_inc(qk_read, 2)
                dve.sem_inc(v_lo_done, 2)
                dve.wait_ge(w_hi, 1)
                nc.vector.tensor_tensor(wqk[1][:], raw_w[:], wqk[0][:].bitcast(F32), ALU.subtract).then_inc(w_lo, 1)
                dve.wait_ge(x_hi_done, 1)
                nc.vector.tensor_tensor(x_lo[0][:], x_raw[0][:], x_hi[0][:].bitcast(F32), ALU.subtract).then_inc(x_lo_done, 1)
                dve.wait_ge(w_hi, 2)
                nc.vector.tensor_tensor(wv[1][:], raw_w[:, :, 0:DIM], wv[0][:].bitcast(F32), ALU.subtract).then_inc(w_lo, 1)
                dve.wait_ge(tables_in, 4 * DMA)

                def qk_low(c, m):
                    dve.wait_ge(hi_done, PAIRS * c + m + 1)
                    nc.vector.tensor_tensor(out_lo[m % 2][:], turned[m % 2][:], out_hi[m % 2][:].bitcast(F32), ALU.subtract).then_inc(lo_done, 1)

                def v_low(c, m):
                    dve.wait_ge(v_hi_done, VT * c + m + 1)
                    nc.vector.tensor_tensor(v_out[m % 2][:, :, 1, :], ps_v[m % 2][:], v_out[m % 2][:, :, 0, :].bitcast(F32), ALU.subtract).then_inc(v_lo_done, 1)

                with dve.Fori(0, BATCH) as b:
                    for half in range(2):
                        c = 2 * b + half
                        nxt = 1 - half
                        cols = slice(half * CHUNK, half * CHUNK + CHUNK)
                        for m in range(PAIRS):
                            n = PAIRS * c + m
                            i = m % 2
                            dve.wait_ge(qk_done, n + 1)
                            for src, table, dst, sem in ((0, plain, by_real, real_done), (1, cross, by_imag, imag_done)):
                                last = nc.vector.tensor_tensor(
                                    dst[i][:],
                                    ps_qk[i][:, src : src + 1, :].to_broadcast([P, 2, CHUNK]),
                                    table[m // 2][:, :, cols],
                                    ALU.mult,
                                ).then_inc(sem if src == 0 else qk_read, 1)
                            dve.wait_ge(real_done, n + 1)
                            dve.wait_ge(qk_read, n + 3)
                            nc.vector.tensor_tensor(turned[i][:], by_real[i][:], by_imag[i][:], ALU.add).then_inc(turned_done, 1)
                            if m:
                                qk_low(c, m - 1)
                                v_low(c, m - 1)
                            if m == 1:
                                dve.wait_ge(x_hi_done, c + 2)
                                nc.vector.tensor_tensor(x_lo[nxt][:], x_raw[nxt][:], x_hi[nxt][:].bitcast(F32), ALU.subtract).then_inc(x_lo_done, 1)
                        qk_low(c, PAIRS - 1)
                        v_low(c, PAIRS - 1)

            @block.tensor
            def _(pe):
                pe.sem_inc(v_done, 2 * VT)
                pe.wait_ge(w_lo, 2)
                with pe.Fori(0, BATCH) as b:
                    for half in range(2):
                        c = 2 * b + half
                        pe.wait_ge(x_lo_done, c + 1)
                        for m in range(PAIRS):
                            pe.wait_ge(qk_read, PAIRS * c + m + 1)
                            for ri in range(2):
                                cols = slice((2 * m + ri) * P, (2 * m + ri) * P + P)
                                for k in range(KD):
                                    last = split_product(
                                        nc, ps_qk[m % 2][:, ri, :],
                                        (wqk[0][:, k, cols], wqk[1][:, k, cols]),
                                        (x_hi[half][:, k, :], x_lo[half][:, k, :]),
                                        k == 0, k == KD - 1)
                            last.then_inc(qk_done, 1)
                            pe.wait_ge(v_lo_done, VT * c + m + 1)
                            toks = slice(m * P, m * P + P)
                            for k in range(KD):
                                last = split_product(
                                    nc, ps_v[m % 2][:],
                                    (x_hi[half][:, k, toks], x_lo[half][:, k, toks]),
                                    (wv[0][:, k, :], wv[1][:, k, :]),
                                    k == 0, k == KD - 1)
                            last.then_inc(v_done, 1)


def attend(nc, q_parts, k_parts, v_parts, x, lambdas, subln, w_out, gate_t, ident_in, before_in, empty_slots, x1, routed, slots):
    TILES = SEQ // P
    STEPS = HEADS * TILES
    LOADS_QK = 12
    BIG = 1.0e6
    with Stage(nc, "att") as st:
        q_buf = [st.sbuf(f"q{i}", [P, 2, SEQ], F32R) for i in range(2)]
        k_hi = [st.sbuf(f"k_hi{i}", [P, 2, SEQ], F32R) for i in range(2)]
        k_lo = [st.sbuf(f"k_lo{i}", [P, 2, SEQ], F32R) for i in range(2)]
        v_buf = [st.sbuf(f"v{i}", [P, TILES, 2 * VD], F32R) for i in range(2)]
        prob = [[st.sbuf(f"prob{s}{i}", [P, SEQ]) for i in range(2)] for s in range(2)]
        diff = [st.sbuf(f"diff{i}", [P, SEQ]) for i in range(2)]
        diff_hi = [st.sbuf(f"diff_hi{i}", [P, TILES, P], F32R) for i in range(2)]
        diff_lo = [st.sbuf(f"diff_lo{i}", [P, TILES, P], F32R) for i in range(2)]
        neg_max = st.sbuf("neg_max", [P, 2, 2])
        mass = st.sbuf("mass", [P, 2, 2])
        mass_inv = st.sbuf("mass_inv", [P, 2])
        weight2 = st.sbuf("weight2", [P, 2])
        lam_in = st.sbuf("lam_in", [P, 4, HALF])
        lam_prod = st.sbuf("lam_prod", [P, 2, HALF])
        lam_sum = st.sbuf("lam_sum", [P, 2])
        lam_exp = st.sbuf("lam_exp", [P, 2])
        lam_diff = st.sbuf("lam_diff", [P, 1])
        neg_lam = st.sbuf("neg_lam", [P, 1])
        cross_sum = st.sbuf("cross_sum", [P, VD])
        raw = st.sbuf("raw", [P, 2, TILES, HEADS, VD])
        squares = st.sbuf("squares", [P, 2, TILES, HEADS])
        eps_mass = st.sbuf("eps_mass", [P, 2, TILES, HEADS])
        square_junk = st.sbuf("square_junk", [P, VD])
        wo_raw = st.sbuf("wo_raw", [P, KD, DIM])
        wo = [st.sbuf(f"wo_{part}", [P, KD, DIM], F32R) for part in ("hi", "lo")]
        subln_col = st.sbuf("subln_col", [P, 1])
        gate_raw = st.sbuf("gate_raw", [P, KD, EXPERTS])
        gate = [st.sbuf(f"gate_{part}", [P, KD, EXPERTS], F32R) for part in ("hi", "lo")]
        ident = st.sbuf("ident", [P, P])
        before_f = st.sbuf("before_f", [P, P])
        before = st.sbuf("before", [P, P], BF16)
        ones = st.sbuf("ones", [P, P], BF16)
        zeros = st.sbuf("zeros", [P, DIM])
        iota_i = st.sbuf("iota_i", [P, EXPERTS], I32)
        iota = st.sbuf("iota", [P, EXPERTS])
        token_i = st.sbuf("token_i", [P, 1], I32)
        token = st.sbuf("token", [P, 1])
        pow_col = st.sbuf("pow_col", [P, HEADS])
        rms_sum = st.sbuf("rms_sum", [P, HEADS])
        rms_mean = st.sbuf("rms_mean", [P, HEADS])
        rms = st.sbuf("rms", [P, HEADS])
        normed = st.sbuf("normed", [P, HEADS, VD])
        heads_t = [st.sbuf(f"heads_t_{part}", [P, KD, P], F32R) for part in ("hi", "lo")]
        x_in = [st.sbuf(f"x_in{i}", [P, DIM]) for i in range(2)]
        summed = st.sbuf("summed", [P, DIM])
        stats = st.sbuf("stats", [P, 6])
        mean_var = st.sbuf("mean_var", [P, 2])
        var_eps = st.sbuf("var_eps", [P, 1])
        rstd = st.sbuf("rstd", [P, 1])
        shift = st.sbuf("shift", [P, 1])
        x1_buf = [st.sbuf(f"x1_{i}", [P, DIM]) for i in range(2)]
        x1_t = [st.sbuf(f"x1_t_{part}", [P, KD, P], F32R) for part in ("hi", "lo")]
        logit_max = st.sbuf("logit_max", [P, 1])
        score_exp = st.sbuf("score_exp", [P, EXPERTS])
        score_sum = st.sbuf("score_sum", [P, 1])
        score_inv = st.sbuf("score_inv", [P, 1])
        score = st.sbuf("score", [P, EXPERTS])
        top_val = st.sbuf("top_val", [P, 8])
        top_idx = st.sbuf("top_idx", [P, 8], U32)
        chosen = st.sbuf("chosen", [P, TOPK])
        hit = st.sbuf("hit", [P, TOPK, EXPERTS])
        mask_f = st.sbuf("mask_f", [P, EXPERTS])
        mask = st.sbuf("mask", [P, EXPERTS], BF16)
        mask_seen = st.sbuf("mask_seen", [P, EXPERTS], BF16)
        pos = st.sbuf("pos", [P, EXPERTS])
        hit_pos = st.sbuf("hit_pos", [P, TOPK, EXPERTS])
        pos_k = st.sbuf("pos_k", [P, TOPK])
        over = st.sbuf("over", [P, TOPK])
        slot_f = st.sbuf("slot_f", [P, TOPK])
        slot = st.sbuf("slot", [P, TOPK], I32)
        entry = st.sbuf("entry", [P, TOPK, 2])
        valid = st.sbuf("valid", [P, 1])
        room = st.sbuf("room", [P, 1])

        ps_s = [st.psum(f"ps_s{s}", [P, SEQ]) for s in range(2)]
        ps_t = st.psum("ps_t", [P, TILES, P])
        ps_o = st.psum("ps_o", [P, 512])
        ps_m = st.psum("ps_m", [P, 512])
        POS = slice(2 * VD, 2 * VD + EXPERTS)

        weights_in, lam_loaded, consts_in, pads_out = (st.sem(n) for n in ("weights_in", "lam_loaded", "consts_in", "pads_out"))
        held = st.sem("held")
        setup_pool, setup_dve, setup_act = st.sem("setup_pool"), st.sem("setup_dve"), st.sem("setup_act")
        qk_in = [st.sem(f"qk_in{i}") for i in range(2)]
        v_in = [st.sem(f"v_in{i}") for i in range(2)]
        s_done = [st.sem(f"s_done{s}") for s in range(2)]
        max_done = [st.sem(f"max_done{s}") for s in range(2)]
        exp_done = [st.sem(f"exp_done{s}") for s in range(2)]
        inv_done, weight_done, diff_done = st.sem("inv_done"), st.sem("weight_done"), st.sem("diff_done")
        t_done, hi_done, lo_done = st.sem("t_done"), st.sem("hi_done"), st.sem("lo_done")
        o_done, cross_done, raw_done, square_done = (st.sem(n) for n in ("o_done", "cross_done", "raw_done", "square_done"))
        rms_step, normed_done = st.sem("rms_step"), st.sem("normed_done")
        at_done, at_hi_done, at_lo_done = st.sem("at_done"), st.sem("at_hi_done"), st.sem("at_lo_done")
        x_loaded = [st.sem(f"x_loaded{i}") for i in range(2)]
        y_done, sum_done, stats_done, mv_done = (st.sem(n) for n in ("y_done", "sum_done", "stats_done", "mv_done"))
        ln_step, ln_done, x1_done = st.sem("ln_step"), st.sem("ln_done"), st.sem("x1_done")
        x1_stored = [st.sem(f"x1_stored{i}") for i in range(2)]
        xt_done, xt_hi_done, xt_lo_done = st.sem("xt_done"), st.sem("xt_hi_done"), st.sem("xt_lo_done")
        gate_done, lmax_done, score_done = st.sem("gate_done"), st.sem("lmax_done"), st.sem("score_done")
        route_step, mask_done, pos_done, pos_read = (st.sem(n) for n in ("route_step", "mask_done", "pos_done", "pos_read"))
        slot_step, slot_done, scattered, entry_free = (st.sem(n) for n in ("slot_step", "slot_done", "scattered", "entry_free"))

        SETUP_DVE = 14
        NORMED_CREDIT = 2 * TILES
        ROUTE_STEPS, SLOT_STEPS, RMS_STEPS, LN_STEPS = 8, 6, 3, 2

        def of_lag(b, jl, lag):
            jj = jl - lag
            bb = b if jj >= 0 else b - 1
            jj = jj % STEPS
            return bb, jj // TILES, jj % TILES, bb * STEPS + jj

        def turns(attn, out, first, lag_max=4):
            for jl in range(STEPS):
                live = {lag: (jl >= lag if first else (attn or jl < lag)) for lag in range(lag_max + 1)}
                yield jl, live, (jl // 4, jl % 4) if out else (None, None)

        def sp_turns(sp, b, attn, out, first):
            for jl, live, (k, piece) in turns(attn, out, first):
                h, t = jl // TILES, jl % TILES
                if attn:
                    nb, nh = (b, h + 1) if h + 1 < HEADS else (b + 1, 0)
                    i = nh % 2
                    skip = first and h == 0
                    if t == 1:
                        if not skip:
                            sp.wait_ge(s_done[1], STEPS * b + TILES * h)
                        load_qk(sp, nb, nh, i)
                    if t == 5:
                        if not skip:
                            sp.wait_ge(o_done, STEPS * b + TILES * h)
                        load_v(sp, nb, nh, i)
                if out:
                    n = TILES * (b - 1) + k
                    if piece == 0:
                        sp.wait_ge(sum_done, n + 1)
                        sp.dma_start(x_in[k % 2][:], x[bass.ds(n * P, P), :]).then_inc(x_loaded[k % 2], DMA)
                    if piece == 2:
                        sp.wait_ge(x1_done, n + 2)
                        sp.dma_start(x1[bass.ds(n * P, P), :], x1_buf[k % 2][:]).then_inc(x1_stored[k % 2], DMA)
                        sp.dma_start(routed[bass.ds(n * P, P), :], x1_buf[k % 2][:]).then_inc(x1_stored[k % 2], DMA)

        def load_qk(sp, b, h, i):
            if isinstance(b, int) and b >= BATCH:
                return
            if not isinstance(b, int) and h == 0:
                b = b % BATCH
            src = slice(2 * h * FREQ, (2 * h + 2) * FREQ)
            for part in range(2):
                for ri in range(2):
                    def rows(parts, p):
                        return parts[b, p, ri, src, :].rearrange("(s f) t -> f s t", s=2)

                    at = 2 * part * FREQ + ri * FREQ
                    sp.dma_start(q_buf[i][at : at + FREQ].bitcast(F32), rows(q_parts, part)).then_inc(qk_in[i], DMA)
                    sp.dma_start(k_hi[i][at : at + FREQ].bitcast(F32), rows(k_parts, 0)).then_inc(qk_in[i], DMA)
                    sp.dma_start(k_lo[i][at : at + FREQ].bitcast(F32), rows(k_parts, 1)).then_inc(qk_in[i], DMA)

        def load_v(sp, b, h, i):
            if not isinstance(b, int) and h == 0:
                b = b % BATCH
            sp.dma_start(v_buf[i][:].bitcast(F32), v_parts[b, h].rearrange("(t p) c -> p t c", p=P)).then_inc(v_in[i], DMA)

        def pe_turns(pe, b, attn, out, first):
            for jl, live, (k, piece) in turns(attn, out, first):
                if attn:
                    h, t, j = jl // TILES, jl % TILES, STEPS * b + jl
                    if t == 0:
                        pe.wait_ge(qk_in[h % 2], DMA * LOADS_QK * (2 * b + h // 2 + 1))
                    q_cols = slice(t * P, t * P + P)
                    for s in range(2):
                        if not (first and jl == 0):
                            pe.wait_ge(exp_done[s], j)
                        for half in range(2):
                            cols = slice(half * CHUNK, half * CHUNK + CHUNK)
                            nc.tensor.matmul(ps_s[s][:, cols], q_buf[h % 2][:, s, q_cols], k_hi[h % 2][:, s, cols], start=True, stop=False)
                            last = nc.tensor.matmul(ps_s[s][:, cols], q_buf[h % 2][:, s, q_cols], k_lo[h % 2][:, s, cols], start=False, stop=True)
                        last.then_inc(s_done[s], 1)
                if out:
                    n = TILES * (b - 1) + k
                    pe_piece(pe, n, piece, k)
                if live[2]:
                    _, _, _, j = of_lag(b, jl, 2)
                    pe.wait_ge(diff_done, j + 1)
                    if not (first and jl == 2):
                        pe.wait_ge(lo_done, j)
                    for t in range(TILES):
                        last = nc.tensor.transpose(ps_t[:, t, :], diff[jl % 2][:, t * P : t * P + P], ident[:])
                    last.then_inc(t_done, 1)
                if live[3]:
                    bb, h, t, j = of_lag(b, jl, 3)
                    if t == 0:
                        pe.wait_ge(v_in[h % 2], DMA * (2 * bb + h // 2 + 1))
                    pe.wait_ge(lo_done, j + 1)
                    if not (first and jl == 3):
                        pe.wait_ge(raw_done, j)
                    if out and piece == 1:
                        pe_positions(pe, TILES * (b - 1) + k - 1)
                    i = (jl - 3) % 2
                    for t in range(TILES):
                        nc.tensor.matmul(ps_o[:, 0 : 2 * VD], diff_hi[i][:, t, :], v_buf[h % 2][:, t, :], start=t == 0, stop=False)
                        last = nc.tensor.matmul(ps_o[:, 0 : 2 * VD], diff_lo[i][:, t, :], v_buf[h % 2][:, t, :], start=False, stop=t == TILES - 1)
                    last.then_inc(o_done, 1)
                elif out and piece == 1:
                    pe.wait_ge(raw_done, STEPS * BATCH)
                    pe_positions(pe, TILES * (b - 1) + k - 1)

        def pe_positions(pe, n):
            pe.wait_ge(mask_done, n + 2)
            nc.tensor.matmul(ps_o[:, POS], before[:], mask[:], start=True, stop=False)
            nc.tensor.matmul(ps_o[:, POS], ones[:], mask_seen[:], start=False, stop=True).then_inc(pos_done, 1)

        def pe_piece(pe, n, piece, k):
            if piece == 0:
                pe.wait_ge(normed_done, NORMED_CREDIT + n + 1)
                pe.wait_ge(score_done, n + 1)
                for h in range(HEADS):
                    last = nc.tensor.transpose(ps_m[:, h * P : h * P + P], normed[:, h, :], ident[:])
                last.then_inc(at_done, 1)
            if piece == 1:
                pe.wait_ge(at_lo_done, n + 1)
                for e in range(KD):
                    last = split_product(nc, ps_m[:], (heads_t[0][:, e, :], heads_t[1][:, e, :]), (wo[0][:, e, :], wo[1][:, e, :]), e == 0, e == KD - 1)
                last.then_inc(y_done, 1)
            if piece == 2:
                pe.wait_ge(x1_done, n + 2)
                for c in range(KD):
                    last = nc.tensor.transpose(ps_m[:, c * P : c * P + P], x1_buf[k % 2][:, c * P : c * P + P], ident[:])
                last.then_inc(xt_done, 1)
            if piece == 3:
                pe.wait_ge(xt_lo_done, n + 1)
                for c in range(KD):
                    last = split_product(nc, ps_m[:, 0:EXPERTS], (x1_t[0][:, c, :], x1_t[1][:, c, :]), (gate[0][:, c, :], gate[1][:, c, :]), c == 0, c == KD - 1)
                last.then_inc(gate_done, 1)

        def act_turns(act, b, attn, out, first):
            for jl, live, (k, piece) in turns(attn, out, first):
                n = TILES * (b - 1) + k if out else None
                if live[4]:
                    _, _, _, j = of_lag(b, jl, 4)
                    act.wait_ge(o_done, j + 1)
                    nc.scalar.copy(cross_sum[:], ps_o[:, VD : 2 * VD]).then_inc(cross_done, 1)
                if out and piece == 0:
                    act.wait_ge(at_done, n + 2)
                    act.wait_ge(y_done, n + 1)
                    nc.scalar.copy(heads_t[0][:], ps_m[:].rearrange("p (h t) -> p h t", t=P)).then_inc(at_hi_done, 1)
                if attn:
                    exp(act, b, jl, 0, first)
                if out and piece == 2:
                    act.wait_ge(xt_done, n + 1)
                    act.wait_ge(gate_done, n + 1)
                    nc.scalar.copy(x1_t[0][:], ps_m[:].rearrange("p (h t) -> p h t", t=P)).then_inc(xt_hi_done, 1)
                if attn:
                    exp(act, b, jl, 1, first)
                if live[2]:
                    _, _, _, j = of_lag(b, jl, 2)
                    act.wait_ge(t_done, j + 1)
                    if not (first and jl < 4):
                        act.wait_ge(o_done, j - 1)
                    nc.scalar.copy(diff_hi[jl % 2][:], ps_t[:]).then_inc(hi_done, 1)
                if live[4]:
                    bb, h, t, j = of_lag(b, jl, 4)
                    act.wait_ge(raw_done, j + 1)
                    if not (first and jl == 4):
                        act.wait_ge(square_done, j)
                    par = bb % 2
                    nc.scalar.activation(square_junk[:], raw[:, par, t, h, :], ACT.Square, accum_out=squares[:, par, t, h : h + 1]).then_inc(square_done, 1)
                if out and piece == 1:
                    act.wait_ge(ln_done, n + 1)
                    act.wait_ge(x1_stored[k % 2], 2 * DMA * (TILES // 2 * (b - 1) + k // 2 + 1))
                    nc.scalar.activation(x1_buf[k % 2][:], summed[:], ACT.Identity, bias=shift[:], scale=rstd[:]).then_inc(x1_done, 1)
                if out and piece == 3:
                    act.wait_ge(lmax_done, n + 1)
                    act.wait_ge(slot_done, n + 1)
                    nc.scalar.activation(score_exp[:], ps_m[:, 0:EXPERTS], ACT.Exp, bias=logit_max[:], accum_out=score_sum[:]).then_inc(score_done, 1)

        def exp(act, b, jl, s, first):
            j = STEPS * b + jl
            act.wait_ge(max_done[s], j + 1)
            if not (first and jl < 2):
                act.wait_ge(diff_done, j - 1)
            i = jl % 2
            nc.scalar.activation(prob[s][i][:], ps_s[s][:], ACT.Exp, bias=neg_max[:, s, i : i + 1], accum_out=mass[:, s, i : i + 1]).then_inc(exp_done[s], 1)

        def dve_turns(dve, b, attn, out, first):
            for jl, live, (k, piece) in turns(attn, out, first):
                n = TILES * (b - 1) + k if out else None
                j = STEPS * b + jl
                if attn:
                    row_max(dve, j, 0, jl % 2)
                if live[4]:
                    bb, h, t, j4 = of_lag(b, jl, 4)
                    dve.wait_ge(cross_done, j4 + 1)
                    if out and piece == 2:
                        read_positions(dve, n - 1)
                    par = bb % 2
                    nc.vector.tensor_tensor(raw[:, par, t, h, :], ps_o[:, 0:VD], cross_sum[:], ALU.add).then_inc(raw_done, 1)
                if attn:
                    row_max(dve, j, 1, jl % 2)
                if out and piece == 0:
                    dve.wait_ge(at_hi_done, n + 1)
                    nc.vector.tensor_tensor(heads_t[1][:], ps_m[:].rearrange("p (h t) -> p h t", t=P), heads_t[0][:].bitcast(F32), ALU.subtract).then_inc(at_lo_done, 1)
                if out and piece == 1:
                    dve.wait_ge(y_done, n + 2)
                    dve.wait_ge(x_loaded[k % 2], DMA * (TILES // 2 * (b - 1) + k // 2 + 1))
                    dve.wait_ge(x1_done, n + 1)
                    nc.vector.tensor_tensor(summed[:], ps_m[:], x_in[k % 2][:], ALU.add).then_inc(sum_done, 1)
                    dve.wait_ge(sum_done, n + 3)
                    nc.vector.bn_stats(stats[:], summed[:]).then_inc(stats_done, 1)
                    dve.wait_ge(stats_done, n + 1)
                    dve.sem_inc(held, 1)
                    nc.vector.bn_aggr(mean_var[:], stats[:]).then_inc(mv_done, 1)
                if out and piece == 2:
                    dve.wait_ge(xt_hi_done, n + 1)
                    nc.vector.tensor_tensor(x1_t[1][:], ps_m[:].rearrange("p (h t) -> p h t", t=P), x1_t[0][:].bitcast(F32), ALU.subtract).then_inc(xt_lo_done, 1)
                if live[1]:
                    softmax_difference(dve, b, jl, first)
                if live[2]:
                    _, _, _, j2 = of_lag(b, jl, 2)
                    dve.wait_ge(hi_done, j2 + 1)
                    nc.vector.tensor_tensor(diff_lo[jl % 2][:], ps_t[:], diff_hi[jl % 2][:].bitcast(F32), ALU.subtract).then_inc(lo_done, 1)
                if out and piece == 0:
                    route(dve, n - 1)
                if out and piece == 2:
                    if not live[4]:
                        read_positions(dve, n - 1)
                    find_slots(dve, n - 1)
                    if k == 0:
                        nc.vector.memset(valid[:], 1.0)
                        nc.vector.memset(room[:], float(CAP)).then_inc(setup_dve, 1)
                        dve.wait_ge(setup_dve, SETUP_DVE + b)
                if out and piece == 3:
                    dve.wait_ge(gate_done, n + 2)
                    nc.vector.tensor_reduce(logit_max[:], ps_m[:, 0:EXPERTS], AX.X, ALU.max, negate=True).then_inc(lmax_done, 1)

        def read_positions(dve, n):
            dve.wait_ge(pos_done, n + 2)
            nc.vector.tensor_copy(pos[:], ps_o[:, POS]).then_inc(pos_read, 1)

        def row_max(dve, j, s, i):
            dve.wait_ge(s_done[s], j + 1)
            nc.vector.tensor_reduce(neg_max[:, s, i : i + 1], ps_s[s][:], AX.X, ALU.max, negate=True).then_inc(max_done[s], 1)

        def softmax_difference(dve, b, jl, first):
            bb, h, t, j = of_lag(b, jl, 1)
            i = (jl - 1) % 2
            par = bb % 2
            dve.wait_ge(exp_done[1], j + 1)
            nc.vector.reciprocal(mass_inv[:, i : i + 1], mass[:, 1, i : i + 1]).then_inc(inv_done, 1)
            dve.wait_ge(normed_done, TILES * bb + t + 1)
            nc.vector.tensor_scalar(eps_mass[:, par, t, h : h + 1], mass[:, 0, i : i + 1], VD * EPS, mass[:, 0, i : i + 1], ALU.mult, ALU.mult)
            dve.wait_ge(inv_done, j + 1)
            nc.vector.tensor_scalar(weight2[:, i : i + 1], mass_inv[:, i : i + 1], mass[:, 0, i : i + 1], neg_lam[:], ALU.mult, ALU.mult).then_inc(weight_done, 1)
            dve.wait_ge(weight_done, j + 1)
            if not (first and jl < 3):
                dve.wait_ge(t_done, j - 1)
            nc.vector.scalar_tensor_tensor(diff[i][:], prob[1][i][:], weight2[:, i : i + 1], prob[0][i][:], ALU.mult, ALU.add).then_inc(diff_done, 1)

        def route(dve, n):
            at = [ROUTE_STEPS * (n + 1)]

            def step(ins):
                at[0] += 1
                ins.then_inc(route_step, 1)
                dve.wait_ge(route_step, at[0])

            dve.wait_ge(score_done, n + 2)
            step(nc.vector.reciprocal(score_inv[:], score_sum[:]))
            step(nc.vector.tensor_scalar(score[:], score_exp[:], score_inv[:], None, ALU.mult))
            dve.sem_inc(held, 1)
            step(nc.vector.max(top_val[:], score[:]))
            dve.sem_inc(held, 1)
            step(nc.vector.max_index(top_idx[:], top_val[:], score[:]))
            step(nc.vector.tensor_copy(chosen[:], top_idx[:, 0:TOPK]))
            step(nc.vector.tensor_tensor(
                hit[:], iota[:].unsqueeze(1).to_broadcast([P, TOPK, EXPERTS]),
                chosen[:].unsqueeze(2).to_broadcast([P, TOPK, EXPERTS]), ALU.is_equal))
            step(nc.vector.tensor_reduce(mask_f[:], hit[:].rearrange("p k e -> p e k"), AX.X, ALU.add))
            step(nc.vector.tensor_scalar(mask[:], mask_f[:], valid[:], None, ALU.mult))
            dve.wait_ge(entry_free, n + 2)
            nc.vector.tensor_copy(entry[:, :, 1], top_val[:, 0:TOPK])
            nc.vector.tensor_copy(entry[:, :, 0], token[:].to_broadcast([P, TOPK])).then_inc(mask_done, 1)

        def find_slots(dve, n):
            at = [SLOT_STEPS * (n + 1)]

            def step(ins):
                at[0] += 1
                ins.then_inc(slot_step, 1)
                dve.wait_ge(slot_step, at[0])

            dve.wait_ge(pos_read, n + 2)
            dve.wait_ge(mask_done, n + 2)
            step(nc.vector.tensor_tensor(hit_pos[:], hit[:], pos[:].unsqueeze(1).to_broadcast([P, TOPK, EXPERTS]), ALU.mult))
            step(nc.vector.tensor_reduce(pos_k[:], hit_pos[:], AX.X, ALU.add))
            step(nc.vector.tensor_scalar(over[:], pos_k[:], room[:], BIG, ALU.is_ge, ALU.mult))
            step(nc.vector.scalar_tensor_tensor(slot_f[:], chosen[:], float(CAP), pos_k[:], ALU.mult, ALU.add))
            step(nc.vector.tensor_tensor(slot[:], slot_f[:], over[:], ALU.add))
            step(nc.vector.tensor_tensor(mask_seen[:], mask_seen[:], mask[:], ALU.add))
            nc.vector.tensor_scalar_add(token[:], token[:], float(P)).then_inc(slot_done, 1)

        def pool_tiles(pool, b):
            for k in range(TILES):
                n = TILES * (b - 1) + k
                j = STEPS * (b - 1) + TILES * (HEADS - 1) + k
                par = (b - 1) % 2
                pool.wait_ge(square_done, j + 1)
                pool.wait_ge(diff_done, j + 1)
                nc.gpsimd.tensor_tensor(rms_sum[:], squares[:, par, k, :], eps_mass[:, par, k, :], ALU.add).then_inc(rms_step, 1)
                pool.wait_ge(rms_step, RMS_STEPS * n + 1)
                pool.sem_inc(held, 1)
                nc.gpsimd.tensor_scalar(rms_mean[:], rms_sum[:], 1.0 / VD, 0.0, ALU.mult, ALU.add).then_inc(rms_step, 1)
                pool.wait_ge(rms_step, RMS_STEPS * n + 2)
                nc.gpsimd.tensor_tensor(rms[:], rms_mean[:], pow_col[:], ALU.pow).then_inc(rms_step, 1)
                pool.wait_ge(rms_step, RMS_STEPS * n + 3)
                pool.wait_ge(at_done, n + 1)
                nc.gpsimd.tensor_tensor(normed[:], raw[:, par, k, :, :], rms[:].unsqueeze(2).to_broadcast([P, HEADS, VD]), ALU.mult).then_inc(normed_done, 1)
                pool.wait_ge(mv_done, n + 1)
                pool.wait_ge(x1_done, n + 1)
                pool.sem_inc(held, 1)
                nc.gpsimd.tensor_scalar(var_eps[:], mean_var[:, 1:2], EPS, 1.0, ALU.add, ALU.mult).then_inc(ln_step, 1)
                pool.wait_ge(ln_step, LN_STEPS * n + 1)
                nc.gpsimd.tensor_tensor(rstd[:], var_eps[:], pow_col[:, 0:1], ALU.pow).then_inc(ln_step, 1)
                pool.wait_ge(ln_step, LN_STEPS * n + 2)
                pool.sem_inc(held, 1)
                nc.gpsimd.tensor_scalar(shift[:], mean_var[:, 0:1], rstd[:], -1.0, ALU.mult, ALU.mult).then_inc(ln_done, 1)
                pool_scatter(pool, n - 1)

        def pool_scatter(pool, n):
            pool.wait_ge(slot_done, n + 2)
            pool.sem_inc(held, 1)
            for c in range(TOPK):
                nc.gpsimd.indirect_dma_start(
                    slots, bass.IndirectOffsetOnAxis(ap=slot[:, c : c + 1], axis=0), entry[:, c, :], None,
                    bounds_check=EXPERTS * CAP - 1, oob_is_err=False,
                ).then_inc(scattered, DMA)
            pool.wait_ge(scattered, DMA * TOPK * (n + 2))
            pool.sem_inc(entry_free, 1)

        with nc.Block() as block:

            @block.sync
            def _(sp):
                load_qk(sp, 0, 0, 0)
                sp.dma_start(ident[:], ident_in).then_inc(consts_in, DMA)
                sp.dma_start(before_f[:], before_in).then_inc(consts_in, DMA)
                sp.dma_start(lam_in[:], lambdas.partition_broadcast(P)).then_inc(lam_loaded, DMA)
                load_v(sp, 0, 0, 0)
                sp.dma_start(wo_raw[:], w_out.rearrange("(k p) n -> p k n", p=P)).then_inc(weights_in, DMA)
                sp.dma_start(gate_raw[:], gate_t.rearrange("(k p) n -> p k n", p=P)).then_inc(weights_in, DMA)
                sp.dma_start(subln_col[:], subln).then_inc(weights_in, DMA)
                sp.dma_start(slots, empty_slots).then_inc(pads_out, DMA)
                sp.wait_ge(setup_pool, 7)
                sp.dma_start(x1[TOKENS : TOKENS + CAP, :], zeros[:]).then_inc(pads_out, DMA)
                sp.dma_start(routed[TOKENS : TOKENS + CAP, :], zeros[:]).then_inc(pads_out, DMA)
                sp_turns(sp, 0, True, False, True)
                with sp.Fori(1, BATCH) as b:
                    sp_turns(sp, b, True, True, False)
                sp_turns(sp, BATCH, False, True, False)
                sp.wait_ge(qk_in[0], DMA * LOADS_QK * (BATCH * HEADS // 2 + 1))
                sp.wait_ge(v_in[0], DMA * (BATCH * HEADS // 2 + 1))
                sp.wait_ge(pads_out, 3 * DMA)
                for i in range(2):
                    sp.wait_ge(x1_stored[i], 2 * DMA * (TOKENS // P // 2 + 1))
                sp.wait_ge(scattered, DMA * TOPK * (TOKENS // P + 1))

            @block.tensor
            def _(pe):
                pe.sem_inc(at_done, 1)
                pe.sem_inc(y_done, 1)
                pe.sem_inc(gate_done, 1)
                pe.wait_ge(consts_in, 2 * DMA)
                pe_turns(pe, 0, True, False, True)
                pe.wait_ge(setup_dve, SETUP_DVE)
                with pe.Fori(1, BATCH) as b:
                    pe_turns(pe, b, True, True, False)
                pe_turns(pe, BATCH, False, True, False)
                pe_positions(pe, TOKENS // P - 1)

            @block.scalar
            def _(act):
                act.sem_inc(x1_done, 1)
                act.sem_inc(score_done, 1)
                act.sem_inc(x1_stored[0], 2 * DMA)
                act.sem_inc(x1_stored[1], 2 * DMA)
                act.wait_ge(setup_dve, 2)
                nc.scalar.activation(lam_exp[:], lam_sum[:], ACT.Exp).then_inc(setup_act, 1)
                act.wait_ge(setup_dve, 5)
                nc.scalar.copy(wo[0][:], wo_raw[:]).then_inc(setup_act, 1)
                nc.scalar.copy(gate[0][:], gate_raw[:]).then_inc(setup_act, 1)
                act_turns(act, 0, True, False, True)
                with act.Fori(1, BATCH) as b:
                    act_turns(act, b, True, True, False)
                act_turns(act, BATCH, False, True, False)

            @block.vector
            def _(dve):
                dve.sem_inc(sum_done, 2)
                dve.wait_ge(lam_loaded, DMA)
                nc.vector.tensor_tensor(lam_prod[:], lam_in[:, 0:2, :], lam_in[:, 2:4, :], ALU.mult).then_inc(setup_dve, 1)
                dve.wait_ge(setup_dve, 1)
                nc.vector.tensor_reduce(lam_sum[:], lam_prod[:], AX.X, ALU.add).then_inc(setup_dve, 1)
                dve.wait_ge(setup_act, 1)
                nc.vector.tensor_tensor(lam_diff[:], lam_exp[:, 1:2], lam_exp[:, 0:1], ALU.subtract).then_inc(setup_dve, 1)
                dve.wait_ge(setup_dve, 3)
                nc.vector.tensor_scalar_add(neg_lam[:], lam_diff[:], -LAMBDA_INIT).then_inc(setup_dve, 1)
                dve.wait_ge(weights_in, 3 * DMA)
                nc.vector.tensor_scalar(wo_raw[:], wo_raw[:], subln_col[:], None, ALU.mult).then_inc(setup_dve, 1)
                dve.wait_ge(setup_act, 3)
                nc.vector.tensor_tensor(wo[1][:], wo_raw[:], wo[0][:].bitcast(F32), ALU.subtract).then_inc(setup_dve, 1)
                nc.vector.tensor_tensor(gate[1][:], gate_raw[:], gate[0][:].bitcast(F32), ALU.subtract).then_inc(setup_dve, 1)
                dve.wait_ge(consts_in, 2 * DMA)
                nc.vector.tensor_copy(before[:], before_f[:]).then_inc(setup_dve, 1)
                nc.vector.memset(ones[:], 1.0).then_inc(setup_dve, 1)
                nc.vector.memset(mask_seen[:], 0.0).then_inc(setup_dve, 1)
                nc.vector.memset(valid[:], 0.0).then_inc(setup_dve, 1)
                nc.vector.memset(room[:], 0.0).then_inc(setup_dve, 1)
                dve.wait_ge(setup_pool, 7)
                nc.vector.tensor_copy(iota[:], iota_i[:]).then_inc(setup_dve, 1)
                nc.vector.tensor_copy(token[:], token_i[:]).then_inc(setup_dve, 1)
                dve.wait_ge(setup_dve, SETUP_DVE)
                dve_turns(dve, 0, True, False, True)
                with dve.Fori(1, BATCH) as b:
                    dve_turns(dve, b, True, True, False)
                dve_turns(dve, BATCH, False, True, False)
                n = TOKENS // P - 1
                route(dve, n)
                read_positions(dve, n)
                find_slots(dve, n)

            @block.gpsimd
            def _(pool):
                pool.sem_inc(normed_done, NORMED_CREDIT)
                pool.sem_inc(entry_free, 1)
                nc.gpsimd.memset(zeros[:], 0.0).then_inc(setup_pool, 1)
                nc.gpsimd.memset(pow_col[:], -0.5).then_inc(setup_pool, 1)
                nc.gpsimd.memset(score_exp[:], 1.0).then_inc(setup_pool, 1)
                nc.gpsimd.memset(score_sum[:], 1.0).then_inc(setup_pool, 1)
                nc.gpsimd.iota(iota_i[:], [[1, EXPERTS]], base=0, channel_multiplier=0).then_inc(setup_pool, 1)
                nc.gpsimd.iota(token_i[:], [[0, 1]], base=-P, channel_multiplier=1).then_inc(setup_pool, 1)
                nc.gpsimd.memset(square_junk[:], 0.0).then_inc(setup_pool, 1)
                pool.wait_ge(setup_pool, 7)
                pool.wait_ge(pads_out, 3 * DMA)
                with pool.Fori(1, BATCH + 1) as b:
                    pool_tiles(pool, b)
                pool_scatter(pool, TOKENS // P - 1)


def experts(nc, x1, slots, w13_t, w2_t, sw13_t, sw2_t, ident_in, routed, shared_out):
    FULL = SHARED // P
    REST = SHARED - FULL * P
    UNITS = FULL + 1
    GROUPS = TOKENS // CHUNK
    PER = EXPERTS // GROUPS
    TT = CHUNK // P
    HT = -(-INTER // P)
    LAST = INTER - (HT - 1) * P
    W_LOADS = 3
    assert REST == HALF
    with Stage(nc, "exp") as st:
        sw13 = [st.sbuf(f"sw13_{part}", [P, KD, 2 * SHARED], F32R) for part in ("hi", "lo")]
        sw2 = [st.sbuf(f"sw2_{part}", [P, UNITS, DIM], F32R) for part in ("hi", "lo")]
        w13 = [st.sbuf(f"w13_{i}", [P, KD, 2 * INTER]) for i in range(2)]
        w2 = [st.sbuf(f"w2_{i}", [P, HT, DIM]) for i in range(2)]
        ident = st.sbuf("ident", [P, P])
        x_in = st.sbuf("x_in", [P, TT, DIM])
        x_t = [st.sbuf(f"x_t_{part}", [P, KD, CHUNK], F32R) for part in ("hi", "lo")]
        silu = [st.sbuf(f"silu{i}", [P, CHUNK]) for i in range(2)]
        hid = [st.sbuf(f"hid{i}", [P, CHUNK]) for i in range(2)]
        hid_hi = st.sbuf("hid_hi", [P, UNITS, CHUNK], F32R)
        hid_lo = st.sbuf("hid_lo", [P, FULL, CHUNK], F32R)
        z_buf = [st.sbuf(f"z{i}", [P, DIM]) for i in range(2)]
        table = st.sbuf("table", [EXPERTS, CAP, 2])
        row_of = st.sbuf("row_of", [P, EXPERTS], I32)
        gate_of = st.sbuf("gate_of", [P, EXPERTS])
        rows = [st.sbuf(f"rows{i}", [P, 1], I32) for i in range(2)]
        gates = [st.sbuf(f"gates{i}", [P, 1]) for i in range(2)]
        xe = [st.sbuf(f"xe{i}", [P, DIM]) for i in range(2)]
        xe_t = st.sbuf("xe_t", [P, KD, P])
        e_silu = st.sbuf("e_silu", [P, INTER])
        e_hid = st.sbuf("e_hid", [P, INTER])
        e_hid_t = st.sbuf("e_hid_t", [P, HT, P])
        ye = [st.sbuf(f"ye{i}", [P, DIM]) for i in range(2)]

        ps_ab = [st.psum(f"ps_ab{i}", [P, 2, CHUNK]) for i in range(2)]
        ps_a, ps_b, ps_et, ps_y = (st.psum(n, [P, 512]) for n in ("ps_a", "ps_b", "ps_et", "ps_y"))

        const_in, table_in, shared_in = st.sem("const_in"), st.sem("table_in"), st.sem("shared_in")
        held = st.sem("held")
        split_hi, split_lo = st.sem("split_hi"), st.sem("split_lo")
        table_t, table_done = st.sem("table_t"), st.sem("table_done")
        w_in = [st.sem(f"w_in{i}") for i in range(2)]
        gathered = [st.sem(f"gathered{i}") for i in range(2)]
        row_picked, gate_picked = st.sem("row_picked"), st.sem("gate_picked")
        added, ye_free = st.sem("added"), st.sem("ye_free")
        xet_done, xet_copied = st.sem("xet_done"), st.sem("xet_copied")
        ab_done, esilu_done, ehid_done = st.sem("ab_done"), st.sem("esilu_done"), st.sem("ehid_done")
        eht_done, eht_copied, ey_done, ye_done = (st.sem(n) for n in ("eht_done", "eht_copied", "ey_done", "ye_done"))
        x_loaded = st.sem("x_loaded")
        xt_done, xt_hi_done, xt_lo_done = st.sem("xt_done"), st.sem("xt_hi_done"), st.sem("xt_lo_done")
        up_done, silu_done, hid_done = st.sem("up_done"), st.sem("silu_done"), st.sem("hid_done")
        hid_hi_done, hid_lo_done = st.sem("hid_hi_done"), st.sem("hid_lo_done")
        z_done, z_read = st.sem("z_done"), st.sem("z_read")
        z_stored = [st.sem(f"z_stored{i}") for i in range(2)]

        PLAN = [["x", 0, 1], [2, 3, 4], [5, "z0", "z1"], ["z2", "z3", None]]

        def expert_weights(sp, e, i):
            sp.dma_start(w13[i][:], w13_t[e].rearrange("(k p) n -> p k n", p=P)).then_inc(w_in[i], DMA)
            sp.dma_start(w2[i][:, 0 : HT - 1, :], w2_t[e, 0 : (HT - 1) * P, :].rearrange("(k p) n -> p k n", p=P)).then_inc(w_in[i], DMA)
            sp.dma_start(w2[i][0:LAST, HT - 1, :], w2_t[e, (HT - 1) * P : INTER, :]).then_inc(w_in[i], DMA)

        def sp_group(sp, g, final):
            for r in range(PER):
                e = PER * g + r
                for u in PLAN[r]:
                    if u == "x" and not final:
                        sp.wait_ge(xt_done, KD * (g + 1))
                        sp.dma_start(x_in[:], x1[bass.ds((g + 1) * CHUNK, CHUNK), :].rearrange("(t p) d -> p t d", p=P)).then_inc(x_loaded, DMA)
                    if isinstance(u, str) and u[0] == "z":
                        t = int(u[1])
                        sp.wait_ge(z_read, TT * g + t + 1 + TT)
                        sp.dma_start(shared_out[bass.ds(g * CHUNK + t * P, P), :], z_buf[t % 2][:]).then_inc(z_stored[t % 2], DMA)
                if not (final and r >= PER - 2):
                    sp.wait_ge(ey_done, e + 2)
                    expert_weights(sp, e + 2, r % 2)

        def pe_group(pe, g):
            for r in range(PER):
                e, i = PER * g + r, r % 2
                pe.wait_ge(gathered[i], DMA * (PER // 2 * g + r // 2 + 1))
                pe.wait_ge(eht_copied, e + 1)
                for c in range(KD):
                    last = nc.tensor.transpose(ps_et[:, c * P : c * P + P], xe[i][:, c * P : c * P + P], ident[:])
                last.then_inc(xet_done, 1)
                pe_unit(pe, g, PLAN[r][0])
                pe.wait_ge(w_in[i], DMA * W_LOADS * (PER // 2 * g + r // 2 + 1))
                pe.wait_ge(xet_copied, e + 1)
                pe.wait_ge(ehid_done, e + 1)
                for c in range(KD):
                    nc.tensor.matmul(ps_a[:, 0:INTER], xe_t[:, c, :], w13[i][:, c, 0:INTER], start=c == 0, stop=c == KD - 1)
                    last = nc.tensor.matmul(ps_b[:, 0:INTER], xe_t[:, c, :], w13[i][:, c, INTER : 2 * INTER], start=c == 0, stop=c == KD - 1)
                last.then_inc(ab_done, 1)
                pe_unit(pe, g, PLAN[r][1])
                pe.wait_ge(ehid_done, e + 2)
                for c in range(HT):
                    w = LAST if c == HT - 1 else P
                    last = nc.tensor.transpose(ps_et[0:w, c * P : c * P + P], e_hid[:, c * P : c * P + w], ident[:])
                last.then_inc(eht_done, 1)
                pe_unit(pe, g, PLAN[r][2])
                pe.wait_ge(eht_copied, e + 2)
                pe.wait_ge(ye_done, e + 1)
                for c in range(HT):
                    w = LAST if c == HT - 1 else P
                    last = nc.tensor.matmul(ps_y[:], e_hid_t[0:w, c, :], w2[i][0:w, c, :], start=c == 0, stop=c == HT - 1)
                last.then_inc(ey_done, 1)

        def pe_unit(pe, g, u):
            if u == "x":
                pe.wait_ge(x_loaded, DMA * (g + 1))
                pe.wait_ge(z_read, TT * (g + 1))
                for c in range(KD):
                    for t in range(TT):
                        last = nc.tensor.transpose(ps_ab[c // 2][:, c % 2, t * P : t * P + P], x_in[:, t, c * P : c * P + P], ident[:])
                    last.then_inc(xt_done, 1)
            elif isinstance(u, int):
                if u < 2:
                    pe.wait_ge(xt_lo_done, KD * (g + 1))
                else:
                    pe.wait_ge(hid_done, UNITS * g + u + 1)
                tiles = [u, FULL + u] if u < FULL else [2 * FULL]
                for ab, tile in enumerate(tiles):
                    for c in range(KD):
                        cols = slice(tile * P, tile * P + P)
                        last = split_product(nc, ps_ab[u % 2][:, ab, :], (sw13[0][:, c, cols], sw13[1][:, c, cols]), (x_t[0][:, c, :], x_t[1][:, c, :]), c == 0, c == KD - 1)
                last.then_inc(up_done, 1)
            elif u is not None:
                t = int(u[1])
                pe.wait_ge(hid_lo_done, UNITS * (g + 1))
                out = ps_ab[t // 2][:, t % 2, :]
                toks = slice(t * P, t * P + P)
                for c in range(FULL):
                    split_product(nc, out, (hid_hi[:, c, toks], hid_lo[:, c, toks]), (sw2[0][:, c, :], sw2[1][:, c, :]), c == 0, False)
                nc.tensor.matmul(out, hid_hi[:, FULL, toks], sw2[0][:, FULL, :], start=False, stop=False)
                nc.tensor.matmul(out, hid_hi[:, FULL, toks], sw2[1][:, FULL, :], start=False, stop=True).then_inc(z_done, 1)

        def act_group(act, g):
            for r in range(PER):
                e, i = PER * g + r, r % 2
                act.wait_ge(xet_done, e + 2)
                act.wait_ge(ab_done, e + 1)
                nc.scalar.copy(xe_t[:], ps_et[:].rearrange("p (c t) -> p c t", t=P)).then_inc(xet_copied, 1)
                act_unit(act, g, PLAN[r][0])
                act.wait_ge(ab_done, e + 2)
                nc.scalar.activation(e_silu[:], ps_a[:, 0:INTER], ACT.Silu).then_inc(esilu_done, 1)
                act_unit(act, g, PLAN[r][1])
                act_unit(act, g, PLAN[r][2])
                act.wait_ge(ey_done, e + 2)
                act.wait_ge(gate_picked, e + 1)
                act.wait_ge(ye_free, e + 1)
                nc.scalar.activation(ye[i][:], ps_y[:], ACT.Copy, scale=gates[i][:]).then_inc(ye_done, 1)

        def act_unit(act, g, u):
            if u == "x":
                act.wait_ge(up_done, UNITS * (g + 1))
                for c in range(KD):
                    act.wait_ge(xt_done, KD * g + c + 1)
                    nc.scalar.copy(x_t[0][:, c, :], ps_ab[c // 2][:, c % 2, :]).then_inc(xt_hi_done, 1)
            elif isinstance(u, int):
                n = UNITS * g + u
                w = P if u < FULL else REST
                act.wait_ge(up_done, n + 1 + UNITS)
                act.wait_ge(hid_done, n + 1)
                nc.scalar.activation(silu[u % 2][0:w, :], ps_ab[u % 2][0:w, 0, :], ACT.Silu).then_inc(silu_done, 1)
                act.wait_ge(hid_done, n + 3)
                if u == 0:
                    act.wait_ge(z_done, TT * (g + 1))
                nc.scalar.copy(hid_hi[0:w, u, :], hid[u % 2][0:w, :]).then_inc(hid_hi_done, 1)

        def dve_group(dve, g):
            for r in range(PER):
                e, i = PER * g + r, r % 2
                dve_unit(dve, g, PLAN[r][0])
                dve.wait_ge(esilu_done, e + 1)
                dve.wait_ge(eht_done, e + 1)
                nc.vector.tensor_tensor(e_hid[:], ps_b[:, 0:INTER], e_silu[:], ALU.mult).then_inc(ehid_done, 1)
                dve_unit(dve, g, PLAN[r][1])
                dve.wait_ge(eht_done, e + 2)
                dve.wait_ge(ey_done, e + 1)
                nc.vector.tensor_copy(e_hid_t[:, 0 : HT - 1, :], ps_et[:, 0 : (HT - 1) * P].rearrange("p (c t) -> p c t", t=P))
                nc.vector.tensor_copy(e_hid_t[0:LAST, HT - 1, :], ps_et[0:LAST, (HT - 1) * P : HT * P]).then_inc(eht_copied, 1)
                dve_unit(dve, g, PLAN[r][2])

        def dve_unit(dve, g, u):
            if u == "x":
                for c in range(KD):
                    dve.wait_ge(xt_hi_done, KD * g + c + 1)
                    nc.vector.tensor_tensor(x_t[1][:, c, :], ps_ab[c // 2][:, c % 2, :], x_t[0][:, c, :].bitcast(F32), ALU.subtract).then_inc(xt_lo_done, 1)
            elif isinstance(u, int):
                n = UNITS * g + u
                dve.wait_ge(silu_done, n + 1)
                if u < FULL:
                    nc.vector.tensor_tensor(hid[u % 2][:], ps_ab[u % 2][:, 1, :], silu[u % 2][:], ALU.mult).then_inc(hid_done, 1)
                    low, w = hid_lo[:, u, :], P
                else:
                    nc.vector.tensor_tensor(hid[u % 2][0:REST, :], ps_ab[u % 2][REST:P, 0, :], silu[u % 2][0:REST, :], ALU.mult).then_inc(hid_done, 1)
                    low, w = hid_hi[REST:P, u, :], REST
                dve.wait_ge(hid_hi_done, n + 1)
                nc.vector.tensor_tensor(low, hid[u % 2][0:w, :], hid_hi[0:w, u, :].bitcast(F32), ALU.subtract).then_inc(hid_lo_done, 1)
            elif u is not None:
                t = int(u[1])
                dve.wait_ge(z_done, TT * g + t + 1 + TT)
                dve.wait_ge(z_stored[t % 2], DMA * (TT // 2 * g + t // 2 + 1))
                nc.vector.tensor_copy(z_buf[t % 2][:], ps_ab[t // 2][:, t % 2, :]).then_inc(z_read, 1)

        def pick(pool, e, i):
            nc.gpsimd.tensor_copy(rows[i][:], row_of[:, bass.ds(e, 1)]).then_inc(row_picked, 1)
            nc.gpsimd.tensor_copy(gates[i][:], gate_of[:, bass.ds(e, 1)]).then_inc(gate_picked, 1)
            pool.wait_ge(row_picked, e + 1)
            pool.wait_ge(xet_done, e)
            pool.sem_inc(held, 1)
            nc.gpsimd.indirect_dma_start(
                xe[i][:], None, x1, bass.IndirectOffsetOnAxis(ap=rows[i][:, 0:1], axis=0),
                bounds_check=TOKENS + CAP - 1, oob_is_err=False,
            ).then_inc(gathered[i], DMA)

        def pool_group(pool, g, final):
            for r in range(PER):
                e, i = PER * g + r, r % 2
                if not (final and r == PER - 1):
                    pick(pool, e + 1, 1 - i)
                pool.wait_ge(ye_done, e + 2)
                pool.sem_inc(held, 1)
                nc.gpsimd.indirect_dma_start(
                    routed, bass.IndirectOffsetOnAxis(ap=rows[i][:, 0:1], axis=0), ye[i][:], None,
                    bounds_check=TOKENS + CAP - 1, compute_op=ALU.add,
                ).then_inc(added, DMA)
                pool.wait_ge(added, DMA * (e + 1))
                pool.sem_inc(ye_free, 1)

        with nc.Block() as block:

            @block.sync
            def _(sp):
                sp.dma_start(ident[:], ident_in).then_inc(const_in, DMA)
                sp.dma_start(table[:], slots.rearrange("(e c) w -> e c w", c=CAP)).then_inc(table_in, DMA)
                for i in range(2):
                    sp.dma_start(w13[i][:], sw13_t[:, i * SHARED : (i + 1) * SHARED].rearrange("(k p) n -> p k n", p=P)).then_inc(shared_in, DMA)
                sp.dma_start(w2[0][:], sw2_t[0 : 3 * P, :].rearrange("(k p) n -> p k n", p=P)).then_inc(shared_in, DMA)
                sp.dma_start(w2[1][:, 0:2, :], sw2_t[3 * P : 5 * P, :].rearrange("(k p) n -> p k n", p=P)).then_inc(shared_in, DMA)
                for top in (0, REST):
                    sp.dma_start(w2[1][top : top + REST, 2, :], sw2_t[FULL * P : SHARED, :]).then_inc(shared_in, DMA)
                sp.dma_start(x_in[:], x1[0:CHUNK, :].rearrange("(t p) d -> p t d", p=P)).then_inc(x_loaded, DMA)
                sp.wait_ge(split_lo, 4)
                expert_weights(sp, 0, 0)
                expert_weights(sp, 1, 1)
                with sp.Fori(0, GROUPS - 1) as g:
                    sp_group(sp, g, False)
                sp_group(sp, GROUPS - 1, True)
                for i in range(2):
                    sp.wait_ge(z_stored[i], DMA * (TT // 2 * GROUPS + 1))
                sp.wait_ge(added, DMA * EXPERTS)

            @block.tensor
            def _(pe):
                pe.sem_inc(xet_done, 1)
                pe.sem_inc(ab_done, 1)
                pe.sem_inc(eht_done, 1)
                pe.sem_inc(ey_done, 1)
                pe.sem_inc(up_done, UNITS)
                pe.sem_inc(z_done, TT)
                pe.wait_ge(const_in, DMA)
                pe.wait_ge(table_in, DMA)
                for w in range(2):
                    nc.tensor.transpose(ps_y[:, w * EXPERTS : (w + 1) * EXPERTS], table[:, :, w], ident[0:EXPERTS, 0:EXPERTS]).then_inc(table_t, 1)
                pe.wait_ge(split_lo, 4)
                with pe.Fori(0, GROUPS - 1) as g:
                    pe_group(pe, g)
                pe_group(pe, GROUPS - 1)

            @block.scalar
            def _(act):
                act.sem_inc(ye_done, 1)
                act.wait_ge(shared_in, 6 * DMA)
                for i in range(2):
                    nc.scalar.copy(sw13[0][:, :, i * SHARED : (i + 1) * SHARED], w13[i][:]).then_inc(split_hi, 1)
                for i in range(2):
                    nc.scalar.copy(sw2[0][:, 3 * i : 3 * i + 3, :], w2[i][:]).then_inc(split_hi, 1)
                with act.Fori(0, GROUPS - 1) as g:
                    act_group(act, g)
                act_group(act, GROUPS - 1)

            @block.vector
            def _(dve):
                dve.sem_inc(ehid_done, 1)
                dve.sem_inc(eht_copied, 1)
                dve.sem_inc(hid_done, 2)
                dve.sem_inc(z_read, TT)
                dve.wait_ge(table_t, 2)
                nc.vector.tensor_copy(row_of[:], ps_y[:, 0:EXPERTS]).then_inc(table_done, 1)
                nc.vector.tensor_copy(gate_of[:], ps_y[:, EXPERTS : 2 * EXPERTS]).then_inc(table_done, 1)
                for i in range(2):
                    dve.wait_ge(split_hi, i + 1)
                    cols = slice(i * SHARED, (i + 1) * SHARED)
                    nc.vector.tensor_tensor(sw13[1][:, :, cols], w13[i][:], sw13[0][:, :, cols].bitcast(F32), ALU.subtract).then_inc(split_lo, 1)
                for i in range(2):
                    dve.wait_ge(split_hi, i + 3)
                    tiles = slice(3 * i, 3 * i + 3)
                    nc.vector.tensor_tensor(sw2[1][:, tiles, :], w2[i][:], sw2[0][:, tiles, :].bitcast(F32), ALU.subtract).then_inc(split_lo, 1)
                with dve.Fori(0, GROUPS - 1) as g:
                    dve_group(dve, g)
                dve_group(dve, GROUPS - 1)

            @block.gpsimd
            def _(pool):
                pool.sem_inc(ye_free, 2)
                for i in range(2):
                    pool.sem_inc(z_stored[i], DMA)
                pool.wait_ge(table_done, 2)
                nc.gpsimd.tensor_copy(rows[0][:], row_of[:, 0:1]).then_inc(row_picked, 1)
                nc.gpsimd.tensor_copy(gates[0][:], gate_of[:, 0:1]).then_inc(gate_picked, 1)
                pool.wait_ge(row_picked, 1)
                nc.gpsimd.indirect_dma_start(
                    xe[0][:], None, x1, bass.IndirectOffsetOnAxis(ap=rows[0][:, 0:1], axis=0),
                    bounds_check=TOKENS + CAP - 1, oob_is_err=False,
                ).then_inc(gathered[0], DMA)
                with pool.Fori(0, GROUPS - 1) as g:
                    pool_group(pool, g, False)
                pool_group(pool, GROUPS - 1, True)


def finish(nc, routed, shared_out, out):
    TT = 4
    GROUPS = TOKENS // (P * TT)

    def view(t):
        return t[0:TOKENS, :].rearrange("(g p t) d -> g p t d", p=P, t=TT)

    routed_v, shared_v, out_v = view(routed), view(shared_out), view(out)
    with Stage(nc, "fin") as st:
        a = [st.sbuf(f"a{i}", [P, TT, DIM]) for i in range(2)]
        z = [st.sbuf(f"z{i}", [P, TT, DIM]) for i in range(2)]
        s = [st.sbuf(f"s{i}", [P, TT, DIM]) for i in range(2)]
        o = [st.sbuf(f"o{i}", [P, TT, DIM]) for i in range(2)]
        stats = st.sbuf("stats", [P, TT, 6])
        mean_var = [st.sbuf(f"mean_var{i}", [P, TT, 2]) for i in range(2)]
        half = st.sbuf("half", [P, TT])
        var_eps = st.sbuf("var_eps", [P, TT])
        mean_rstd = st.sbuf("mean_rstd", [P, TT])
        rstd = [st.sbuf(f"rstd{i}", [P, TT]) for i in range(2)]
        shift = [st.sbuf(f"shift{i}", [P, TT]) for i in range(2)]
        loaded = [st.sem(f"loaded{i}") for i in range(2)]
        stored = [st.sem(f"stored{i}") for i in range(2)]
        summed, stats_done, mv_done, half_done = (st.sem(n) for n in ("summed", "stats_done", "mv_done", "half_done"))
        held = st.sem("held")
        pool_step, ready, normed = st.sem("pool_step"), st.sem("ready"), st.sem("normed")
        with nc.Block() as block:

            @block.sync
            def _(sp):
                with sp.Fori(0, GROUPS // 2) as gg:
                    for i in range(2):
                        g = 2 * gg + i
                        sp.wait_ge(summed, g + 1)
                        sp.dma_start(a[i][:], routed_v[g]).then_inc(loaded[i], DMA)
                        sp.dma_start(z[i][:], shared_v[g]).then_inc(loaded[i], DMA)

            @block.vector
            def _(dve):
                dve.sem_inc(summed, 2)
                with dve.Fori(0, GROUPS // 2) as gg:
                    for i in range(2):
                        g = 2 * gg + i
                        dve.wait_ge(loaded[i], 2 * DMA * (gg + 1))
                        dve.wait_ge(normed, g + 1)
                        nc.vector.tensor_tensor(s[i][:], a[i][:], z[i][:], ALU.add).then_inc(summed, 1)
                        dve.wait_ge(summed, g + 3)
                        dve.wait_ge(mv_done, g + 1)
                        for t in range(TT):
                            last = nc.vector.bn_stats(stats[:, t, :], s[i][:, t, :])
                        last.then_inc(stats_done, 1)
                        dve.wait_ge(stats_done, g + 1)
                        dve.sem_inc(held, 1)
                        for t in range(TT):
                            last = nc.vector.bn_aggr(mean_var[i][:, t, :], stats[:, t, :])
                        last.then_inc(mv_done, 1)

            @block.gpsimd
            def _(pool):
                nc.gpsimd.memset(half[:], -0.5).then_inc(half_done, 1)
                pool.wait_ge(half_done, 1)
                with pool.Fori(0, GROUPS // 2) as gg:
                    for i in range(2):
                        g = 2 * gg + i
                        pool.wait_ge(mv_done, g + 2)
                        pool.wait_ge(normed, g + 1)
                        pool.sem_inc(held, 1)
                        nc.gpsimd.tensor_scalar(var_eps[:], mean_var[i][:, :, 1], EPS, 1.0, ALU.add, ALU.mult).then_inc(pool_step, 1)
                        pool.wait_ge(pool_step, 3 * g + 1)
                        nc.gpsimd.tensor_tensor(rstd[i][:], var_eps[:], half[:], ALU.pow).then_inc(pool_step, 1)
                        pool.wait_ge(pool_step, 3 * g + 2)
                        nc.gpsimd.tensor_tensor(mean_rstd[:], mean_var[i][:, :, 0], rstd[i][:], ALU.mult).then_inc(pool_step, 1)
                        pool.wait_ge(pool_step, 3 * g + 3)
                        pool.sem_inc(held, 1)
                        nc.gpsimd.tensor_scalar(shift[i][:], mean_rstd[:], -1.0, 0.0, ALU.mult, ALU.add).then_inc(ready, 1)

            @block.scalar
            def _(act):
                act.sem_inc(normed, 2)
                act.sem_inc(mv_done, 1)
                for i in range(2):
                    act.sem_inc(stored[i], DMA)
                with act.Fori(0, GROUPS // 2) as gg:
                    for i in range(2):
                        g = 2 * gg + i
                        act.wait_ge(ready, g + 1)
                        act.wait_ge(stored[i], DMA * (gg + 1))
                        for t in range(TT):
                            last = nc.scalar.activation(o[i][:, t, :], s[i][:, t, :], ACT.Identity, bias=shift[i][:, t : t + 1], scale=rstd[i][:, t : t + 1])
                        last.then_inc(normed, 1)
                        act.wait_ge(normed, g + 3)
                        act.dma_start(out_v[g], o[i][:]).then_inc(stored[i], DMA)
                for i in range(2):
                    act.wait_ge(stored[i], DMA * (GROUPS // 2 + 1))


def layer(nc, x, x_t, w_qk, w_v, w_out, lambdas, subln, gate_t, w13_t, w2_t, sw13_t, sw2_t, rope, ident, before, empty_slots, out):
    q_parts = nc.dram_tensor("q_parts", (BATCH, 2, 2, SUBS * FREQ, SEQ), F32).ap()
    k_parts = nc.dram_tensor("k_parts", (BATCH, 2, 2, SUBS * FREQ, SEQ), F32).ap()
    v_parts = nc.dram_tensor("v_parts", (BATCH, HEADS, SEQ, 2 * VD), F32).ap()
    x1 = nc.dram_tensor("x1", (TOKENS + CAP, DIM), F32).ap()
    routed = nc.dram_tensor("routed", (TOKENS + CAP, DIM), F32).ap()
    shared_out = nc.dram_tensor("shared_out", (TOKENS, DIM), F32).ap()
    slots = nc.dram_tensor("slots", (EXPERTS * CAP, 2), F32).ap()
    project(nc, x_t, w_qk, w_v, (rope[0], rope[2]), (rope[1], rope[3]), q_parts, k_parts, v_parts)
    attend(nc, q_parts, k_parts, v_parts, x, lambdas, subln, w_out, gate_t, ident, before, empty_slots, x1, routed, slots)
    experts(nc, x1, slots, w13_t, w2_t, sw13_t, sw2_t, ident, routed, shared_out)
    finish(nc, routed, shared_out, out)


def shape_constants():
    inv = 1.0 / 10000.0 ** (np.arange(0, HALF, 2)[: HALF // 2].astype(np.float64) / HALF)
    angle = np.outer(np.arange(SEQ), inv)
    cos = np.tile(np.cos(angle).astype(np.float32).T, (GROUP, 1))
    sin = np.tile(np.sin(angle).astype(np.float32).T, (GROUP, 1))
    plain, cross = np.stack([cos, sin], 1), np.stack([-sin, cos], 1)
    rope = np.stack([plain * np.float32(SCALE), cross * np.float32(SCALE), plain, cross])
    ident = np.eye(P, dtype=np.float32)
    before = np.triu(np.ones((P, P), np.float32), 1)
    empty = np.zeros((EXPERTS * CAP, 2), np.float32)
    empty[:, 0] = TOKENS + np.tile(np.arange(CAP), EXPERTS)
    return {"rope": np.ascontiguousarray(rope), "ident": ident, "before": before, "empty_slots": empty}


def by_rotation(w):
    w = w.reshape(SUBS // GROUP, GROUP, FREQ, 2, DIM)
    return w.transpose(0, 3, 1, 2, 4).reshape(DIM, DIM).T


def kernel(**inputs):
    import concourse.bacc as bacc
    from concourse.bass_utils import run_bass_kernel_spmd

    a = {name.removeprefix("L0_"): np.asarray(value) for name, value in inputs.items()}
    x = a["attn_x"].reshape(TOKENS, DIM)
    sw1, sw3 = a["ffn_sw1"], a["ffn_sw3"]
    full = SHARED // P * P
    arrays = {
        "x": x,
        "x_t": x.T,
        "w_qk": np.concatenate([by_rotation(a["attn_wq"]), by_rotation(a["attn_wk"])], 1),
        "w_v": a["attn_wv"].T,
        "w_out": a["attn_wout"].T,
        "lambdas": np.stack([a[f"attn_lambda_{n}"] for n in ("q1", "q2", "k1", "k2")]),
        "subln": a["attn_subln_weight"][:, None],
        "gate_t": a["ffn_gate_w"].T,
        "w13_t": np.concatenate([a["ffn_w1"].transpose(0, 2, 1), a["ffn_w3"].transpose(0, 2, 1)], 2),
        "w2_t": a["ffn_w2"].transpose(0, 2, 1),
        "sw13_t": np.concatenate([sw1[:full], sw3[:full], sw1[full:], sw3[full:]]).T,
        "sw2_t": a["ffn_sw2"].T,
        **shape_constants(),
    }
    nc = bacc.Bacc("TRN2", target_bir_lowering=False, num_devices=1)
    args = {}
    for name, value in arrays.items():
        arrays[name] = value = np.ascontiguousarray(value)
        args[name] = nc.dram_tensor(f"in_{name}", value.shape, mybir.dt.from_np(value.dtype), kind="ExternalInput").ap()
    out = nc.dram_tensor("out", (TOKENS, DIM), F32, kind="ExternalOutput").ap()
    layer(nc, out=out, **args)
    result = run_bass_kernel_spmd(nc, [{f"in_{name}": value for name, value in arrays.items()}], core_ids=[0])
    return result.results[0]["out"].reshape(BATCH, SEQ, DIM)
```

```python
from contextlib import ExitStack

import numpy as np

import concourse.bass as bass
from concourse import mybir

F32 = mybir.dt.float32
F32R = mybir.dt.float32r
BF16 = mybir.dt.bfloat16
I32 = mybir.dt.int32
U32 = mybir.dt.uint32
ALU = mybir.AluOpType
ACT = mybir.ActivationFunctionType
AX = mybir.AxisListType

P = 128
BATCH, SEQ, DIM = 8, 1024, 512
TOKENS = BATCH * SEQ
KD = DIM // P
HALF = 64
SUBS = DIM // HALF
HEADS = SUBS // 2
VD = 2 * HALF
FREQ = HALF // 2
GROUP = P // FREQ
LAMBDA_INIT = 0.8 - 0.6 * float(np.exp(-0.3 * 12))
SCALE = 1.0 / (128**-0.5)
EPS = 1e-5
EXPERTS, TOPK, CAP, INTER = 64, 6, 128, 352
SHARED = 704
CHUNK = 512
DMA = 16


class Stage:

    def __init__(self, nc, name):
        self.nc, self.name, self.stack = nc, name, ExitStack()

    def __enter__(self):
        return self

    def __exit__(self, *error):
        return self.stack.__exit__(*error)

    def sbuf(self, name, shape, dt=F32):
        return self.stack.enter_context(self.nc.sbuf_tensor(f"{self.name}_{name}", shape, dt))

    def psum(self, name, shape, dt=F32):
        return self.stack.enter_context(self.nc.psum_tensor(f"{self.name}_{name}", shape, dt))

    def sem(self, name):
        return self.stack.enter_context(self.nc.semaphore(f"{self.name}_{name}"))


def split_product(nc, out, lhs, rhs, first, last):
    nc.tensor.matmul(out, lhs[0], rhs[0], start=first, stop=False)
    nc.tensor.matmul(out, lhs[0], rhs[1], start=False, stop=False)
    return nc.tensor.matmul(out, lhs[1], rhs[0], start=False, stop=last)


def project(nc, x_t, w_qk, w_v, rope_plain, rope_cross, q_parts, k_parts, v_parts):
    x_view = x_t.rearrange("(k p) t -> p k t", p=P)
    with Stage(nc, "proj") as st:
        raw_w = st.sbuf("raw_w", [P, KD, 2 * DIM])
        wqk = [st.sbuf(f"wqk_{part}", [P, KD, 2 * DIM], F32R) for part in ("hi", "lo")]
        wv = [st.sbuf(f"wv_{part}", [P, KD, DIM], F32R) for part in ("hi", "lo")]
        plain = [st.sbuf(f"plain{i}", [P, 2, SEQ]) for i in range(2)]
        cross = [st.sbuf(f"cross{i}", [P, 2, SEQ]) for i in range(2)]
        x_raw = [st.sbuf(f"x_raw{i}", [P, KD, CHUNK]) for i in range(2)]
        x_hi = [st.sbuf(f"x_hi{i}", [P, KD, CHUNK], F32R) for i in range(2)]
        x_lo = [st.sbuf(f"x_lo{i}", [P, KD, CHUNK], F32R) for i in range(2)]
        by_real = [st.sbuf(f"by_real{i}", [P, 2, CHUNK]) for i in range(2)]
        by_imag = [st.sbuf(f"by_imag{i}", [P, 2, CHUNK]) for i in range(2)]
        turned = [st.sbuf(f"turned{i}", [P, 2, CHUNK]) for i in range(2)]
        out_hi = [st.sbuf(f"out_hi{i}", [P, 2, CHUNK], F32R) for i in range(2)]
        out_lo = [st.sbuf(f"out_lo{i}", [P, 2, CHUNK], F32R) for i in range(2)]
        v_out = [st.sbuf(f"v_out{i}", [P, HEADS, 2, VD], F32R) for i in range(2)]
        ps_qk = [st.psum(f"ps_qk{i}", [P, 2, CHUNK]) for i in range(2)]
        ps_v = [st.psum(f"ps_v{i}", [P, HEADS, VD]) for i in range(2)]

        w_qk_in, w_v_in, tables_in = st.sem("w_qk_in"), st.sem("w_v_in"), st.sem("tables_in")
        w_hi, w_lo = st.sem("w_hi"), st.sem("w_lo")
        x_in = [st.sem(f"x_in{i}") for i in range(2)]
        x_hi_done, x_lo_done = st.sem("x_hi_done"), st.sem("x_lo_done")
        qk_done, qk_read = st.sem("qk_done"), st.sem("qk_read")
        real_done, imag_done, turned_done = st.sem("real_done"), st.sem("imag_done"), st.sem("turned_done")
        hi_done, lo_done = st.sem("hi_done"), st.sem("lo_done")
        v_done, v_hi_done, v_lo_done = st.sem("v_done"), st.sem("v_hi_done"), st.sem("v_lo_done")
        qk_stored = [st.sem(f"qk_stored{i}") for i in range(2)]
        v_stored = [st.sem(f"v_stored{i}") for i in range(2)]

        PAIRS = 2 * SUBS // GROUP
        VT = CHUNK // P
        chunks = 2 * BATCH

        with nc.Block() as block:

            @block.sync
            def _(sp):
                sp.dma_start(raw_w[:], w_qk.rearrange("(k p) n -> p k n", p=P)).then_inc(w_qk_in, DMA)
                sp.dma_start(x_raw[0][:], x_view[:, :, 0:CHUNK]).then_inc(x_in[0], DMA)
                for i in range(2):
                    sp.dma_start(plain[i][:], rope_plain[i]).then_inc(tables_in, DMA)
                    sp.dma_start(cross[i][:], rope_cross[i]).then_inc(tables_in, DMA)
                sp.wait_ge(w_lo, 1)
                sp.dma_start(raw_w[:, :, 0:DIM], w_v.rearrange("(k p) n -> p k n", p=P)).then_inc(w_v_in, DMA)
                with sp.Fori(0, BATCH) as b:
                    for half in range(2):
                        c = 2 * b + half
                        nxt = 1 - half
                        sp.wait_ge(x_lo_done, c + 1)
                        at = ((c + 1) % chunks) * CHUNK
                        sp.dma_start(x_raw[nxt][:], x_view[:, :, bass.ds(at, CHUNK)]).then_inc(x_in[nxt], DMA)
                        for m in range(PAIRS):
                            parts = (q_parts, k_parts)[m // 2]
                            rows = slice(P * (m % 2), P * (m % 2) + P)
                            cols = slice(half * CHUNK, half * CHUNK + CHUNK)
                            sp.wait_ge(hi_done, PAIRS * c + m + 1)
                            for ri in range(2):
                                sp.dma_start(parts[b, 0, ri, rows, cols], out_hi[m % 2][:, ri, :].bitcast(F32)).then_inc(qk_stored[m % 2], DMA)
                            sp.wait_ge(lo_done, PAIRS * c + m + 1)
                            for ri in range(2):
                                sp.dma_start(parts[b, 1, ri, rows, cols], out_lo[m % 2][:, ri, :].bitcast(F32)).then_inc(qk_stored[m % 2], DMA)
                            sp.wait_ge(v_lo_done, VT * c + m + 1 + 2)
                            s0 = half * CHUNK + m * P
                            sp.dma_start(
                                v_parts[b, :, s0 : s0 + P, :].rearrange("h s c -> s h c"),
                                v_out[m % 2][:].rearrange("p h l c -> p h (l c)").bitcast(F32),
                            ).then_inc(v_stored[m % 2], DMA)
                for i in range(2):
                    sp.wait_ge(qk_stored[i], 4 * DMA * (PAIRS // 2 * chunks + 1))
                    sp.wait_ge(v_stored[i], DMA * (VT // 2 * chunks + 1))
                sp.wait_ge(x_in[0], DMA * (BATCH + 1))

            @block.scalar
            def _(act):
                act.sem_inc(qk_stored[0], 4 * DMA)
                act.sem_inc(qk_stored[1], 4 * DMA)
                act.sem_inc(v_stored[0], DMA)
                act.sem_inc(v_stored[1], DMA)
                act.wait_ge(w_qk_in, DMA)
                nc.scalar.copy(wqk[0][:], raw_w[:]).then_inc(w_hi, 1)
                act.wait_ge(x_in[0], DMA)
                nc.scalar.copy(x_hi[0][:], x_raw[0][:]).then_inc(x_hi_done, 1)
                act.wait_ge(w_v_in, DMA)
                nc.scalar.copy(wv[0][:], raw_w[:, :, 0:DIM]).then_inc(w_hi, 1)
                with act.Fori(0, BATCH) as b:
                    for half in range(2):
                        c = 2 * b + half
                        nxt = 1 - half
                        act.wait_ge(v_done, VT * (c + 2))
                        act.wait_ge(x_in[nxt], DMA * (b + 1 + half))
                        nc.scalar.copy(x_hi[nxt][:], x_raw[nxt][:]).then_inc(x_hi_done, 1)
                        for m in range(PAIRS):
                            n = PAIRS * c + m
                            act.wait_ge(turned_done, n + 1)
                            act.wait_ge(qk_stored[m % 2], 4 * DMA * (2 * c + m // 2 + 1))
                            nc.scalar.copy(out_hi[m % 2][:], turned[m % 2][:]).then_inc(hi_done, 1)
                            act.wait_ge(v_done, VT * (c + 2) + m + 1)
                            act.wait_ge(v_stored[m % 2], DMA * (2 * c + m // 2 + 1))
                            nc.scalar.copy(v_out[m % 2][:, :, 0, :], ps_v[m % 2][:]).then_inc(v_hi_done, 1)

            @block.vector
            def _(dve):
                dve.sem_inc(qk_read, 2)
                dve.sem_inc(v_lo_done, 2)
                dve.wait_ge(w_hi, 1)
                nc.vector.tensor_tensor(wqk[1][:], raw_w[:], wqk[0][:].bitcast(F32), ALU.subtract).then_inc(w_lo, 1)
                dve.wait_ge(x_hi_done, 1)
                nc.vector.tensor_tensor(x_lo[0][:], x_raw[0][:], x_hi[0][:].bitcast(F32), ALU.subtract).then_inc(x_lo_done, 1)
                dve.wait_ge(w_hi, 2)
                nc.vector.tensor_tensor(wv[1][:], raw_w[:, :, 0:DIM], wv[0][:].bitcast(F32), ALU.subtract).then_inc(w_lo, 1)
                dve.wait_ge(tables_in, 4 * DMA)

                def qk_low(c, m):
                    dve.wait_ge(hi_done, PAIRS * c + m + 1)
                    nc.vector.tensor_tensor(out_lo[m % 2][:], turned[m % 2][:], out_hi[m % 2][:].bitcast(F32), ALU.subtract).then_inc(lo_done, 1)

                def v_low(c, m):
                    dve.wait_ge(v_hi_done, VT * c + m + 1)
                    nc.vector.tensor_tensor(v_out[m % 2][:, :, 1, :], ps_v[m % 2][:], v_out[m % 2][:, :, 0, :].bitcast(F32), ALU.subtract).then_inc(v_lo_done, 1)

                with dve.Fori(0, BATCH) as b:
                    for half in range(2):
                        c = 2 * b + half
                        nxt = 1 - half
                        cols = slice(half * CHUNK, half * CHUNK + CHUNK)
                        for m in range(PAIRS):
                            n = PAIRS * c + m
                            i = m % 2
                            dve.wait_ge(qk_done, n + 1)
                            for src, table, dst, sem in ((0, plain, by_real, real_done), (1, cross, by_imag, imag_done)):
                                last = nc.vector.tensor_tensor(
                                    dst[i][:],
                                    ps_qk[i][:, src : src + 1, :].to_broadcast([P, 2, CHUNK]),
                                    table[m // 2][:, :, cols],
                                    ALU.mult,
                                ).then_inc(sem if src == 0 else qk_read, 1)
                            dve.wait_ge(real_done, n + 1)
                            dve.wait_ge(qk_read, n + 3)
                            nc.vector.tensor_tensor(turned[i][:], by_real[i][:], by_imag[i][:], ALU.add).then_inc(turned_done, 1)
                            if m:
                                qk_low(c, m - 1)
                                v_low(c, m - 1)
                            if m == 1:
                                dve.wait_ge(x_hi_done, c + 2)
                                nc.vector.tensor_tensor(x_lo[nxt][:], x_raw[nxt][:], x_hi[nxt][:].bitcast(F32), ALU.subtract).then_inc(x_lo_done, 1)
                        qk_low(c, PAIRS - 1)
                        v_low(c, PAIRS - 1)

            @block.tensor
            def _(pe):
                pe.sem_inc(v_done, 2 * VT)
                pe.wait_ge(w_lo, 2)
                with pe.Fori(0, BATCH) as b:
                    for half in range(2):
                        c = 2 * b + half
                        pe.wait_ge(x_lo_done, c + 1)
                        for m in range(PAIRS):
                            pe.wait_ge(qk_read, PAIRS * c + m + 1)
                            for ri in range(2):
                                cols = slice((2 * m + ri) * P, (2 * m + ri) * P + P)
                                for k in range(KD):
                                    last = split_product(
                                        nc, ps_qk[m % 2][:, ri, :],
                                        (wqk[0][:, k, cols], wqk[1][:, k, cols]),
                                        (x_hi[half][:, k, :], x_lo[half][:, k, :]),
                                        k == 0, k == KD - 1)
                            last.then_inc(qk_done, 1)
                            pe.wait_ge(v_lo_done, VT * c + m + 1)
                            toks = slice(m * P, m * P + P)
                            for k in range(KD):
                                last = split_product(
                                    nc, ps_v[m % 2][:],
                                    (x_hi[half][:, k, toks], x_lo[half][:, k, toks]),
                                    (wv[0][:, k, :], wv[1][:, k, :]),
                                    k == 0, k == KD - 1)
                            last.then_inc(v_done, 1)


def attend(nc, q_parts, k_parts, v_parts, x, lambdas, subln, w_out, gate_t, ident_in, before_in, empty_slots, x1, routed, slots):
    TILES = SEQ // P
    STEPS = HEADS * TILES
    LOADS_QK = 12
    BIG = 1.0e6
    with Stage(nc, "att") as st:
        q_buf = [st.sbuf(f"q{i}", [P, 2, SEQ], F32R) for i in range(2)]
        k_hi = [st.sbuf(f"k_hi{i}", [P, 2, SEQ], F32R) for i in range(2)]
        k_lo = [st.sbuf(f"k_lo{i}", [P, 2, SEQ], F32R) for i in range(2)]
        v_buf = [st.sbuf(f"v{i}", [P, TILES, 2 * VD], F32R) for i in range(2)]
        prob = [[st.sbuf(f"prob{s}{i}", [P, SEQ]) for i in range(2)] for s in range(2)]
        diff = [st.sbuf(f"diff{i}", [P, SEQ]) for i in range(2)]
        diff_hi = [st.sbuf(f"diff_hi{i}", [P, TILES, P], F32R) for i in range(2)]
        diff_lo = [st.sbuf(f"diff_lo{i}", [P, TILES, P], F32R) for i in range(2)]
        neg_max = st.sbuf("neg_max", [P, 2, 2])
        mass0 = st.sbuf("mass0", [P, 2, TILES, HEADS])
        mass1 = st.sbuf("mass1", [P, 2])
        mass1_inv = st.sbuf("mass1_inv", [P, 2])
        weight2 = st.sbuf("weight2", [P, 2])
        lam_in = st.sbuf("lam_in", [P, 4, HALF])
        lam_prod = st.sbuf("lam_prod", [P, 2, HALF])
        lam_sum = st.sbuf("lam_sum", [P, 2])
        lam_exp = st.sbuf("lam_exp", [P, 2])
        lam_diff = st.sbuf("lam_diff", [P, 1])
        neg_lam = st.sbuf("neg_lam", [P, 1])
        cross_sum = st.sbuf("cross_sum", [P, VD])
        raw = st.sbuf("raw", [P, 2, TILES, HEADS, VD])
        squares = st.sbuf("squares", [P, 2, TILES, HEADS])
        mass_squared = st.sbuf("mass_squared", [P, HEADS])
        eps_mass = st.sbuf("eps_mass", [P, HEADS])
        eps_col = st.sbuf("eps_col", [P, HEADS])
        square_junk = st.sbuf("square_junk", [P, VD])
        wo_raw = st.sbuf("wo_raw", [P, KD, DIM])
        wo = [st.sbuf(f"wo_{part}", [P, KD, DIM], F32R) for part in ("hi", "lo")]
        subln_col = st.sbuf("subln_col", [P, 1])
        gate_raw = st.sbuf("gate_raw", [P, KD, EXPERTS])
        gate = [st.sbuf(f"gate_{part}", [P, KD, EXPERTS], F32R) for part in ("hi", "lo")]
        ident = st.sbuf("ident", [P, P])
        neg_ident = st.sbuf("neg_ident", [P, P], F32R)
        before_f = st.sbuf("before_f", [P, P])
        before = st.sbuf("before", [P, P], BF16)
        ones = st.sbuf("ones", [P, P], BF16)
        zeros = st.sbuf("zeros", [P, DIM])
        iota_i = st.sbuf("iota_i", [P, EXPERTS], I32)
        iota = st.sbuf("iota", [P, EXPERTS])
        token_i = st.sbuf("token_i", [P, 1], I32)
        token = st.sbuf("token", [P, 1])
        pow_col = st.sbuf("pow_col", [P, HEADS])
        rms_sum = st.sbuf("rms_sum", [P, HEADS])
        rms = st.sbuf("rms", [P, HEADS])
        normed = st.sbuf("normed", [P, HEADS, VD])
        heads_t = [st.sbuf(f"heads_t_{part}", [P, KD, P], F32R) for part in ("hi", "lo")]
        x_in = [st.sbuf(f"x_in{i}", [P, DIM]) for i in range(2)]
        summed = st.sbuf("summed", [P, DIM])
        stats = st.sbuf("stats", [P, 6])
        mean_var = st.sbuf("mean_var", [P, 2])
        var_eps = st.sbuf("var_eps", [P, 1])
        neg_mean = st.sbuf("neg_mean", [P, 1])
        rstd = st.sbuf("rstd", [P, 1])
        shift = st.sbuf("shift", [P, 1])
        x1_buf = [st.sbuf(f"x1_{i}", [P, DIM]) for i in range(2)]
        x1_t = [st.sbuf(f"x1_t_{part}", [P, KD, P], F32R) for part in ("hi", "lo")]
        logit_max = st.sbuf("logit_max", [P, 1])
        score_exp = st.sbuf("score_exp", [P, EXPERTS])
        score_sum = st.sbuf("score_sum", [P, 1])
        score_inv = st.sbuf("score_inv", [P, 1])
        score = st.sbuf("score", [P, EXPERTS])
        top_val = st.sbuf("top_val", [P, 8])
        top_idx = st.sbuf("top_idx", [P, 8], U32)
        chosen = st.sbuf("chosen", [P, TOPK])
        hit = st.sbuf("hit", [P, TOPK, EXPERTS])
        mask_f = st.sbuf("mask_f", [P, EXPERTS])
        mask = st.sbuf("mask", [P, EXPERTS], BF16)
        mask_seen = st.sbuf("mask_seen", [P, EXPERTS], BF16)
        pos = st.sbuf("pos", [P, EXPERTS])
        hit_pos = st.sbuf("hit_pos", [P, TOPK, EXPERTS])
        pos_k = st.sbuf("pos_k", [P, TOPK])
        over = st.sbuf("over", [P, TOPK])
        slot_f = st.sbuf("slot_f", [P, TOPK])
        slot = st.sbuf("slot", [P, TOPK], I32)
        entry = st.sbuf("entry", [P, TOPK, 2])
        valid = st.sbuf("valid", [P, 1])
        room = st.sbuf("room", [P, 1])

        ps_s = [st.psum(f"ps_s{s}", [P, SEQ]) for s in range(2)]
        ps_t = st.psum("ps_t", [P, TILES, P])
        ps_o = st.psum("ps_o", [P, 512])
        ps_m = st.psum("ps_m", [P, 512])
        POS = slice(2 * VD, 2 * VD + EXPERTS)

        weights_in, lam_loaded, consts_in, pads_out = (st.sem(n) for n in ("weights_in", "lam_loaded", "consts_in", "pads_out"))
        held = st.sem("held")
        neg_ident_done, before_done = st.sem("neg_ident_done"), st.sem("before_done")
        weight_step = st.sem("weight_step")
        setup_pool, setup_dve, setup_act = st.sem("setup_pool"), st.sem("setup_dve"), st.sem("setup_act")
        qk_in = [st.sem(f"qk_in{i}") for i in range(2)]
        v_in = [st.sem(f"v_in{i}") for i in range(2)]
        s_done = [st.sem(f"s_done{s}") for s in range(2)]
        max_done = [st.sem(f"max_done{s}") for s in range(2)]
        exp_done = [st.sem(f"exp_done{s}") for s in range(2)]
        inv_done, weight_done, diff_done = st.sem("inv_done"), st.sem("weight_done"), st.sem("diff_done")
        t_done, hi_done, lo_done = st.sem("t_done"), st.sem("hi_done"), st.sem("lo_done")
        rest_done, lo2_done = st.sem("rest_done"), st.sem("lo2_done")
        o_done, cross_done, raw_done, square_done = (st.sem(n) for n in ("o_done", "cross_done", "raw_done", "square_done"))
        rms_step, normed_done = st.sem("rms_step"), st.sem("normed_done")
        at_done, at_hi_done, at_lo_done = st.sem("at_done"), st.sem("at_hi_done"), st.sem("at_lo_done")
        x_loaded = [st.sem(f"x_loaded{i}") for i in range(2)]
        y_done, sum_done, stats_done, mv_done = (st.sem(n) for n in ("y_done", "sum_done", "stats_done", "mv_done"))
        ln_step, ln_done, x1_done = st.sem("ln_step"), st.sem("ln_done"), st.sem("x1_done")
        x1_stored = [st.sem(f"x1_stored{i}") for i in range(2)]
        xt_done, xt_hi_done, xt_lo_done = st.sem("xt_done"), st.sem("xt_hi_done"), st.sem("xt_lo_done")
        gate_done, lmax_done, score_done = st.sem("gate_done"), st.sem("lmax_done"), st.sem("score_done")
        hit_pos_done = st.sem("hit_pos_done")
        route_step, mask_done, pos_done, pos_read = (st.sem(n) for n in ("route_step", "mask_done", "pos_done", "pos_read"))
        slot_step, slot_done, scattered, entry_free = (st.sem(n) for n in ("slot_step", "slot_done", "scattered", "entry_free"))

        SETUP_POOL, SETUP_DVE = 8, 10
        NORMED_CREDIT = 2 * TILES
        ROUTE_STEPS, SLOT_STEPS, RMS_STEPS, LN_STEPS = 8, 4, 4, 3

        def of_lag(b, jl, lag):
            jj = jl - lag
            bb = b if jj >= 0 else b - 1
            jj = jj % STEPS
            return bb, jj // TILES, jj % TILES, bb * STEPS + jj

        def turns(attn, out, first, lag_max=4):
            for jl in range(STEPS):
                live = {lag: (jl >= lag if first else (attn or jl < lag)) for lag in range(lag_max + 1)}
                yield jl, live, (jl // 4, jl % 4) if out else (None, None)

        def sp_turns(sp, b, attn, out, first):
            for jl, live, (k, piece) in turns(attn, out, first):
                h, t = jl // TILES, jl % TILES
                if attn:
                    nb, nh = (b, h + 1) if h + 1 < HEADS else (b + 1, 0)
                    i = nh % 2
                    skip = first and h == 0
                    if t == 1:
                        if not skip:
                            sp.wait_ge(s_done[1], STEPS * b + TILES * h)
                        load_qk(sp, nb, nh, i)
                    if t == 5:
                        if not skip:
                            sp.wait_ge(o_done, STEPS * b + TILES * h)
                        load_v(sp, nb, nh, i)
                if out:
                    n = TILES * (b - 1) + k
                    if piece == 0:
                        sp.wait_ge(sum_done, n + 1)
                        sp.dma_start(x_in[k % 2][:], x[bass.ds(n * P, P), :]).then_inc(x_loaded[k % 2], DMA)
                    if piece == 2:
                        sp.wait_ge(x1_done, n + 2)
                        sp.dma_start(x1[bass.ds(n * P, P), :], x1_buf[k % 2][:]).then_inc(x1_stored[k % 2], DMA)
                        sp.dma_start(routed[bass.ds(n * P, P), :], x1_buf[k % 2][:]).then_inc(x1_stored[k % 2], DMA)

        def load_qk(sp, b, h, i):
            if isinstance(b, int) and b >= BATCH:
                return
            if not isinstance(b, int) and h == 0:
                b = b % BATCH
            src = slice(2 * h * FREQ, (2 * h + 2) * FREQ)
            for part in range(2):
                for ri in range(2):
                    def rows(parts, p):
                        return parts[b, p, ri, src, :].rearrange("(s f) t -> f s t", s=2)

                    at = 2 * part * FREQ + ri * FREQ
                    sp.dma_start(q_buf[i][at : at + FREQ].bitcast(F32), rows(q_parts, part)).then_inc(qk_in[i], DMA)
                    sp.dma_start(k_hi[i][at : at + FREQ].bitcast(F32), rows(k_parts, 0)).then_inc(qk_in[i], DMA)
                    sp.dma_start(k_lo[i][at : at + FREQ].bitcast(F32), rows(k_parts, 1)).then_inc(qk_in[i], DMA)

        def load_v(sp, b, h, i):
            if not isinstance(b, int) and h == 0:
                b = b % BATCH
            sp.dma_start(v_buf[i][:].bitcast(F32), v_parts[b, h].rearrange("(t p) c -> p t c", p=P)).then_inc(v_in[i], DMA)

        def pe_turns(pe, b, attn, out, first):
            for jl, live, (k, piece) in turns(attn, out, first):
                if attn:
                    h, t, j = jl // TILES, jl % TILES, STEPS * b + jl
                    if t == 0:
                        pe.wait_ge(qk_in[h % 2], DMA * LOADS_QK * (2 * b + h // 2 + 1))
                    q_cols = slice(t * P, t * P + P)
                    for s in range(2):
                        if not (first and jl == 0):
                            pe.wait_ge(exp_done[s], j)
                        for half in range(2):
                            cols = slice(half * CHUNK, half * CHUNK + CHUNK)
                            nc.tensor.matmul(ps_s[s][:, cols], q_buf[h % 2][:, s, q_cols], k_hi[h % 2][:, s, cols], start=True, stop=False)
                            last = nc.tensor.matmul(ps_s[s][:, cols], q_buf[h % 2][:, s, q_cols], k_lo[h % 2][:, s, cols], start=False, stop=True)
                        last.then_inc(s_done[s], 1)
                if live[2]:
                    _, _, _, j2 = of_lag(b, jl, 2)
                    pe.wait_ge(diff_done, j2 + 1)
                    if not (first and jl == 2):
                        pe.wait_ge(lo_done, j2)
                        pe.wait_ge(lo2_done, j2)
                    for t in range(TILES):
                        last = nc.tensor.matmul(
                            ps_t[:, t, :], diff[jl % 2][:, t * P : t * P + P], ident[:], is_transpose=True,
                            start=t <= TILES // 2, stop=t < TILES // 2 or t == TILES - 1)
                    last.then_inc(t_done, 1)
                if out:
                    pe_piece(pe, TILES * (b - 1) + k, piece, k)
                if live[3]:
                    bb, h, t, j = of_lag(b, jl, 3)
                    if t == 0:
                        pe.wait_ge(v_in[h % 2], DMA * (2 * bb + h // 2 + 1))
                    pe.wait_ge(lo_done, j + 1)
                    pe.wait_ge(lo2_done, j + 1)
                    if not (first and jl == 3):
                        pe.wait_ge(raw_done, j)
                    if out and piece == 1:
                        pe_positions(pe, TILES * (b - 1) + k - 1)
                    i = (jl - 3) % 2
                    for t in range(TILES):
                        nc.tensor.matmul(ps_o[:, 0 : 2 * VD], diff_hi[i][:, t, :], v_buf[h % 2][:, t, :], start=t == 0, stop=False)
                        last = nc.tensor.matmul(ps_o[:, 0 : 2 * VD], diff_lo[i][:, t, :], v_buf[h % 2][:, t, :], start=False, stop=t == TILES - 1)
                    last.then_inc(o_done, 1)
                elif out and piece == 1:
                    pe.wait_ge(raw_done, STEPS * BATCH)
                    pe_positions(pe, TILES * (b - 1) + k - 1)
                if live[2]:
                    pe.wait_ge(hi_done, j2 + 1)
                    nc.tensor.matmul(ps_t[:, TILES // 2 :, :], neg_ident[:], diff_hi[jl % 2][:, TILES // 2 :, :], start=False, stop=True, skip_group_check=True).then_inc(rest_done, 1)

        def pe_positions(pe, n):
            pe.wait_ge(mask_done, n + 2)
            nc.tensor.matmul(ps_o[:, POS], before[:], mask[:], start=True, stop=False)
            nc.tensor.matmul(ps_o[:, POS], ones[:], mask_seen[:], start=False, stop=True).then_inc(pos_done, 1)

        def pe_piece(pe, n, piece, k):
            if piece == 0:
                pe.wait_ge(normed_done, NORMED_CREDIT + n + 1)
                pe.wait_ge(score_done, n + 1)
                for h in range(HEADS):
                    last = nc.tensor.transpose(ps_m[:, h * P : h * P + P], normed[:, h, :], ident[:])
                last.then_inc(at_done, 1)
            if piece == 1:
                pe.wait_ge(at_lo_done, n + 1)
                for e in range(KD):
                    last = split_product(nc, ps_m[:], (heads_t[0][:, e, :], heads_t[1][:, e, :]), (wo[0][:, e, :], wo[1][:, e, :]), e == 0, e == KD - 1)
                last.then_inc(y_done, 1)
            if piece == 2:
                pe.wait_ge(x1_done, n + 2)
                for c in range(KD):
                    last = nc.tensor.transpose(ps_m[:, c * P : c * P + P], x1_buf[k % 2][:, c * P : c * P + P], ident[:])
                last.then_inc(xt_done, 1)
            if piece == 3:
                pe.wait_ge(xt_lo_done, n + 1)
                for c in range(KD):
                    last = split_product(nc, ps_m[:, 0:EXPERTS], (x1_t[0][:, c, :], x1_t[1][:, c, :]), (gate[0][:, c, :], gate[1][:, c, :]), c == 0, c == KD - 1)
                last.then_inc(gate_done, 1)

        def act_turns(act, b, attn, out, first):
            for jl, live, (k, piece) in turns(attn, out, first):
                n = TILES * (b - 1) + k if out else None
                if out and piece == 2:
                    act.wait_ge(ln_done, n + 1)
                    act.wait_ge(x1_stored[k % 2], 2 * DMA * (TILES // 2 * (b - 1) + k // 2 + 1))
                    nc.scalar.activation(x1_buf[k % 2][:], summed[:], ACT.Identity, bias=shift[:], scale=rstd[:]).then_inc(x1_done, 1)
                if attn:
                    exp(act, b, jl, 0, first)
                if live[2]:
                    _, _, _, j2 = of_lag(b, jl, 2)
                    act.wait_ge(t_done, j2 + 1)
                    if not (first and jl < 4):
                        act.wait_ge(o_done, j2 - 1)
                    nc.scalar.copy(diff_hi[jl % 2][:], ps_t[:]).then_inc(hi_done, 1)
                if out and piece == 0:
                    act.wait_ge(at_done, n + 2)
                    act.wait_ge(y_done, n + 1)
                    nc.scalar.copy(heads_t[0][:], ps_m[:].rearrange("p (h t) -> p h t", t=P)).then_inc(at_hi_done, 1)
                if out and piece == 2:
                    act.wait_ge(xt_done, n + 1)
                    act.wait_ge(gate_done, n + 1)
                    nc.scalar.copy(x1_t[0][:], ps_m[:].rearrange("p (h t) -> p h t", t=P)).then_inc(xt_hi_done, 1)
                if attn:
                    exp(act, b, jl, 1, first)
                if live[3]:
                    _, _, _, j = of_lag(b, jl, 3)
                    act.wait_ge(o_done, j + 1)
                    if not (first and jl == 3):
                        act.wait_ge(raw_done, j)
                    nc.scalar.copy(cross_sum[:], ps_o[:, VD : 2 * VD]).then_inc(cross_done, 1)
                if live[4]:
                    bb, h, t, j = of_lag(b, jl, 4)
                    act.wait_ge(raw_done, j + 1)
                    if not (first and jl == 4):
                        act.wait_ge(square_done, j)
                    par = bb % 2
                    nc.scalar.activation(square_junk[:], raw[:, par, t, h, :], ACT.Square, scale=VD**-0.5, accum_out=squares[:, par, t, h : h + 1]).then_inc(square_done, 1)
                if live[2]:
                    act.wait_ge(rest_done, j2 + 1)
                    nc.scalar.copy(diff_lo[jl % 2][:, TILES // 2 :, :], ps_t[:, TILES // 2 :, :]).then_inc(lo2_done, 1)
                if out and piece == 3:
                    act.wait_ge(lmax_done, n + 1)
                    act.wait_ge(route_step, ROUTE_STEPS * (n + 1))
                    nc.scalar.activation(score_exp[:], ps_m[:, 0:EXPERTS], ACT.Exp, bias=logit_max[:], accum_out=score_sum[:]).then_inc(score_done, 1)

        def exp(act, b, jl, s, first):
            j = STEPS * b + jl
            act.wait_ge(max_done[s], j + 1)
            if not (first and jl < 2):
                act.wait_ge(diff_done, j - 1)
            i = jl % 2
            if s == 0:
                act.wait_ge(normed_done, TILES * b + jl % TILES + 1)
                total = mass0[:, b % 2, jl % TILES, jl // TILES : jl // TILES + 1]
            else:
                total = mass1[:, i : i + 1]
            nc.scalar.activation(prob[s][i][:], ps_s[s][:], ACT.Exp, bias=neg_max[:, s, i : i + 1], accum_out=total).then_inc(exp_done[s], 1)

        def dve_turns(dve, b, attn, out, first):
            for jl, live, (k, piece) in turns(attn, out, first):
                n = TILES * (b - 1) + k if out else None
                j = STEPS * b + jl
                if attn:
                    row_max(dve, j, 0, jl % 2)
                if live[4]:
                    bb, h, t, j4 = of_lag(b, jl, 4)
                    dve.wait_ge(cross_done, j4 + 1)
                    if out and piece == 2:
                        read_positions(dve, n - 1)
                    par = bb % 2
                    nc.vector.tensor_tensor(raw[:, par, t, h, :], ps_o[:, 0:VD], cross_sum[:], ALU.add).then_inc(raw_done, 1)
                elif out and piece == 2:
                    read_positions(dve, n - 1)
                if out:
                    dve_route(dve, n - 1, piece, 0)
                if live[1]:
                    bb, h, t, j1 = of_lag(b, jl, 1)
                    i = (jl - 1) % 2
                    dve.wait_ge(exp_done[1], j1 + 1)
                    nc.vector.reciprocal(mass1_inv[:, i : i + 1], mass1[:, i : i + 1]).then_inc(inv_done, 1)
                if out:
                    dve_route(dve, n - 1, piece, 1)
                if attn:
                    row_max(dve, j, 1, jl % 2)
                if live[1]:
                    dve.wait_ge(inv_done, j1 + 1)
                    nc.vector.tensor_scalar(weight2[:, i : i + 1], mass1_inv[:, i : i + 1], mass0[:, bb % 2, t, h : h + 1], neg_lam[:], ALU.mult, ALU.mult).then_inc(weight_done, 1)
                if out:
                    dve_route(dve, n - 1, piece, 2)
                if live[1]:
                    dve.wait_ge(weight_done, j1 + 1)
                    if not (first and jl < 3):
                        dve.wait_ge(t_done, j1 - 1)
                    nc.vector.scalar_tensor_tensor(diff[i][:], prob[1][i][:], weight2[:, i : i + 1], prob[0][i][:], ALU.mult, ALU.add).then_inc(diff_done, 1)
                if out:
                    dve_route(dve, n - 1, piece, 3)
                if live[2]:
                    _, _, _, j2 = of_lag(b, jl, 2)
                    dve.wait_ge(hi_done, j2 + 1)
                    nc.vector.tensor_tensor(diff_lo[jl % 2][:, 0 : TILES // 2, :], ps_t[:, 0 : TILES // 2, :], diff_hi[jl % 2][:, 0 : TILES // 2, :].bitcast(F32), ALU.subtract).then_inc(lo_done, 1)
                if out:
                    dve_route(dve, n - 1, piece, 4)
                if out and piece == 0:
                    dve.wait_ge(at_hi_done, n + 1)
                    nc.vector.tensor_tensor(heads_t[1][:], ps_m[:].rearrange("p (h t) -> p h t", t=P), heads_t[0][:].bitcast(F32), ALU.subtract).then_inc(at_lo_done, 1)
                if out and piece == 1:
                    dve.wait_ge(y_done, n + 2)
                    dve.wait_ge(x_loaded[k % 2], DMA * (TILES // 2 * (b - 1) + k // 2 + 1))
                    dve.wait_ge(x1_done, n + 1)
                    nc.vector.tensor_tensor(summed[:], ps_m[:], x_in[k % 2][:], ALU.add).then_inc(sum_done, 1)
                    dve.wait_ge(sum_done, n + 3)
                    nc.vector.bn_stats(stats[:], summed[:]).then_inc(stats_done, 1)
                    dve.wait_ge(stats_done, n + 1)
                    dve.sem_inc(held, 1)
                    nc.vector.bn_aggr(mean_var[:], stats[:]).then_inc(mv_done, 1)
                if out and piece == 2:
                    dve.wait_ge(xt_hi_done, n + 1)
                    nc.vector.tensor_tensor(x1_t[1][:], ps_m[:].rearrange("p (h t) -> p h t", t=P), x1_t[0][:].bitcast(F32), ALU.subtract).then_inc(xt_lo_done, 1)
                if out and piece == 3:
                    if k == 0:
                        dve.wait_ge(slot_done, n + 1)
                        nc.vector.memset(valid[:], 1.0)
                        nc.vector.memset(room[:], float(CAP)).then_inc(setup_dve, 1)
                        dve.wait_ge(setup_dve, SETUP_DVE + b)
                    dve.wait_ge(gate_done, n + 2)
                    nc.vector.tensor_reduce(logit_max[:], ps_m[:, 0:EXPERTS], AX.X, ALU.max, negate=True).then_inc(lmax_done, 1)

        def read_positions(dve, n):
            dve.wait_ge(pos_done, n + 2)
            nc.vector.tensor_copy(pos[:], ps_o[:, POS]).then_inc(pos_read, 1)

        def row_max(dve, j, s, i):
            dve.wait_ge(s_done[s], j + 1)
            nc.vector.tensor_reduce(neg_max[:, s, i : i + 1], ps_s[s][:], AX.X, ALU.max, negate=True).then_inc(max_done[s], 1)

        def dve_route(dve, n, piece, place):
            done = ROUTE_STEPS * (n + 1)
            if piece == 0:
                if place == 0:
                    dve.wait_ge(score_done, n + 2)
                    nc.vector.reciprocal(score_inv[:], score_sum[:]).then_inc(route_step, 1)
                if place == 1:
                    dve.wait_ge(route_step, done + 1)
                    nc.vector.tensor_scalar(score[:], score_exp[:], score_inv[:], None, ALU.mult).then_inc(route_step, 1)
                if place == 2:
                    dve.wait_ge(route_step, done + 2)
                    dve.sem_inc(held, 1)
                    nc.vector.max(top_val[:], score[:]).then_inc(route_step, 1)
                if place == 3:
                    dve.wait_ge(route_step, done + 3)
                    dve.sem_inc(held, 1)
                    nc.vector.max_index(top_idx[:], top_val[:], score[:]).then_inc(route_step, 1)
                if place == 4:
                    dve.wait_ge(route_step, done + 4)
                    nc.vector.tensor_copy(chosen[:], top_idx[:, 0:TOPK]).then_inc(route_step, 1)
            if piece == 1:
                if place == 0:
                    dve.wait_ge(route_step, done + 5)
                    nc.vector.tensor_tensor(
                        hit[:], iota[:].unsqueeze(1).to_broadcast([P, TOPK, EXPERTS]),
                        chosen[:].unsqueeze(2).to_broadcast([P, TOPK, EXPERTS]), ALU.is_equal).then_inc(route_step, 1)
                if place == 1:
                    dve.wait_ge(route_step, done + 6)
                    nc.vector.tensor_reduce(mask_f[:], hit[:].rearrange("p k e -> p e k"), AX.X, ALU.add).then_inc(route_step, 1)
                if place == 2:
                    dve.wait_ge(entry_free, n + 2)
                    nc.vector.tensor_copy(entry[:, :, 1], top_val[:, 0:TOPK])
                    nc.vector.tensor_copy(entry[:, :, 0], token[:].to_broadcast([P, TOPK])).then_inc(route_step, 1)
                    dve.wait_ge(route_step, done + 8)
                    nc.vector.tensor_scalar(mask[:], mask_f[:], valid[:], None, ALU.mult).then_inc(mask_done, 1)
            done = SLOT_STEPS * (n + 1)
            if piece == 2 and place == 3:
                dve.wait_ge(hit_pos_done, n + 2)
                nc.vector.tensor_reduce(pos_k[:], hit_pos[:], AX.X, ALU.add).then_inc(slot_step, 1)
            if piece == 2 and place == 4:
                dve.wait_ge(slot_step, done + 1)
                nc.vector.tensor_scalar(over[:], pos_k[:], room[:], BIG, ALU.is_ge, ALU.mult)
                nc.vector.scalar_tensor_tensor(slot_f[:], chosen[:], float(CAP), pos_k[:], ALU.mult, ALU.add).then_inc(slot_step, 1)
            if piece == 3 and place == 0:
                dve.wait_ge(slot_step, done + 2)
                nc.vector.tensor_tensor(slot[:], slot_f[:], over[:], ALU.add).then_inc(slot_step, 1)
                dve.wait_ge(mask_done, n + 2)
                dve.wait_ge(pos_done, n + 2)
                nc.vector.tensor_tensor(mask_seen[:], mask_seen[:], mask[:], ALU.add).then_inc(slot_step, 1)
            if piece == 3 and place == 1:
                dve.wait_ge(slot_step, done + 4)
                nc.vector.tensor_scalar_add(token[:], token[:], float(P)).then_inc(slot_done, 1)

        def pool_norm_heads(pool, b, k):
            n = TILES * b + k
            j = STEPS * b + TILES * (HEADS - 1) + k
            par = b % 2
            pool.wait_ge(exp_done[0], j + 1)
            nc.gpsimd.tensor_tensor(mass_squared[:], mass0[:, par, k, :], mass0[:, par, k, :], ALU.mult).then_inc(rms_step, 1)
            pool.wait_ge(rms_step, RMS_STEPS * n + 1)
            nc.gpsimd.tensor_tensor(eps_mass[:], mass_squared[:], eps_col[:], ALU.mult).then_inc(rms_step, 1)
            pool.wait_ge(rms_step, RMS_STEPS * n + 2)
            pool.wait_ge(square_done, j + 1)
            nc.gpsimd.tensor_tensor(rms_sum[:], squares[:, par, k, :], eps_mass[:], ALU.add).then_inc(rms_step, 1)
            pool.wait_ge(rms_step, RMS_STEPS * n + 3)
            nc.gpsimd.tensor_tensor(rms[:], rms_sum[:], pow_col[:], ALU.pow).then_inc(rms_step, 1)
            pool.wait_ge(rms_step, RMS_STEPS * n + 4)
            pool.wait_ge(at_done, n + 1)
            nc.gpsimd.tensor_tensor(normed[:], raw[:, par, k, :, :], rms[:].unsqueeze(2).to_broadcast([P, HEADS, VD]), ALU.mult).then_inc(normed_done, 1)

        def pool_tiles(pool, b, final):
            for k in range(TILES):
                n = TILES * (b - 1) + k
                pool.wait_ge(mv_done, n + 1)
                pool.wait_ge(x1_done, n + 1)
                nc.gpsimd.tensor_tensor(var_eps[:], mean_var[:, 1:2], eps_col[:, 0:1], ALU.add).then_inc(ln_step, 1)
                nc.gpsimd.tensor_tensor(neg_mean[:], zeros[:, 0:1], mean_var[:, 0:1], ALU.subtract).then_inc(ln_step, 1)
                pool.wait_ge(ln_step, LN_STEPS * n + 2)
                nc.gpsimd.tensor_tensor(rstd[:], var_eps[:], pow_col[:, 0:1], ALU.pow).then_inc(ln_step, 1)
                pool.wait_ge(ln_step, LN_STEPS * n + 3)
                nc.gpsimd.tensor_tensor(shift[:], neg_mean[:], rstd[:], ALU.mult).then_inc(ln_done, 1)
                pool_hit_pos(pool, n - 1)
                if k < TILES - 1:
                    pool_norm_heads(pool, b - 1, k + 1)
                elif not final:
                    pool_norm_heads(pool, b, 0)
                pool_scatter(pool, n - 1)

        def pool_hit_pos(pool, n):
            pool.wait_ge(pos_read, n + 2)
            pool.wait_ge(mask_done, n + 2)
            nc.gpsimd.tensor_tensor(hit_pos[:], hit[:], pos[:].unsqueeze(1).to_broadcast([P, TOPK, EXPERTS]), ALU.mult).then_inc(hit_pos_done, 1)

        def pool_scatter(pool, n):
            pool.wait_ge(slot_done, n + 2)
            pool.sem_inc(held, 1)
            for c in range(TOPK):
                nc.gpsimd.indirect_dma_start(
                    slots, bass.IndirectOffsetOnAxis(ap=slot[:, c : c + 1], axis=0), entry[:, c, :], None,
                    bounds_check=EXPERTS * CAP - 1, oob_is_err=False,
                ).then_inc(scattered, DMA)
            pool.wait_ge(scattered, DMA * TOPK * (n + 2))
            pool.sem_inc(entry_free, 1)

        with nc.Block() as block:

            @block.sync
            def _(sp):
                sp.dma_start(ident[:], ident_in).then_inc(consts_in, DMA)
                sp.dma_start(before_f[:], before_in).then_inc(consts_in, DMA)
                load_qk(sp, 0, 0, 0)
                sp.dma_start(lam_in[:], lambdas.partition_broadcast(P)).then_inc(lam_loaded, DMA)
                load_v(sp, 0, 0, 0)
                sp.dma_start(wo_raw[:], w_out.rearrange("(k p) n -> p k n", p=P)).then_inc(weights_in, DMA)
                sp.dma_start(gate_raw[:], gate_t.rearrange("(k p) n -> p k n", p=P)).then_inc(weights_in, DMA)
                sp.dma_start(subln_col[:], subln).then_inc(weights_in, DMA)
                sp.dma_start(slots, empty_slots).then_inc(pads_out, DMA)
                sp.wait_ge(setup_pool, SETUP_POOL)
                sp.dma_start(x1[TOKENS : TOKENS + CAP, :], zeros[:]).then_inc(pads_out, DMA)
                sp.dma_start(routed[TOKENS : TOKENS + CAP, :], zeros[:]).then_inc(pads_out, DMA)
                sp_turns(sp, 0, True, False, True)
                with sp.Fori(1, BATCH) as b:
                    sp_turns(sp, b, True, True, False)
                sp_turns(sp, BATCH, False, True, False)
                sp.wait_ge(qk_in[0], DMA * LOADS_QK * (BATCH * HEADS // 2 + 1))
                sp.wait_ge(v_in[0], DMA * (BATCH * HEADS // 2 + 1))
                sp.wait_ge(pads_out, 3 * DMA)
                for i in range(2):
                    sp.wait_ge(x1_stored[i], 2 * DMA * (TOKENS // P // 2 + 1))
                sp.wait_ge(scattered, DMA * TOPK * (TOKENS // P + 1))

            @block.tensor
            def _(pe):
                pe.sem_inc(at_done, 1)
                pe.sem_inc(y_done, 1)
                pe.sem_inc(gate_done, 1)
                pe.wait_ge(consts_in, 2 * DMA)
                pe.wait_ge(neg_ident_done, 1)
                pe_turns(pe, 0, True, False, True)
                pe.wait_ge(before_done, 1)
                pe.wait_ge(setup_dve, SETUP_DVE)
                pe.wait_ge(weight_step, 3)
                with pe.Fori(1, BATCH) as b:
                    pe_turns(pe, b, True, True, False)
                pe_turns(pe, BATCH, False, True, False)
                pe_positions(pe, TOKENS // P - 1)

            @block.scalar
            def _(act):
                act.sem_inc(x1_done, 1)
                act.sem_inc(score_done, 1)
                act.sem_inc(x1_stored[0], 2 * DMA)
                act.sem_inc(x1_stored[1], 2 * DMA)
                act.wait_ge(setup_dve, 2)
                nc.scalar.activation(lam_exp[:], lam_sum[:], ACT.Exp).then_inc(setup_act, 1)
                act_turns(act, 0, True, False, True)
                act.wait_ge(weight_step, 1)
                nc.scalar.copy(wo[0][:], wo_raw[:]).then_inc(setup_act, 1)
                nc.scalar.copy(gate[0][:], gate_raw[:]).then_inc(setup_act, 1)
                with act.Fori(1, BATCH) as b:
                    act_turns(act, b, True, True, False)
                act_turns(act, BATCH, False, True, False)

            @block.vector
            def _(dve):
                dve.sem_inc(sum_done, 2)
                dve.wait_ge(consts_in, 2 * DMA)
                nc.vector.tensor_scalar(neg_ident[:], ident[:], -1.0, None, ALU.mult).then_inc(neg_ident_done, 1)
                nc.vector.tensor_copy(before[:], before_f[:]).then_inc(before_done, 1)
                dve.wait_ge(lam_loaded, DMA)
                nc.vector.tensor_tensor(lam_prod[:], lam_in[:, 0:2, :], lam_in[:, 2:4, :], ALU.mult).then_inc(setup_dve, 1)
                dve.wait_ge(setup_dve, 1)
                nc.vector.tensor_reduce(lam_sum[:], lam_prod[:], AX.X, ALU.add).then_inc(setup_dve, 1)
                dve.wait_ge(setup_act, 1)
                nc.vector.tensor_tensor(lam_diff[:], lam_exp[:, 1:2], lam_exp[:, 0:1], ALU.subtract).then_inc(setup_dve, 1)
                dve.wait_ge(setup_dve, 3)
                nc.vector.tensor_scalar_add(neg_lam[:], lam_diff[:], -LAMBDA_INIT).then_inc(setup_dve, 1)
                nc.vector.memset(ones[:], 1.0).then_inc(setup_dve, 1)
                nc.vector.memset(mask_seen[:], 0.0).then_inc(setup_dve, 1)
                nc.vector.memset(valid[:], 0.0).then_inc(setup_dve, 1)
                nc.vector.memset(room[:], 0.0).then_inc(setup_dve, 1)
                dve.wait_ge(setup_pool, SETUP_POOL)
                nc.vector.tensor_copy(iota[:], iota_i[:]).then_inc(setup_dve, 1)
                nc.vector.tensor_copy(token[:], token_i[:]).then_inc(setup_dve, 1)
                dve.wait_ge(setup_dve, SETUP_DVE)
                dve_turns(dve, 0, True, False, True)
                with dve.Fori(1, BATCH) as b:
                    dve_turns(dve, b, True, True, False)
                dve_turns(dve, BATCH, False, True, False)
                n = TOKENS // P - 1
                for piece in range(4):
                    if piece == 2:
                        read_positions(dve, n)
                    for place in range(5):
                        dve_route(dve, n, piece, place)

            @block.gpsimd
            def _(pool):
                pool.sem_inc(normed_done, NORMED_CREDIT)
                pool.sem_inc(entry_free, 1)
                nc.gpsimd.memset(zeros[:], 0.0).then_inc(setup_pool, 1)
                nc.gpsimd.memset(pow_col[:], -0.5).then_inc(setup_pool, 1)
                nc.gpsimd.memset(eps_col[:], EPS).then_inc(setup_pool, 1)
                nc.gpsimd.memset(score_exp[:], 1.0).then_inc(setup_pool, 1)
                nc.gpsimd.memset(score_sum[:], 1.0).then_inc(setup_pool, 1)
                nc.gpsimd.iota(iota_i[:], [[1, EXPERTS]], base=0, channel_multiplier=0).then_inc(setup_pool, 1)
                nc.gpsimd.iota(token_i[:], [[0, 1]], base=-P, channel_multiplier=1).then_inc(setup_pool, 1)
                nc.gpsimd.memset(square_junk[:], 0.0).then_inc(setup_pool, 1)
                pool.wait_ge(setup_pool, SETUP_POOL)
                pool.wait_ge(pads_out, 3 * DMA)
                pool.wait_ge(weights_in, 3 * DMA)
                nc.gpsimd.tensor_tensor(wo_raw[:], wo_raw[:], subln_col[:].unsqueeze(2).to_broadcast([P, KD, DIM]), ALU.mult).then_inc(weight_step, 1)
                pool_norm_heads(pool, 0, 0)
                pool.wait_ge(setup_act, 3)
                nc.gpsimd.tensor_tensor(wo[1][:], wo_raw[:], wo[0][:].bitcast(F32), ALU.subtract).then_inc(weight_step, 1)
                nc.gpsimd.tensor_tensor(gate[1][:], gate_raw[:], gate[0][:].bitcast(F32), ALU.subtract).then_inc(weight_step, 1)
                with pool.Fori(1, BATCH) as b:
                    pool_tiles(pool, b, False)
                pool_tiles(pool, BATCH, True)
                pool_hit_pos(pool, TOKENS // P - 1)
                pool_scatter(pool, TOKENS // P - 1)


def experts(nc, x1, slots, w13_t, w2_t, sw13_t, sw2_t, ident_in, routed, shared_out):
    FULL = SHARED // P
    REST = SHARED - FULL * P
    UNITS = FULL + 1
    GROUPS = TOKENS // CHUNK
    PER = EXPERTS // GROUPS
    TT = CHUNK // P
    HT = -(-INTER // P)
    LAST = INTER - (HT - 1) * P
    W_LOADS = 3
    assert REST == HALF
    with Stage(nc, "exp") as st:
        sw13 = [st.sbuf(f"sw13_{part}", [P, KD, 2 * SHARED], F32R) for part in ("hi", "lo")]
        sw2 = [st.sbuf(f"sw2_{part}", [P, UNITS, DIM], F32R) for part in ("hi", "lo")]
        w13 = [st.sbuf(f"w13_{i}", [P, KD, 2 * INTER]) for i in range(2)]
        w2 = [st.sbuf(f"w2_{i}", [P, HT, DIM]) for i in range(2)]
        ident = st.sbuf("ident", [P, P])
        x_in = st.sbuf("x_in", [P, TT, DIM])
        x_t = [st.sbuf(f"x_t_{part}", [P, KD, CHUNK], F32R) for part in ("hi", "lo")]
        silu = [st.sbuf(f"silu{i}", [P, CHUNK]) for i in range(2)]
        hid = [st.sbuf(f"hid{i}", [P, CHUNK]) for i in range(2)]
        hid_hi = st.sbuf("hid_hi", [P, UNITS, CHUNK], F32R)
        hid_lo = st.sbuf("hid_lo", [P, FULL, CHUNK], F32R)
        z_buf = [st.sbuf(f"z{i}", [P, DIM]) for i in range(2)]
        table = st.sbuf("table", [EXPERTS, CAP, 2])
        row_of = st.sbuf("row_of", [P, EXPERTS], I32)
        gate_of = st.sbuf("gate_of", [P, EXPERTS])
        rows = [st.sbuf(f"rows{i}", [P, 1], I32) for i in range(2)]
        gates = [st.sbuf(f"gates{i}", [P, 1]) for i in range(2)]
        xe = [st.sbuf(f"xe{i}", [P, DIM]) for i in range(2)]
        xe_t = st.sbuf("xe_t", [P, KD, P])
        e_silu = st.sbuf("e_silu", [P, INTER])
        e_hid = st.sbuf("e_hid", [P, INTER])
        e_hid_t = st.sbuf("e_hid_t", [P, HT, P])
        ye = [st.sbuf(f"ye{i}", [P, DIM]) for i in range(2)]

        ps_ab = [st.psum(f"ps_ab{i}", [P, 2, CHUNK]) for i in range(2)]
        ps_a, ps_b, ps_et, ps_y = (st.psum(n, [P, 512]) for n in ("ps_a", "ps_b", "ps_et", "ps_y"))

        const_in, table_in, shared_in = st.sem("const_in"), st.sem("table_in"), st.sem("shared_in")
        held = st.sem("held")
        split_hi, split_lo = st.sem("split_hi"), st.sem("split_lo")
        table_t, table_done = st.sem("table_t"), st.sem("table_done")
        w_in = [st.sem(f"w_in{i}") for i in range(2)]
        gathered = [st.sem(f"gathered{i}") for i in range(2)]
        row_picked, gate_picked = st.sem("row_picked"), st.sem("gate_picked")
        added, ye_free = st.sem("added"), st.sem("ye_free")
        xet_done, xet_copied = st.sem("xet_done"), st.sem("xet_copied")
        ab_done, esilu_done, ehid_done = st.sem("ab_done"), st.sem("esilu_done"), st.sem("ehid_done")
        eht_done, eht_copied, ey_done, ye_done = (st.sem(n) for n in ("eht_done", "eht_copied", "ey_done", "ye_done"))
        x_loaded = st.sem("x_loaded")
        xt_done, xt_hi_done, xt_lo_done = st.sem("xt_done"), st.sem("xt_hi_done"), st.sem("xt_lo_done")
        up_done, silu_done, hid_done = st.sem("up_done"), st.sem("silu_done"), st.sem("hid_done")
        hid_hi_done, hid_lo_done = st.sem("hid_hi_done"), st.sem("hid_lo_done")
        z_done, z_read = st.sem("z_done"), st.sem("z_read")
        z_stored = [st.sem(f"z_stored{i}") for i in range(2)]

        PLAN = [["x", 0, 1], [2, 3, 4], [5, "z0", "z1"], ["z2", "z3", None]]

        def expert_weights(sp, e, i):
            sp.dma_start(w13[i][:], w13_t[e].rearrange("(k p) n -> p k n", p=P)).then_inc(w_in[i], DMA)
            sp.dma_start(w2[i][:, 0 : HT - 1, :], w2_t[e, 0 : (HT - 1) * P, :].rearrange("(k p) n -> p k n", p=P)).then_inc(w_in[i], DMA)
            sp.dma_start(w2[i][0:LAST, HT - 1, :], w2_t[e, (HT - 1) * P : INTER, :]).then_inc(w_in[i], DMA)

        def sp_group(sp, g, final):
            for r in range(PER):
                e = PER * g + r
                for u in PLAN[r]:
                    if u == "x" and not final:
                        sp.wait_ge(xt_done, KD * (g + 1))
                        sp.dma_start(x_in[:], x1[bass.ds((g + 1) * CHUNK, CHUNK), :].rearrange("(t p) d -> p t d", p=P)).then_inc(x_loaded, DMA)
                    if isinstance(u, str) and u[0] == "z":
                        t = int(u[1])
                        sp.wait_ge(z_read, TT * g + t + 1 + TT)
                        sp.dma_start(shared_out[bass.ds(g * CHUNK + t * P, P), :], z_buf[t % 2][:]).then_inc(z_stored[t % 2], DMA)
                if not (final and r >= PER - 2):
                    sp.wait_ge(ey_done, e + 2)
                    expert_weights(sp, e + 2, r % 2)

        def pe_group(pe, g):
            for r in range(PER):
                e, i = PER * g + r, r % 2
                pe.wait_ge(gathered[i], DMA * (PER // 2 * g + r // 2 + 1))
                pe.wait_ge(eht_copied, e + 1)
                for c in range(KD):
                    last = nc.tensor.transpose(ps_et[:, c * P : c * P + P], xe[i][:, c * P : c * P + P], ident[:])
                last.then_inc(xet_done, 1)
                pe_unit(pe, g, PLAN[r][0])
                pe.wait_ge(w_in[i], DMA * W_LOADS * (PER // 2 * g + r // 2 + 1))
                pe.wait_ge(xet_copied, e + 1)
                pe.wait_ge(ehid_done, e + 1)
                for c in range(KD):
                    nc.tensor.matmul(ps_a[:, 0:INTER], xe_t[:, c, :], w13[i][:, c, 0:INTER], start=c == 0, stop=c == KD - 1)
                    last = nc.tensor.matmul(ps_b[:, 0:INTER], xe_t[:, c, :], w13[i][:, c, INTER : 2 * INTER], start=c == 0, stop=c == KD - 1)
                last.then_inc(ab_done, 1)
                pe_unit(pe, g, PLAN[r][1])
                pe.wait_ge(ehid_done, e + 2)
                for c in range(HT):
                    w = LAST if c == HT - 1 else P
                    last = nc.tensor.transpose(ps_et[0:w, c * P : c * P + P], e_hid[:, c * P : c * P + w], ident[:])
                last.then_inc(eht_done, 1)
                pe_unit(pe, g, PLAN[r][2])
                pe.wait_ge(eht_copied, e + 2)
                pe.wait_ge(ye_done, e + 1)
                for c in range(HT):
                    w = LAST if c == HT - 1 else P
                    last = nc.tensor.matmul(ps_y[:], e_hid_t[0:w, c, :], w2[i][0:w, c, :], start=c == 0, stop=c == HT - 1)
                last.then_inc(ey_done, 1)

        def pe_unit(pe, g, u):
            if u == "x":
                pe.wait_ge(x_loaded, DMA * (g + 1))
                pe.wait_ge(z_read, TT * (g + 1))
                for c in range(KD):
                    for t in range(TT):
                        last = nc.tensor.transpose(ps_ab[c // 2][:, c % 2, t * P : t * P + P], x_in[:, t, c * P : c * P + P], ident[:])
                    last.then_inc(xt_done, 1)
            elif isinstance(u, int):
                if u < 2:
                    pe.wait_ge(xt_lo_done, KD * (g + 1))
                else:
                    pe.wait_ge(hid_done, UNITS * g + u + 1)
                tiles = [u, FULL + u] if u < FULL else [2 * FULL]
                for ab, tile in enumerate(tiles):
                    for c in range(KD):
                        cols = slice(tile * P, tile * P + P)
                        last = split_product(nc, ps_ab[u % 2][:, ab, :], (sw13[0][:, c, cols], sw13[1][:, c, cols]), (x_t[0][:, c, :], x_t[1][:, c, :]), c == 0, c == KD - 1)
                last.then_inc(up_done, 1)
            elif u is not None:
                t = int(u[1])
                pe.wait_ge(hid_lo_done, UNITS * (g + 1))
                out = ps_ab[t // 2][:, t % 2, :]
                toks = slice(t * P, t * P + P)
                for c in range(FULL):
                    split_product(nc, out, (hid_hi[:, c, toks], hid_lo[:, c, toks]), (sw2[0][:, c, :], sw2[1][:, c, :]), c == 0, False)
                nc.tensor.matmul(out, hid_hi[:, FULL, toks], sw2[0][:, FULL, :], start=False, stop=False)
                nc.tensor.matmul(out, hid_hi[:, FULL, toks], sw2[1][:, FULL, :], start=False, stop=True).then_inc(z_done, 1)

        def act_group(act, g):
            for r in range(PER):
                e, i = PER * g + r, r % 2
                act.wait_ge(xet_done, e + 2)
                act.wait_ge(ab_done, e + 1)
                nc.scalar.copy(xe_t[:], ps_et[:].rearrange("p (c t) -> p c t", t=P)).then_inc(xet_copied, 1)
                act_unit(act, g, PLAN[r][0])
                act.wait_ge(ab_done, e + 2)
                nc.scalar.activation(e_silu[:], ps_a[:, 0:INTER], ACT.Silu).then_inc(esilu_done, 1)
                act_unit(act, g, PLAN[r][1])
                act_unit(act, g, PLAN[r][2])
                act.wait_ge(ey_done, e + 2)
                act.wait_ge(gate_picked, e + 1)
                act.wait_ge(ye_free, e + 1)
                nc.scalar.activation(ye[i][:], ps_y[:], ACT.Copy, scale=gates[i][:]).then_inc(ye_done, 1)

        def act_unit(act, g, u):
            if u == "x":
                act.wait_ge(up_done, UNITS * (g + 1))
                for c in range(KD):
                    act.wait_ge(xt_done, KD * g + c + 1)
                    nc.scalar.copy(x_t[0][:, c, :], ps_ab[c // 2][:, c % 2, :]).then_inc(xt_hi_done, 1)
            elif isinstance(u, int):
                n = UNITS * g + u
                w = P if u < FULL else REST
                act.wait_ge(up_done, n + 1 + UNITS)
                act.wait_ge(hid_done, n + 1)
                nc.scalar.activation(silu[u % 2][0:w, :], ps_ab[u % 2][0:w, 0, :], ACT.Silu).then_inc(silu_done, 1)
                act.wait_ge(hid_done, n + 3)
                if u == 0:
                    act.wait_ge(z_done, TT * (g + 1))
                nc.scalar.copy(hid_hi[0:w, u, :], hid[u % 2][0:w, :]).then_inc(hid_hi_done, 1)

        def dve_group(dve, g):
            for r in range(PER):
                e, i = PER * g + r, r % 2
                dve_unit(dve, g, PLAN[r][0])
                dve.wait_ge(esilu_done, e + 1)
                dve.wait_ge(eht_done, e + 1)
                nc.vector.tensor_tensor(e_hid[:], ps_b[:, 0:INTER], e_silu[:], ALU.mult).then_inc(ehid_done, 1)
                dve_unit(dve, g, PLAN[r][1])
                dve.wait_ge(eht_done, e + 2)
                dve.wait_ge(ey_done, e + 1)
                nc.vector.tensor_copy(e_hid_t[:, 0 : HT - 1, :], ps_et[:, 0 : (HT - 1) * P].rearrange("p (c t) -> p c t", t=P))
                nc.vector.tensor_copy(e_hid_t[0:LAST, HT - 1, :], ps_et[0:LAST, (HT - 1) * P : HT * P]).then_inc(eht_copied, 1)
                dve_unit(dve, g, PLAN[r][2])

        def dve_unit(dve, g, u):
            if u == "x":
                for c in range(KD):
                    dve.wait_ge(xt_hi_done, KD * g + c + 1)
                    nc.vector.tensor_tensor(x_t[1][:, c, :], ps_ab[c // 2][:, c % 2, :], x_t[0][:, c, :].bitcast(F32), ALU.subtract).then_inc(xt_lo_done, 1)
            elif isinstance(u, int):
                n = UNITS * g + u
                dve.wait_ge(silu_done, n + 1)
                if u < FULL:
                    nc.vector.tensor_tensor(hid[u % 2][:], ps_ab[u % 2][:, 1, :], silu[u % 2][:], ALU.mult).then_inc(hid_done, 1)
                    low, w = hid_lo[:, u, :], P
                else:
                    nc.vector.tensor_tensor(hid[u % 2][0:REST, :], ps_ab[u % 2][REST:P, 0, :], silu[u % 2][0:REST, :], ALU.mult).then_inc(hid_done, 1)
                    low, w = hid_hi[REST:P, u, :], REST
                dve.wait_ge(hid_hi_done, n + 1)
                nc.vector.tensor_tensor(low, hid[u % 2][0:w, :], hid_hi[0:w, u, :].bitcast(F32), ALU.subtract).then_inc(hid_lo_done, 1)
            elif u is not None:
                t = int(u[1])
                dve.wait_ge(z_done, TT * g + t + 1 + TT)
                dve.wait_ge(z_stored[t % 2], DMA * (TT // 2 * g + t // 2 + 1))
                nc.vector.tensor_copy(z_buf[t % 2][:], ps_ab[t // 2][:, t % 2, :]).then_inc(z_read, 1)

        def pick(pool, e, i):
            nc.gpsimd.tensor_copy(rows[i][:], row_of[:, bass.ds(e, 1)]).then_inc(row_picked, 1)
            nc.gpsimd.tensor_copy(gates[i][:], gate_of[:, bass.ds(e, 1)]).then_inc(gate_picked, 1)
            pool.wait_ge(row_picked, e + 1)
            pool.wait_ge(xet_done, e)
            pool.sem_inc(held, 1)
            nc.gpsimd.indirect_dma_start(
                xe[i][:], None, x1, bass.IndirectOffsetOnAxis(ap=rows[i][:, 0:1], axis=0),
                bounds_check=TOKENS + CAP - 1, oob_is_err=False,
            ).then_inc(gathered[i], DMA)

        def pool_group(pool, g, final):
            for r in range(PER):
                e, i = PER * g + r, r % 2
                if not (final and r == PER - 1):
                    pick(pool, e + 1, 1 - i)
                pool.wait_ge(ye_done, e + 2)
                pool.sem_inc(held, 1)
                nc.gpsimd.indirect_dma_start(
                    routed, bass.IndirectOffsetOnAxis(ap=rows[i][:, 0:1], axis=0), ye[i][:], None,
                    bounds_check=TOKENS + CAP - 1, compute_op=ALU.add,
                ).then_inc(added, DMA)
                pool.wait_ge(added, DMA * (e + 1))
                pool.sem_inc(ye_free, 1)

        with nc.Block() as block:

            @block.sync
            def _(sp):
                sp.dma_start(ident[:], ident_in).then_inc(const_in, DMA)
                sp.dma_start(table[:], slots.rearrange("(e c) w -> e c w", c=CAP)).then_inc(table_in, DMA)
                for i in range(2):
                    sp.dma_start(w13[i][:], sw13_t[:, i * SHARED : (i + 1) * SHARED].rearrange("(k p) n -> p k n", p=P)).then_inc(shared_in, DMA)
                sp.dma_start(w2[0][:], sw2_t[0 : 3 * P, :].rearrange("(k p) n -> p k n", p=P)).then_inc(shared_in, DMA)
                sp.dma_start(w2[1][:, 0:2, :], sw2_t[3 * P : 5 * P, :].rearrange("(k p) n -> p k n", p=P)).then_inc(shared_in, DMA)
                for top in (0, REST):
                    sp.dma_start(w2[1][top : top + REST, 2, :], sw2_t[FULL * P : SHARED, :]).then_inc(shared_in, DMA)
                sp.dma_start(x_in[:], x1[0:CHUNK, :].rearrange("(t p) d -> p t d", p=P)).then_inc(x_loaded, DMA)
                sp.wait_ge(split_lo, 4)
                expert_weights(sp, 0, 0)
                expert_weights(sp, 1, 1)
                with sp.Fori(0, GROUPS - 1) as g:
                    sp_group(sp, g, False)
                sp_group(sp, GROUPS - 1, True)
                for i in range(2):
                    sp.wait_ge(z_stored[i], DMA * (TT // 2 * GROUPS + 1))
                sp.wait_ge(added, DMA * EXPERTS)

            @block.tensor
            def _(pe):
                pe.sem_inc(xet_done, 1)
                pe.sem_inc(ab_done, 1)
                pe.sem_inc(eht_done, 1)
                pe.sem_inc(ey_done, 1)
                pe.sem_inc(up_done, UNITS)
                pe.sem_inc(z_done, TT)
                pe.wait_ge(const_in, DMA)
                pe.wait_ge(table_in, DMA)
                for w in range(2):
                    nc.tensor.transpose(ps_y[:, w * EXPERTS : (w + 1) * EXPERTS], table[:, :, w], ident[0:EXPERTS, 0:EXPERTS]).then_inc(table_t, 1)
                pe.wait_ge(split_lo, 4)
                with pe.Fori(0, GROUPS - 1) as g:
                    pe_group(pe, g)
                pe_group(pe, GROUPS - 1)

            @block.scalar
            def _(act):
                act.sem_inc(ye_done, 1)
                act.wait_ge(shared_in, 6 * DMA)
                for i in range(2):
                    nc.scalar.copy(sw13[0][:, :, i * SHARED : (i + 1) * SHARED], w13[i][:]).then_inc(split_hi, 1)
                for i in range(2):
                    nc.scalar.copy(sw2[0][:, 3 * i : 3 * i + 3, :], w2[i][:]).then_inc(split_hi, 1)
                with act.Fori(0, GROUPS - 1) as g:
                    act_group(act, g)
                act_group(act, GROUPS - 1)

            @block.vector
            def _(dve):
                dve.sem_inc(ehid_done, 1)
                dve.sem_inc(eht_copied, 1)
                dve.sem_inc(hid_done, 2)
                dve.sem_inc(z_read, TT)
                dve.wait_ge(table_t, 2)
                nc.vector.tensor_copy(row_of[:], ps_y[:, 0:EXPERTS]).then_inc(table_done, 1)
                nc.vector.tensor_copy(gate_of[:], ps_y[:, EXPERTS : 2 * EXPERTS]).then_inc(table_done, 1)
                for i in range(2):
                    dve.wait_ge(split_hi, i + 1)
                    cols = slice(i * SHARED, (i + 1) * SHARED)
                    nc.vector.tensor_tensor(sw13[1][:, :, cols], w13[i][:], sw13[0][:, :, cols].bitcast(F32), ALU.subtract).then_inc(split_lo, 1)
                for i in range(2):
                    dve.wait_ge(split_hi, i + 3)
                    tiles = slice(3 * i, 3 * i + 3)
                    nc.vector.tensor_tensor(sw2[1][:, tiles, :], w2[i][:], sw2[0][:, tiles, :].bitcast(F32), ALU.subtract).then_inc(split_lo, 1)
                with dve.Fori(0, GROUPS - 1) as g:
                    dve_group(dve, g)
                dve_group(dve, GROUPS - 1)

            @block.gpsimd
            def _(pool):
                pool.sem_inc(ye_free, 2)
                for i in range(2):
                    pool.sem_inc(z_stored[i], DMA)
                pool.wait_ge(table_done, 2)
                nc.gpsimd.tensor_copy(rows[0][:], row_of[:, 0:1]).then_inc(row_picked, 1)
                nc.gpsimd.tensor_copy(gates[0][:], gate_of[:, 0:1]).then_inc(gate_picked, 1)
                pool.wait_ge(row_picked, 1)
                nc.gpsimd.indirect_dma_start(
                    xe[0][:], None, x1, bass.IndirectOffsetOnAxis(ap=rows[0][:, 0:1], axis=0),
                    bounds_check=TOKENS + CAP - 1, oob_is_err=False,
                ).then_inc(gathered[0], DMA)
                with pool.Fori(0, GROUPS - 1) as g:
                    pool_group(pool, g, False)
                pool_group(pool, GROUPS - 1, True)


def finish(nc, routed, shared_out, out):
    TT = 4
    GROUPS = TOKENS // (P * TT)

    def view(t):
        return t[0:TOKENS, :].rearrange("(g p t) d -> g p t d", p=P, t=TT)

    routed_v, shared_v, out_v = view(routed), view(shared_out), view(out)
    with Stage(nc, "fin") as st:
        a = [st.sbuf(f"a{i}", [P, TT, DIM]) for i in range(2)]
        z = [st.sbuf(f"z{i}", [P, TT, DIM]) for i in range(2)]
        s = [st.sbuf(f"s{i}", [P, TT, DIM]) for i in range(2)]
        o = [st.sbuf(f"o{i}", [P, TT, DIM]) for i in range(2)]
        stats = st.sbuf("stats", [P, TT, 6])
        mean_var = [st.sbuf(f"mean_var{i}", [P, TT, 2]) for i in range(2)]
        half = st.sbuf("half", [P, TT])
        var_eps = st.sbuf("var_eps", [P, TT])
        mean_rstd = st.sbuf("mean_rstd", [P, TT])
        rstd = [st.sbuf(f"rstd{i}", [P, TT]) for i in range(2)]
        shift = [st.sbuf(f"shift{i}", [P, TT]) for i in range(2)]
        loaded = [st.sem(f"loaded{i}") for i in range(2)]
        stored = [st.sem(f"stored{i}") for i in range(2)]
        summed, stats_done, mv_done, half_done = (st.sem(n) for n in ("summed", "stats_done", "mv_done", "half_done"))
        held = st.sem("held")
        pool_step, ready, normed = st.sem("pool_step"), st.sem("ready"), st.sem("normed")
        with nc.Block() as block:

            @block.sync
            def _(sp):
                with sp.Fori(0, GROUPS // 2) as gg:
                    for i in range(2):
                        g = 2 * gg + i
                        sp.wait_ge(summed, g + 1)
                        sp.dma_start(a[i][:], routed_v[g]).then_inc(loaded[i], DMA)
                        sp.dma_start(z[i][:], shared_v[g]).then_inc(loaded[i], DMA)

            @block.vector
            def _(dve):
                dve.sem_inc(summed, 2)
                with dve.Fori(0, GROUPS // 2) as gg:
                    for i in range(2):
                        g = 2 * gg + i
                        dve.wait_ge(loaded[i], 2 * DMA * (gg + 1))
                        dve.wait_ge(normed, g + 1)
                        nc.vector.tensor_tensor(s[i][:], a[i][:], z[i][:], ALU.add).then_inc(summed, 1)
                        dve.wait_ge(summed, g + 3)
                        dve.wait_ge(mv_done, g + 1)
                        for t in range(TT):
                            last = nc.vector.bn_stats(stats[:, t, :], s[i][:, t, :])
                        last.then_inc(stats_done, 1)
                        dve.wait_ge(stats_done, g + 1)
                        dve.sem_inc(held, 1)
                        for t in range(TT):
                            last = nc.vector.bn_aggr(mean_var[i][:, t, :], stats[:, t, :])
                        last.then_inc(mv_done, 1)

            @block.gpsimd
            def _(pool):
                nc.gpsimd.memset(half[:], -0.5).then_inc(half_done, 1)
                pool.wait_ge(half_done, 1)
                with pool.Fori(0, GROUPS // 2) as gg:
                    for i in range(2):
                        g = 2 * gg + i
                        pool.wait_ge(mv_done, g + 2)
                        pool.wait_ge(normed, g + 1)
                        pool.sem_inc(held, 1)
                        nc.gpsimd.tensor_scalar(var_eps[:], mean_var[i][:, :, 1], EPS, 1.0, ALU.add, ALU.mult).then_inc(pool_step, 1)
                        pool.wait_ge(pool_step, 3 * g + 1)
                        nc.gpsimd.tensor_tensor(rstd[i][:], var_eps[:], half[:], ALU.pow).then_inc(pool_step, 1)
                        pool.wait_ge(pool_step, 3 * g + 2)
                        nc.gpsimd.tensor_tensor(mean_rstd[:], mean_var[i][:, :, 0], rstd[i][:], ALU.mult).then_inc(pool_step, 1)
                        pool.wait_ge(pool_step, 3 * g + 3)
                        pool.sem_inc(held, 1)
                        nc.gpsimd.tensor_scalar(shift[i][:], mean_rstd[:], -1.0, 0.0, ALU.mult, ALU.add).then_inc(ready, 1)

            @block.scalar
            def _(act):
                act.sem_inc(normed, 2)
                act.sem_inc(mv_done, 1)
                for i in range(2):
                    act.sem_inc(stored[i], DMA)
                with act.Fori(0, GROUPS // 2) as gg:
                    for i in range(2):
                        g = 2 * gg + i
                        act.wait_ge(ready, g + 1)
                        act.wait_ge(stored[i], DMA * (gg + 1))
                        for t in range(TT):
                            last = nc.scalar.activation(o[i][:, t, :], s[i][:, t, :], ACT.Identity, bias=shift[i][:, t : t + 1], scale=rstd[i][:, t : t + 1])
                        last.then_inc(normed, 1)
                        act.wait_ge(normed, g + 3)
                        act.dma_start(out_v[g], o[i][:]).then_inc(stored[i], DMA)
                for i in range(2):
                    act.wait_ge(stored[i], DMA * (GROUPS // 2 + 1))


def layer(nc, x, x_t, w_qk, w_v, w_out, lambdas, subln, gate_t, w13_t, w2_t, sw13_t, sw2_t, rope, ident, before, empty_slots, out):
    q_parts = nc.dram_tensor("q_parts", (BATCH, 2, 2, SUBS * FREQ, SEQ), F32).ap()
    k_parts = nc.dram_tensor("k_parts", (BATCH, 2, 2, SUBS * FREQ, SEQ), F32).ap()
    v_parts = nc.dram_tensor("v_parts", (BATCH, HEADS, SEQ, 2 * VD), F32).ap()
    x1 = nc.dram_tensor("x1", (TOKENS + CAP, DIM), F32).ap()
    routed = nc.dram_tensor("routed", (TOKENS + CAP, DIM), F32).ap()
    shared_out = nc.dram_tensor("shared_out", (TOKENS, DIM), F32).ap()
    slots = nc.dram_tensor("slots", (EXPERTS * CAP, 2), F32).ap()
    project(nc, x_t, w_qk, w_v, (rope[0], rope[2]), (rope[1], rope[3]), q_parts, k_parts, v_parts)
    attend(nc, q_parts, k_parts, v_parts, x, lambdas, subln, w_out, gate_t, ident, before, empty_slots, x1, routed, slots)
    experts(nc, x1, slots, w13_t, w2_t, sw13_t, sw2_t, ident, routed, shared_out)
    finish(nc, routed, shared_out, out)


def shape_constants():
    inv = 1.0 / 10000.0 ** (np.arange(0, HALF, 2)[: HALF // 2].astype(np.float64) / HALF)
    angle = np.outer(np.arange(SEQ), inv)
    cos = np.tile(np.cos(angle).astype(np.float32).T, (GROUP, 1))
    sin = np.tile(np.sin(angle).astype(np.float32).T, (GROUP, 1))
    plain, cross = np.stack([cos, sin], 1), np.stack([-sin, cos], 1)
    rope = np.stack([plain * np.float32(SCALE), cross * np.float32(SCALE), plain, cross])
    ident = np.eye(P, dtype=np.float32)
    before = np.triu(np.ones((P, P), np.float32), 1)
    empty = np.zeros((EXPERTS * CAP, 2), np.float32)
    empty[:, 0] = TOKENS + np.tile(np.arange(CAP), EXPERTS)
    return {"rope": np.ascontiguousarray(rope), "ident": ident, "before": before, "empty_slots": empty}


def by_rotation(w):
    w = w.reshape(SUBS // GROUP, GROUP, FREQ, 2, DIM)
    return w.transpose(0, 3, 1, 2, 4).reshape(DIM, DIM).T


def kernel(**inputs):
    import concourse.bacc as bacc
    from concourse.bass_utils import run_bass_kernel_spmd

    a = {name.removeprefix("L0_"): np.asarray(value) for name, value in inputs.items()}
    x = a["attn_x"].reshape(TOKENS, DIM)
    sw1, sw3 = a["ffn_sw1"], a["ffn_sw3"]
    full = SHARED // P * P
    arrays = {
        "x": x,
        "x_t": x.T,
        "w_qk": np.concatenate([by_rotation(a["attn_wq"]), by_rotation(a["attn_wk"])], 1),
        "w_v": a["attn_wv"].T,
        "w_out": a["attn_wout"].T,
        "lambdas": np.stack([a[f"attn_lambda_{n}"] for n in ("q1", "q2", "k1", "k2")]),
        "subln": a["attn_subln_weight"][:, None],
        "gate_t": a["ffn_gate_w"].T,
        "w13_t": np.concatenate([a["ffn_w1"].transpose(0, 2, 1), a["ffn_w3"].transpose(0, 2, 1)], 2),
        "w2_t": a["ffn_w2"].transpose(0, 2, 1),
        "sw13_t": np.concatenate([sw1[:full], sw3[:full], sw1[full:], sw3[full:]]).T,
        "sw2_t": a["ffn_sw2"].T,
        **shape_constants(),
    }
    nc = bacc.Bacc("TRN2", target_bir_lowering=False, num_devices=1)
    args = {}
    for name, value in arrays.items():
        arrays[name] = value = np.ascontiguousarray(value)
        args[name] = nc.dram_tensor(f"in_{name}", value.shape, mybir.dt.from_np(value.dtype), kind="ExternalInput").ap()
    out = nc.dram_tensor("out", (TOKENS, DIM), F32, kind="ExternalOutput").ap()
    layer(nc, out=out, **args)
    result = run_bass_kernel_spmd(nc, [{f"in_{name}": value for name, value in arrays.items()}], core_ids=[0])
    return result.results[0]["out"].reshape(BATCH, SEQ, DIM)
```

```python
from contextlib import ExitStack

import numpy as np

import concourse.bass as bass
from concourse import mybir

F32 = mybir.dt.float32
F32R = mybir.dt.float32r
BF16 = mybir.dt.bfloat16
I32 = mybir.dt.int32
U32 = mybir.dt.uint32
ALU = mybir.AluOpType
ACT = mybir.ActivationFunctionType
AX = mybir.AxisListType

P = 128
BATCH, SEQ, DIM = 8, 1024, 512
TOKENS = BATCH * SEQ
KD = DIM // P
HALF = 64
SUBS = DIM // HALF
HEADS = SUBS // 2
VD = 2 * HALF
FREQ = HALF // 2
GROUP = P // FREQ
LAMBDA_INIT = 0.8 - 0.6 * float(np.exp(-0.3 * 12))
SCALE = 1.0 / (128**-0.5)
EPS = 1e-5
EXPERTS, TOPK, CAP, INTER = 64, 6, 128, 352
SHARED = 704
CHUNK = 512
DMA = 16


class Stage:

    def __init__(self, nc, name):
        self.nc, self.name, self.stack = nc, name, ExitStack()

    def __enter__(self):
        return self

    def __exit__(self, *error):
        return self.stack.__exit__(*error)

    def sbuf(self, name, shape, dt=F32):
        return self.stack.enter_context(self.nc.sbuf_tensor(f"{self.name}_{name}", shape, dt))

    def psum(self, name, shape, dt=F32):
        return self.stack.enter_context(self.nc.psum_tensor(f"{self.name}_{name}", shape, dt))

    def sem(self, name):
        return self.stack.enter_context(self.nc.semaphore(f"{self.name}_{name}"))


def split_product(nc, out, lhs, rhs, first, last):
    nc.tensor.matmul(out, lhs[0], rhs[0], start=first, stop=False)
    nc.tensor.matmul(out, lhs[0], rhs[1], start=False, stop=False)
    return nc.tensor.matmul(out, lhs[1], rhs[0], start=False, stop=last)


def project(nc, x_t, w_qk, w_v, rope_plain, rope_cross, q_parts, k_parts, v_parts):
    x_view = x_t.rearrange("(k p) t -> p k t", p=P)
    with Stage(nc, "proj") as st:
        raw_qk = st.sbuf("raw_qk", [P, KD, 2 * DIM])
        raw_v = st.sbuf("raw_v", [P, KD, DIM])
        wqk = [st.sbuf(f"wqk_{part}", [P, KD, 2 * DIM], F32R) for part in ("hi", "lo")]
        wv = [st.sbuf(f"wv_{part}", [P, KD, DIM], F32R) for part in ("hi", "lo")]
        plain = [st.sbuf(f"plain{i}", [P, 2, SEQ]) for i in range(2)]
        cross = [st.sbuf(f"cross{i}", [P, 2, SEQ]) for i in range(2)]
        x_raw = [st.sbuf(f"x_raw{i}", [P, KD, CHUNK]) for i in range(2)]
        x_hi = [st.sbuf(f"x_hi{i}", [P, KD, CHUNK], F32R) for i in range(2)]
        x_lo = [st.sbuf(f"x_lo{i}", [P, KD, CHUNK], F32R) for i in range(2)]
        by_real = [st.sbuf(f"by_real{i}", [P, 2, CHUNK]) for i in range(2)]
        by_imag = [st.sbuf(f"by_imag{i}", [P, 2, CHUNK]) for i in range(2)]
        turned = [st.sbuf(f"turned{i}", [P, 2, CHUNK]) for i in range(2)]
        out_hi = [st.sbuf(f"out_hi{i}", [P, 2, CHUNK], F32R) for i in range(2)]
        out_lo = [st.sbuf(f"out_lo{i}", [P, 2, CHUNK], F32R) for i in range(2)]
        v_out = [st.sbuf(f"v_out{i}", [P, HEADS, 2, VD], F32R) for i in range(2)]
        ps_qk = [st.psum(f"ps_qk{i}", [P, 2, CHUNK]) for i in range(2)]
        ps_v = [st.psum(f"ps_v{i}", [P, HEADS, VD]) for i in range(2)]

        w_in = {name: st.sem(f"w_in_{name}") for name in "qvk"}
        tables_in = [st.sem(f"tables_in{i}") for i in range(2)]
        w_hi, w_lo = st.sem("w_hi"), st.sem("w_lo")
        x_in = [st.sem(f"x_in{i}") for i in range(2)]
        x_hi_done, x_lo_done = st.sem("x_hi_done"), st.sem("x_lo_done")
        qk_done, qk_read = st.sem("qk_done"), st.sem("qk_read")
        real_done, imag_done, turned_done = st.sem("real_done"), st.sem("imag_done"), st.sem("turned_done")
        hi_done, lo_done = st.sem("hi_done"), st.sem("lo_done")
        v_done, v_hi_done, v_lo_done = st.sem("v_done"), st.sem("v_hi_done"), st.sem("v_lo_done")
        qk_stored = [st.sem(f"qk_stored{i}") for i in range(2)]
        v_stored = [st.sem(f"v_stored{i}") for i in range(2)]

        q_cols, k_cols = slice(0, DIM), slice(DIM, 2 * DIM)
        weights = {
            "q": (raw_qk[:, :, q_cols], w_qk[:, q_cols], [w[:, :, q_cols] for w in wqk]),
            "v": (raw_v[:], w_v, [w[:] for w in wv]),
            "k": (raw_qk[:, :, k_cols], w_qk[:, k_cols], [w[:, :, k_cols] for w in wqk]),
        }
        PAIRS = 2 * SUBS // GROUP
        VT = CHUNK // P
        chunks = 2 * BATCH

        with nc.Block() as block:

            @block.sync
            def _(sp):
                sp.dma_start(x_raw[0][:], x_view[:, :, 0:CHUNK]).then_inc(x_in[0], DMA)
                for name in "qvk":
                    raw, source, _ = weights[name]
                    sp.dma_start(raw, source.rearrange("(k p) n -> p k n", p=P)).then_inc(w_in[name], DMA)
                    if name != "q":
                        i = "vk".index(name)
                        sp.dma_start(plain[i][:], rope_plain[i]).then_inc(tables_in[i], DMA)
                        sp.dma_start(cross[i][:], rope_cross[i]).then_inc(tables_in[i], DMA)
                with sp.Fori(0, BATCH) as b:
                    for half in range(2):
                        c = 2 * b + half
                        nxt = 1 - half
                        sp.wait_ge(x_lo_done, c + 1)
                        at = ((c + 1) % chunks) * CHUNK
                        sp.dma_start(x_raw[nxt][:], x_view[:, :, bass.ds(at, CHUNK)]).then_inc(x_in[nxt], DMA)
                        for m in range(PAIRS):
                            parts = (q_parts, k_parts)[m // 2]
                            rows = slice(P * (m % 2), P * (m % 2) + P)
                            cols = slice(half * CHUNK, half * CHUNK + CHUNK)
                            sp.wait_ge(hi_done, PAIRS * c + m + 1)
                            for ri in range(2):
                                sp.dma_start(parts[b, 0, ri, rows, cols], out_hi[m % 2][:, ri, :].bitcast(F32)).then_inc(qk_stored[m % 2], DMA)
                            sp.wait_ge(lo_done, PAIRS * c + m + 1)
                            for ri in range(2):
                                sp.dma_start(parts[b, 1, ri, rows, cols], out_lo[m % 2][:, ri, :].bitcast(F32)).then_inc(qk_stored[m % 2], DMA)
                            sp.wait_ge(v_lo_done, VT * c + m + 1 + 2)
                            s0 = half * CHUNK + m * P
                            sp.dma_start(
                                v_parts[b, :, s0 : s0 + P, :].rearrange("h s c -> s h c"),
                                v_out[m % 2][:].rearrange("p h l c -> p h (l c)").bitcast(F32),
                            ).then_inc(v_stored[m % 2], DMA)
                for i in range(2):
                    sp.wait_ge(qk_stored[i], 4 * DMA * (PAIRS // 2 * chunks + 1))
                    sp.wait_ge(v_stored[i], DMA * (VT // 2 * chunks + 1))
                sp.wait_ge(x_in[0], DMA * (BATCH + 1))

            @block.scalar
            def _(act):
                act.sem_inc(qk_stored[0], 4 * DMA)
                act.sem_inc(qk_stored[1], 4 * DMA)
                act.sem_inc(v_stored[0], DMA)
                act.sem_inc(v_stored[1], DMA)
                act.wait_ge(x_in[0], DMA)
                nc.scalar.copy(x_hi[0][:], x_raw[0][:]).then_inc(x_hi_done, 1)
                for name in "qvk":
                    raw, _, parts = weights[name]
                    act.wait_ge(w_in[name], DMA)
                    nc.scalar.copy(parts[0], raw).then_inc(w_hi, 1)
                with act.Fori(0, BATCH) as b:
                    for half in range(2):
                        c = 2 * b + half
                        nxt = 1 - half
                        act.wait_ge(v_done, VT * (c + 2))
                        act.wait_ge(x_in[nxt], DMA * (b + 1 + half))
                        nc.scalar.copy(x_hi[nxt][:], x_raw[nxt][:]).then_inc(x_hi_done, 1)
                        for m in range(PAIRS):
                            n = PAIRS * c + m
                            act.wait_ge(turned_done, n + 1)
                            act.wait_ge(qk_stored[m % 2], 4 * DMA * (2 * c + m // 2 + 1))
                            nc.scalar.copy(out_hi[m % 2][:], turned[m % 2][:]).then_inc(hi_done, 1)
                            act.wait_ge(v_done, VT * (c + 2) + m + 1)
                            act.wait_ge(v_stored[m % 2], DMA * (2 * c + m // 2 + 1))
                            nc.scalar.copy(v_out[m % 2][:, :, 0, :], ps_v[m % 2][:]).then_inc(v_hi_done, 1)

            @block.vector
            def _(dve):
                dve.sem_inc(qk_read, 2)
                dve.sem_inc(v_lo_done, 2)
                dve.wait_ge(x_hi_done, 1)
                nc.vector.tensor_tensor(x_lo[0][:], x_raw[0][:], x_hi[0][:].bitcast(F32), ALU.subtract).then_inc(x_lo_done, 1)
                for n, name in enumerate("qvk"):
                    raw, _, (high, low) = weights[name]
                    dve.wait_ge(w_hi, n + 1)
                    nc.vector.tensor_tensor(low, raw, high.bitcast(F32), ALU.subtract).then_inc(w_lo, 1)

                def qk_low(c, m):
                    dve.wait_ge(hi_done, PAIRS * c + m + 1)
                    nc.vector.tensor_tensor(out_lo[m % 2][:], turned[m % 2][:], out_hi[m % 2][:].bitcast(F32), ALU.subtract).then_inc(lo_done, 1)

                def v_low(c, m):
                    dve.wait_ge(v_hi_done, VT * c + m + 1)
                    nc.vector.tensor_tensor(v_out[m % 2][:, :, 1, :], ps_v[m % 2][:], v_out[m % 2][:, :, 0, :].bitcast(F32), ALU.subtract).then_inc(v_lo_done, 1)

                with dve.Fori(0, BATCH) as b:
                    for half in range(2):
                        c = 2 * b + half
                        nxt = 1 - half
                        cols = slice(half * CHUNK, half * CHUNK + CHUNK)
                        for m in range(PAIRS):
                            n = PAIRS * c + m
                            i = m % 2
                            dve.wait_ge(qk_done, n + 1)
                            dve.wait_ge(tables_in[m // 2], 2 * DMA)
                            for src, table, dst, sem in ((0, plain, by_real, real_done), (1, cross, by_imag, imag_done)):
                                nc.vector.tensor_tensor(
                                    dst[i][:],
                                    ps_qk[i][:, src : src + 1, :].to_broadcast([P, 2, CHUNK]),
                                    table[m // 2][:, :, cols],
                                    ALU.mult,
                                ).then_inc(sem if src == 0 else qk_read, 1)
                            dve.wait_ge(real_done, n + 1)
                            dve.wait_ge(qk_read, n + 3)
                            nc.vector.tensor_tensor(turned[i][:], by_real[i][:], by_imag[i][:], ALU.add).then_inc(turned_done, 1)
                            if m:
                                qk_low(c, m - 1)
                                v_low(c, m - 1)
                            if m == 1:
                                dve.wait_ge(x_hi_done, c + 2)
                                nc.vector.tensor_tensor(x_lo[nxt][:], x_raw[nxt][:], x_hi[nxt][:].bitcast(F32), ALU.subtract).then_inc(x_lo_done, 1)
                        qk_low(c, PAIRS - 1)
                        v_low(c, PAIRS - 1)

            @block.tensor
            def _(pe):
                pe.sem_inc(v_done, 2 * VT)
                with pe.Fori(0, BATCH) as b:
                    for half in range(2):
                        c = 2 * b + half
                        pe.wait_ge(x_lo_done, c + 1)
                        for m in range(PAIRS):
                            pe.wait_ge(qk_read, PAIRS * c + m + 1)
                            pe.wait_ge(w_lo, 1 if m < PAIRS // 2 else 3)
                            for ri in range(2):
                                cols = slice((2 * m + ri) * P, (2 * m + ri) * P + P)
                                for k in range(KD):
                                    last = split_product(
                                        nc, ps_qk[m % 2][:, ri, :],
                                        (wqk[0][:, k, cols], wqk[1][:, k, cols]),
                                        (x_hi[half][:, k, :], x_lo[half][:, k, :]),
                                        k == 0, k == KD - 1)
                            last.then_inc(qk_done, 1)
                            pe.wait_ge(v_lo_done, VT * c + m + 1)
                            pe.wait_ge(w_lo, 2)
                            toks = slice(m * P, m * P + P)
                            for k in range(KD):
                                last = split_product(
                                    nc, ps_v[m % 2][:],
                                    (x_hi[half][:, k, toks], x_lo[half][:, k, toks]),
                                    (wv[0][:, k, :], wv[1][:, k, :]),
                                    k == 0, k == KD - 1)
                            last.then_inc(v_done, 1)


def attend(nc, q_parts, k_parts, v_parts, x, lambdas, subln, w_out, gate_t, ident_in, before_in, empty_slots, x1, total, slots):
    TILES = SEQ // P
    STEPS = HEADS * TILES
    LOADS_QK = 12
    BIG = 1.0e6
    with Stage(nc, "att") as st:
        q_buf = [st.sbuf(f"q{i}", [P, 2, SEQ], F32R) for i in range(2)]
        k_hi = [st.sbuf(f"k_hi{i}", [P, 2, SEQ], F32R) for i in range(2)]
        k_lo = [st.sbuf(f"k_lo{i}", [P, 2, SEQ], F32R) for i in range(2)]
        v_buf = [st.sbuf(f"v{i}", [P, TILES, 2 * VD], F32R) for i in range(2)]
        prob = [[st.sbuf(f"prob{s}{i}", [P, SEQ]) for i in range(2)] for s in range(2)]
        diff = [st.sbuf(f"diff{i}", [P, SEQ]) for i in range(2)]
        diff_hi = [st.sbuf(f"diff_hi{i}", [P, TILES, P], F32R) for i in range(2)]
        diff_lo = [st.sbuf(f"diff_lo{i}", [P, TILES, P], F32R) for i in range(2)]
        neg_max = st.sbuf("neg_max", [P, 2, 2])
        mass0 = st.sbuf("mass0", [P, 2, TILES, HEADS])
        mass1 = st.sbuf("mass1", [P, 2])
        mass1_inv = st.sbuf("mass1_inv", [P, 2])
        weight2 = st.sbuf("weight2", [P, 2])
        lam_in = st.sbuf("lam_in", [P, 4, HALF])
        lam_prod = st.sbuf("lam_prod", [P, 2, HALF])
        lam_sum = st.sbuf("lam_sum", [P, 2])
        lam_exp = st.sbuf("lam_exp", [P, 2])
        lam_diff = st.sbuf("lam_diff", [P, 1])
        neg_lam = st.sbuf("neg_lam", [P, 1])
        cross_sum = st.sbuf("cross_sum", [P, VD])
        raw = st.sbuf("raw", [P, 2, TILES, HEADS, VD])
        squares = st.sbuf("squares", [P, 2, TILES, HEADS])
        mass_squared = st.sbuf("mass_squared", [P, HEADS])
        eps_mass = st.sbuf("eps_mass", [P, HEADS])
        eps_col = st.sbuf("eps_col", [P, HEADS])
        square_junk = st.sbuf("square_junk", [P, VD])
        wo_raw = st.sbuf("wo_raw", [P, KD, DIM])
        wo = [st.sbuf(f"wo_{part}", [P, KD, DIM], F32R) for part in ("hi", "lo")]
        subln_col = st.sbuf("subln_col", [P, 1])
        gate_raw = st.sbuf("gate_raw", [P, KD, EXPERTS])
        gate = [st.sbuf(f"gate_{part}", [P, KD, EXPERTS], F32R) for part in ("hi", "lo")]
        ident = st.sbuf("ident", [P, P])
        neg_ident = st.sbuf("neg_ident", [P, P], F32R)
        before_f = st.sbuf("before_f", [P, P])
        before = st.sbuf("before", [P, P], BF16)
        ones = st.sbuf("ones", [P, P], BF16)
        zeros = st.sbuf("zeros", [P, DIM])
        iota_i = st.sbuf("iota_i", [P, EXPERTS], I32)
        iota = st.sbuf("iota", [P, EXPERTS])
        token_i = st.sbuf("token_i", [P, 1], I32)
        token = st.sbuf("token", [P, 1])
        pow_col = st.sbuf("pow_col", [P, HEADS])
        rms_sum = st.sbuf("rms_sum", [P, HEADS])
        rms = st.sbuf("rms", [P, HEADS])
        normed = st.sbuf("normed", [P, HEADS, VD])
        heads_t = [st.sbuf(f"heads_t_{part}", [P, KD, P], F32R) for part in ("hi", "lo")]
        x_in = [st.sbuf(f"x_in{i}", [P, DIM]) for i in range(2)]
        summed = st.sbuf("summed", [P, DIM])
        stats = st.sbuf("stats", [P, 6])
        mean_var = st.sbuf("mean_var", [P, 2])
        var_eps = st.sbuf("var_eps", [P, 1])
        neg_mean = st.sbuf("neg_mean", [P, 1])
        rstd = st.sbuf("rstd", [P, 1])
        shift = st.sbuf("shift", [P, 1])
        x1_buf = [st.sbuf(f"x1_{i}", [P, DIM]) for i in range(2)]
        x1_t = [st.sbuf(f"x1_t_{part}", [P, KD, P], F32R) for part in ("hi", "lo")]
        logit_max = st.sbuf("logit_max", [P, 1])
        score_exp = st.sbuf("score_exp", [P, EXPERTS])
        score_sum = st.sbuf("score_sum", [P, 1])
        score_inv = st.sbuf("score_inv", [P, 1])
        score = st.sbuf("score", [P, EXPERTS])
        top_val = st.sbuf("top_val", [P, 8])
        top_idx = st.sbuf("top_idx", [P, 8], U32)
        chosen = st.sbuf("chosen", [P, TOPK])
        hit = st.sbuf("hit", [P, TOPK, EXPERTS])
        mask_f = st.sbuf("mask_f", [P, EXPERTS])
        mask = st.sbuf("mask", [P, EXPERTS], BF16)
        mask_seen = st.sbuf("mask_seen", [P, EXPERTS], BF16)
        pos = st.sbuf("pos", [P, EXPERTS])
        hit_pos = st.sbuf("hit_pos", [P, TOPK, EXPERTS])
        pos_k = st.sbuf("pos_k", [P, TOPK])
        over = st.sbuf("over", [P, TOPK])
        slot_f = st.sbuf("slot_f", [P, TOPK])
        slot = st.sbuf("slot", [P, TOPK], I32)
        entry = st.sbuf("entry", [P, TOPK, 2])
        valid = st.sbuf("valid", [P, 1])
        room = st.sbuf("room", [P, 1])

        ps_s = [st.psum(f"ps_s{s}", [P, SEQ]) for s in range(2)]
        ps_t = st.psum("ps_t", [P, TILES, P])
        ps_o = st.psum("ps_o", [P, 512])
        ps_m = st.psum("ps_m", [P, 512])
        POS = slice(2 * VD, 2 * VD + EXPERTS)

        weights_in, lam_loaded, consts_in, pads_out = (st.sem(n) for n in ("weights_in", "lam_loaded", "consts_in", "pads_out"))
        held = st.sem("held")
        neg_ident_done, before_done = st.sem("neg_ident_done"), st.sem("before_done")
        weight_step = st.sem("weight_step")
        setup_pool, setup_dve, setup_act = st.sem("setup_pool"), st.sem("setup_dve"), st.sem("setup_act")
        qk_in = [st.sem(f"qk_in{i}") for i in range(2)]
        v_in = [st.sem(f"v_in{i}") for i in range(2)]
        s_done = [st.sem(f"s_done{s}") for s in range(2)]
        max_done = [st.sem(f"max_done{s}") for s in range(2)]
        exp_done = [st.sem(f"exp_done{s}") for s in range(2)]
        inv_done, weight_done, diff_done = st.sem("inv_done"), st.sem("weight_done"), st.sem("diff_done")
        t_done, hi_done, lo_done = st.sem("t_done"), st.sem("hi_done"), st.sem("lo_done")
        rest_done, lo2_done = st.sem("rest_done"), st.sem("lo2_done")
        o_done, cross_done, raw_done, square_done = (st.sem(n) for n in ("o_done", "cross_done", "raw_done", "square_done"))
        rms_step, normed_done = st.sem("rms_step"), st.sem("normed_done")
        at_done, at_hi_done, at_lo_done = st.sem("at_done"), st.sem("at_hi_done"), st.sem("at_lo_done")
        x_loaded = [st.sem(f"x_loaded{i}") for i in range(2)]
        y_done, sum_done, stats_done, mv_done = (st.sem(n) for n in ("y_done", "sum_done", "stats_done", "mv_done"))
        ln_step, ln_done, x1_done = st.sem("ln_step"), st.sem("ln_done"), st.sem("x1_done")
        x1_stored = [st.sem(f"x1_stored{i}") for i in range(2)]
        xt_done, xt_hi_done, xt_lo_done = st.sem("xt_done"), st.sem("xt_hi_done"), st.sem("xt_lo_done")
        gate_done, lmax_done, score_done = st.sem("gate_done"), st.sem("lmax_done"), st.sem("score_done")
        hit_pos_done = st.sem("hit_pos_done")
        route_step, mask_done, pos_done, pos_read = (st.sem(n) for n in ("route_step", "mask_done", "pos_done", "pos_read"))
        slot_step, slot_done, scattered, entry_free = (st.sem(n) for n in ("slot_step", "slot_done", "scattered", "entry_free"))

        SETUP_POOL, SETUP_DVE = 8, 10
        NORMED_CREDIT = 2 * TILES
        ROUTE_STEPS, SLOT_STEPS, RMS_STEPS, LN_STEPS = 8, 4, 4, 3

        def of_lag(b, jl, lag):
            jj = jl - lag
            bb = b if jj >= 0 else b - 1
            jj = jj % STEPS
            return bb, jj // TILES, jj % TILES, bb * STEPS + jj

        def turns(attn, out, first, lag_max=4):
            for jl in range(STEPS):
                live = {lag: (jl >= lag if first else (attn or jl < lag)) for lag in range(lag_max + 1)}
                yield jl, live, (jl // 4, jl % 4) if out else (None, None)

        def sp_turns(sp, b, attn, out, first):
            for jl, live, (k, piece) in turns(attn, out, first):
                h, t = jl // TILES, jl % TILES
                if attn:
                    nb, nh = (b, h + 1) if h + 1 < HEADS else (b + 1, 0)
                    i = nh % 2
                    skip = first and h == 0
                    if t == 1:
                        if not skip:
                            sp.wait_ge(s_done[1], STEPS * b + TILES * h)
                        load_qk(sp, nb, nh, i)
                    if t == 5:
                        if not skip:
                            sp.wait_ge(o_done, STEPS * b + TILES * h)
                        load_v(sp, nb, nh, i)
                if out:
                    n = TILES * (b - 1) + k
                    if piece == 0:
                        sp.wait_ge(sum_done, n + 1)
                        sp.dma_start(x_in[k % 2][:], x[bass.ds(n * P, P), :]).then_inc(x_loaded[k % 2], DMA)
                    if piece == 2:
                        sp.wait_ge(x1_done, n + 2)
                        sp.dma_start(x1[bass.ds(n * P, P), :], x1_buf[k % 2][:]).then_inc(x1_stored[k % 2], DMA)
                        sp.dma_start(total[bass.ds(n * P, P), :], x1_buf[k % 2][:]).then_inc(x1_stored[k % 2], DMA)

        def load_qk(sp, b, h, i):
            if isinstance(b, int) and b >= BATCH:
                return
            if not isinstance(b, int) and h == 0:
                b = b % BATCH
            src = slice(2 * h * FREQ, (2 * h + 2) * FREQ)
            for part in range(2):
                for ri in range(2):
                    def rows(parts, p):
                        return parts[b, p, ri, src, :].rearrange("(s f) t -> f s t", s=2)

                    at = 2 * part * FREQ + ri * FREQ
                    sp.dma_start(q_buf[i][at : at + FREQ].bitcast(F32), rows(q_parts, part)).then_inc(qk_in[i], DMA)
                    sp.dma_start(k_hi[i][at : at + FREQ].bitcast(F32), rows(k_parts, 0)).then_inc(qk_in[i], DMA)
                    sp.dma_start(k_lo[i][at : at + FREQ].bitcast(F32), rows(k_parts, 1)).then_inc(qk_in[i], DMA)

        def load_v(sp, b, h, i):
            if not isinstance(b, int) and h == 0:
                b = b % BATCH
            sp.dma_start(v_buf[i][:].bitcast(F32), v_parts[b, h].rearrange("(t p) c -> p t c", p=P)).then_inc(v_in[i], DMA)

        def pe_turns(pe, b, attn, out, first):
            for jl, live, (k, piece) in turns(attn, out, first):
                if attn:
                    h, t, j = jl // TILES, jl % TILES, STEPS * b + jl
                    if t == 0:
                        pe.wait_ge(qk_in[h % 2], DMA * LOADS_QK * (2 * b + h // 2 + 1))
                    q_cols = slice(t * P, t * P + P)
                    for s in range(2):
                        if not (first and jl == 0):
                            pe.wait_ge(exp_done[s], j)
                        for half in range(2):
                            cols = slice(half * CHUNK, half * CHUNK + CHUNK)
                            nc.tensor.matmul(ps_s[s][:, cols], q_buf[h % 2][:, s, q_cols], k_hi[h % 2][:, s, cols], start=True, stop=False)
                            last = nc.tensor.matmul(ps_s[s][:, cols], q_buf[h % 2][:, s, q_cols], k_lo[h % 2][:, s, cols], start=False, stop=True)
                        last.then_inc(s_done[s], 1)
                if live[2]:
                    _, _, _, j2 = of_lag(b, jl, 2)
                    pe.wait_ge(diff_done, j2 + 1)
                    if not (first and jl == 2):
                        pe.wait_ge(lo_done, j2)
                        pe.wait_ge(lo2_done, j2)
                    for t in range(TILES):
                        last = nc.tensor.matmul(
                            ps_t[:, t, :], diff[jl % 2][:, t * P : t * P + P], ident[:], is_transpose=True,
                            start=t <= TILES // 2, stop=t < TILES // 2 or t == TILES - 1)
                    last.then_inc(t_done, 1)
                if out:
                    pe_piece(pe, TILES * (b - 1) + k, piece, k)
                if live[3]:
                    bb, h, t, j = of_lag(b, jl, 3)
                    if t == 0:
                        pe.wait_ge(v_in[h % 2], DMA * (2 * bb + h // 2 + 1))
                    pe.wait_ge(lo_done, j + 1)
                    pe.wait_ge(lo2_done, j + 1)
                    if not (first and jl == 3):
                        pe.wait_ge(raw_done, j)
                    if out and piece == 1:
                        pe_positions(pe, TILES * (b - 1) + k - 1)
                    i = (jl - 3) % 2
                    for t in range(TILES):
                        nc.tensor.matmul(ps_o[:, 0 : 2 * VD], diff_hi[i][:, t, :], v_buf[h % 2][:, t, :], start=t == 0, stop=False)
                        last = nc.tensor.matmul(ps_o[:, 0 : 2 * VD], diff_lo[i][:, t, :], v_buf[h % 2][:, t, :], start=False, stop=t == TILES - 1)
                    last.then_inc(o_done, 1)
                elif out and piece == 1:
                    pe.wait_ge(raw_done, STEPS * BATCH)
                    pe_positions(pe, TILES * (b - 1) + k - 1)
                if live[2]:
                    pe.wait_ge(hi_done, j2 + 1)
                    nc.tensor.matmul(ps_t[:, TILES // 2 :, :], neg_ident[:], diff_hi[jl % 2][:, TILES // 2 :, :], start=False, stop=True, skip_group_check=True).then_inc(rest_done, 1)

        def pe_positions(pe, n):
            pe.wait_ge(mask_done, n + 2)
            nc.tensor.matmul(ps_o[:, POS], before[:], mask[:], start=True, stop=False)
            nc.tensor.matmul(ps_o[:, POS], ones[:], mask_seen[:], start=False, stop=True).then_inc(pos_done, 1)

        def pe_piece(pe, n, piece, k):
            if piece == 0:
                pe.wait_ge(normed_done, NORMED_CREDIT + n + 1)
                pe.wait_ge(score_done, n + 1)
                for h in range(HEADS):
                    last = nc.tensor.transpose(ps_m[:, h * P : h * P + P], normed[:, h, :], ident[:])
                last.then_inc(at_done, 1)
            if piece == 1:
                pe.wait_ge(weight_step, 3)
                pe.wait_ge(at_lo_done, n + 1)
                for e in range(KD):
                    last = split_product(nc, ps_m[:], (heads_t[0][:, e, :], heads_t[1][:, e, :]), (wo[0][:, e, :], wo[1][:, e, :]), e == 0, e == KD - 1)
                last.then_inc(y_done, 1)
            if piece == 2:
                pe.wait_ge(x1_done, n + 2)
                for c in range(KD):
                    last = nc.tensor.transpose(ps_m[:, c * P : c * P + P], x1_buf[k % 2][:, c * P : c * P + P], ident[:])
                last.then_inc(xt_done, 1)
            if piece == 3:
                pe.wait_ge(xt_lo_done, n + 1)
                for c in range(KD):
                    last = split_product(nc, ps_m[:, 0:EXPERTS], (x1_t[0][:, c, :], x1_t[1][:, c, :]), (gate[0][:, c, :], gate[1][:, c, :]), c == 0, c == KD - 1)
                last.then_inc(gate_done, 1)

        def act_turns(act, b, attn, out, first):
            for jl, live, (k, piece) in turns(attn, out, first):
                n = TILES * (b - 1) + k if out else None
                if out and piece == 2:
                    act.wait_ge(ln_done, n + 1)
                    act.wait_ge(x1_stored[k % 2], 2 * DMA * (TILES // 2 * (b - 1) + k // 2 + 1))
                    nc.scalar.activation(x1_buf[k % 2][:], summed[:], ACT.Identity, bias=shift[:], scale=rstd[:]).then_inc(x1_done, 1)
                if attn:
                    exp(act, b, jl, 0, first)
                if live[2]:
                    _, _, _, j2 = of_lag(b, jl, 2)
                    act.wait_ge(t_done, j2 + 1)
                    if not (first and jl < 4):
                        act.wait_ge(o_done, j2 - 1)
                    nc.scalar.copy(diff_hi[jl % 2][:], ps_t[:]).then_inc(hi_done, 1)
                if out and piece == 2:
                    act.wait_ge(xt_done, n + 1)
                    act.wait_ge(gate_done, n + 1)
                    nc.scalar.copy(x1_t[0][:], ps_m[:].rearrange("p (h t) -> p h t", t=P)).then_inc(xt_hi_done, 1)
                if attn:
                    exp(act, b, jl, 1, first)
                if out and piece == 0:
                    act.wait_ge(at_done, n + 2)
                    act.wait_ge(y_done, n + 1)
                    nc.scalar.copy(heads_t[0][:], ps_m[:].rearrange("p (h t) -> p h t", t=P)).then_inc(at_hi_done, 1)
                if live[3]:
                    _, _, _, j = of_lag(b, jl, 3)
                    act.wait_ge(o_done, j + 1)
                    if not (first and jl == 3):
                        act.wait_ge(raw_done, j)
                    nc.scalar.copy(cross_sum[:], ps_o[:, VD : 2 * VD]).then_inc(cross_done, 1)
                if live[2]:
                    act.wait_ge(rest_done, j2 + 1)
                    nc.scalar.copy(diff_lo[jl % 2][:, TILES // 2 :, :], ps_t[:, TILES // 2 :, :]).then_inc(lo2_done, 1)
                if live[4]:
                    bb, h, t, j = of_lag(b, jl, 4)
                    act.wait_ge(raw_done, j + 1)
                    if not (first and jl == 4):
                        act.wait_ge(square_done, j)
                    par = bb % 2
                    nc.scalar.activation(square_junk[:], raw[:, par, t, h, :], ACT.Square, scale=VD**-0.5, accum_out=squares[:, par, t, h : h + 1]).then_inc(square_done, 1)
                if out and piece == 3:
                    act.wait_ge(lmax_done, n + 1)
                    act.wait_ge(route_step, ROUTE_STEPS * (n + 1))
                    nc.scalar.activation(score_exp[:], ps_m[:, 0:EXPERTS], ACT.Exp, bias=logit_max[:], accum_out=score_sum[:]).then_inc(score_done, 1)

        def exp(act, b, jl, s, first):
            j = STEPS * b + jl
            act.wait_ge(max_done[s], j + 1)
            if not (first and jl < 2):
                act.wait_ge(diff_done, j - 1)
            i = jl % 2
            if s == 0:
                act.wait_ge(normed_done, TILES * b + jl % TILES + 1)
                total = mass0[:, b % 2, jl % TILES, jl // TILES : jl // TILES + 1]
            else:
                total = mass1[:, i : i + 1]
            nc.scalar.activation(prob[s][i][:], ps_s[s][:], ACT.Exp, bias=neg_max[:, s, i : i + 1], accum_out=total).then_inc(exp_done[s], 1)

        def dve_turns(dve, b, attn, out, first):
            for jl, live, (k, piece) in turns(attn, out, first):
                n = TILES * (b - 1) + k if out else None
                j = STEPS * b + jl
                if attn:
                    row_max(dve, j, 0, jl % 2)
                if live[4]:
                    bb, h, t, j4 = of_lag(b, jl, 4)
                    dve.wait_ge(cross_done, j4 + 1)
                    if out and piece == 2:
                        read_positions(dve, n - 1)
                    par = bb % 2
                    nc.vector.tensor_tensor(raw[:, par, t, h, :], ps_o[:, 0:VD], cross_sum[:], ALU.add).then_inc(raw_done, 1)
                elif out and piece == 2:
                    read_positions(dve, n - 1)
                if out:
                    dve_route(dve, n - 1, piece, 0)
                if live[1]:
                    bb, h, t, j1 = of_lag(b, jl, 1)
                    i = (jl - 1) % 2
                    dve.wait_ge(exp_done[1], j1 + 1)
                    nc.vector.reciprocal(mass1_inv[:, i : i + 1], mass1[:, i : i + 1]).then_inc(inv_done, 1)
                if out:
                    dve_route(dve, n - 1, piece, 1)
                if attn:
                    row_max(dve, j, 1, jl % 2)
                if live[1]:
                    dve.wait_ge(inv_done, j1 + 1)
                    nc.vector.scalar_tensor_tensor(weight2[:, i : i + 1], mass1_inv[:, i : i + 1], mass0[:, bb % 2, t, h : h + 1], neg_lam[:], ALU.mult, ALU.mult).then_inc(weight_done, 1)
                if out:
                    dve_route(dve, n - 1, piece, 2)
                if live[1]:
                    dve.wait_ge(weight_done, j1 + 1)
                    if not (first and jl < 3):
                        dve.wait_ge(t_done, j1 - 1)
                    nc.vector.scalar_tensor_tensor(diff[i][:], prob[1][i][:], weight2[:, i : i + 1], prob[0][i][:], ALU.mult, ALU.add).then_inc(diff_done, 1)
                if out:
                    dve_route(dve, n - 1, piece, 3)
                if live[2]:
                    _, _, _, j2 = of_lag(b, jl, 2)
                    dve.wait_ge(hi_done, j2 + 1)
                    nc.vector.tensor_tensor(diff_lo[jl % 2][:, 0 : TILES // 2, :], ps_t[:, 0 : TILES // 2, :], diff_hi[jl % 2][:, 0 : TILES // 2, :].bitcast(F32), ALU.subtract).then_inc(lo_done, 1)
                if out:
                    dve_route(dve, n - 1, piece, 4)
                if out and piece == 0:
                    dve.wait_ge(at_hi_done, n + 1)
                    nc.vector.tensor_tensor(heads_t[1][:], ps_m[:].rearrange("p (h t) -> p h t", t=P), heads_t[0][:].bitcast(F32), ALU.subtract).then_inc(at_lo_done, 1)
                if out:
                    dve_route(dve, n - 1, piece, 5)
                if out and piece == 1:
                    dve.wait_ge(y_done, n + 2)
                    dve.wait_ge(x_loaded[k % 2], DMA * (TILES // 2 * (b - 1) + k // 2 + 1))
                    dve.wait_ge(x1_done, n + 1)
                    nc.vector.tensor_tensor(summed[:], ps_m[:], x_in[k % 2][:], ALU.add).then_inc(sum_done, 1)
                    dve.wait_ge(sum_done, n + 3)
                    nc.vector.bn_stats(stats[:], summed[:]).then_inc(stats_done, 1)
                    dve.wait_ge(stats_done, n + 1)
                    dve.sem_inc(held, 1)
                    nc.vector.bn_aggr(mean_var[:], stats[:]).then_inc(mv_done, 1)
                if out and piece == 2:
                    dve.wait_ge(xt_hi_done, n + 1)
                    nc.vector.tensor_tensor(x1_t[1][:], ps_m[:].rearrange("p (h t) -> p h t", t=P), x1_t[0][:].bitcast(F32), ALU.subtract).then_inc(xt_lo_done, 1)
                if out and piece == 3:
                    if k == 0:
                        dve.wait_ge(slot_done, n + 1)
                        nc.vector.memset(valid[:], 1.0)
                        nc.vector.memset(room[:], float(CAP)).then_inc(setup_dve, 1)
                        dve.wait_ge(setup_dve, SETUP_DVE + b)
                    dve.wait_ge(gate_done, n + 2)
                    nc.vector.tensor_reduce(logit_max[:], ps_m[:, 0:EXPERTS], AX.X, ALU.max, negate=True).then_inc(lmax_done, 1)

        def read_positions(dve, n):
            dve.wait_ge(pos_done, n + 2)
            nc.vector.tensor_copy(pos[:], ps_o[:, POS]).then_inc(pos_read, 1)

        def row_max(dve, j, s, i):
            dve.wait_ge(s_done[s], j + 1)
            nc.vector.tensor_reduce(neg_max[:, s, i : i + 1], ps_s[s][:], AX.X, ALU.max, negate=True).then_inc(max_done[s], 1)

        def dve_route(dve, n, piece, place):
            done = ROUTE_STEPS * (n + 1)
            if piece == 0:
                if place == 0:
                    dve.wait_ge(score_done, n + 2)
                    nc.vector.reciprocal(score_inv[:], score_sum[:]).then_inc(route_step, 1)
                if place == 1:
                    dve.wait_ge(route_step, done + 1)
                    nc.vector.tensor_scalar(score[:], score_exp[:], score_inv[:], None, ALU.mult).then_inc(route_step, 1)
                if place == 2:
                    dve.wait_ge(route_step, done + 2)
                    dve.sem_inc(held, 1)
                    nc.vector.max(top_val[:], score[:]).then_inc(route_step, 1)
                if place == 3:
                    dve.wait_ge(route_step, done + 3)
                    dve.sem_inc(held, 1)
                    nc.vector.max_index(top_idx[:], top_val[:], score[:]).then_inc(route_step, 1)
                if place == 4:
                    dve.wait_ge(route_step, done + 4)
                    nc.vector.tensor_copy(chosen[:], top_idx[:, 0:TOPK]).then_inc(route_step, 1)
                if place == 5:
                    dve.wait_ge(route_step, done + 5)
                    nc.vector.tensor_tensor(
                        hit[:], iota[:].unsqueeze(1).to_broadcast([P, TOPK, EXPERTS]),
                        chosen[:].unsqueeze(2).to_broadcast([P, TOPK, EXPERTS]), ALU.is_equal).then_inc(route_step, 1)
            if piece == 1:
                if place == 0:
                    dve.wait_ge(route_step, done + 6)
                    nc.vector.tensor_reduce(mask_f[:], hit[:].rearrange("p k e -> p e k"), AX.X, ALU.add).then_inc(route_step, 1)
                if place == 1:
                    dve.wait_ge(route_step, done + 7)
                    nc.vector.tensor_scalar(mask[:], mask_f[:], valid[:], None, ALU.mult).then_inc(mask_done, 1)
                if place == 2:
                    dve.wait_ge(entry_free, n + 2)
                    nc.vector.tensor_copy(entry[:, :, 1], top_val[:, 0:TOPK])
                    nc.vector.tensor_copy(entry[:, :, 0], token[:].to_broadcast([P, TOPK])).then_inc(route_step, 1)
            done = SLOT_STEPS * (n + 1)
            if piece == 2 and place == 3:
                dve.wait_ge(hit_pos_done, n + 2)
                nc.vector.tensor_reduce(pos_k[:], hit_pos[:], AX.X, ALU.add).then_inc(slot_step, 1)
            if piece == 2 and place == 4:
                dve.wait_ge(slot_step, done + 1)
                nc.vector.tensor_scalar(over[:], pos_k[:], room[:], BIG, ALU.is_ge, ALU.mult)
                nc.vector.scalar_tensor_tensor(slot_f[:], chosen[:], float(CAP), pos_k[:], ALU.mult, ALU.add).then_inc(slot_step, 1)
            if piece == 3 and place == 0:
                dve.wait_ge(slot_step, done + 2)
                nc.vector.tensor_tensor(slot[:], slot_f[:], over[:], ALU.add).then_inc(slot_step, 1)
                dve.wait_ge(mask_done, n + 2)
                dve.wait_ge(pos_done, n + 2)
                nc.vector.tensor_tensor(mask_seen[:], mask_seen[:], mask[:], ALU.add).then_inc(slot_step, 1)
            if piece == 3 and place == 1:
                dve.wait_ge(slot_step, done + 4)
                nc.vector.tensor_scalar_add(token[:], token[:], float(P)).then_inc(slot_done, 1)

        def pool_norm_heads(pool, b, k):
            n = TILES * b + k
            j = STEPS * b + TILES * (HEADS - 1) + k
            par = b % 2
            pool.wait_ge(exp_done[0], j + 1)
            nc.gpsimd.tensor_tensor(mass_squared[:], mass0[:, par, k, :], mass0[:, par, k, :], ALU.mult).then_inc(rms_step, 1)
            pool.wait_ge(rms_step, RMS_STEPS * n + 1)
            nc.gpsimd.tensor_tensor(eps_mass[:], mass_squared[:], eps_col[:], ALU.mult).then_inc(rms_step, 1)
            pool.wait_ge(rms_step, RMS_STEPS * n + 2)
            pool.wait_ge(square_done, j + 1)
            nc.gpsimd.tensor_tensor(rms_sum[:], squares[:, par, k, :], eps_mass[:], ALU.add).then_inc(rms_step, 1)
            pool.wait_ge(rms_step, RMS_STEPS * n + 3)
            nc.gpsimd.tensor_tensor(rms[:], rms_sum[:], pow_col[:], ALU.pow).then_inc(rms_step, 1)
            pool.wait_ge(rms_step, RMS_STEPS * n + 4)
            pool.wait_ge(at_done, n + 1)
            nc.gpsimd.tensor_tensor(normed[:], raw[:, par, k, :, :], rms[:].unsqueeze(2).to_broadcast([P, HEADS, VD]), ALU.mult).then_inc(normed_done, 1)

        def pool_tiles(pool, b, final):
            for k in range(TILES):
                n = TILES * (b - 1) + k
                pool.wait_ge(mv_done, n + 1)
                pool.wait_ge(x1_done, n + 1)
                nc.gpsimd.tensor_tensor(var_eps[:], mean_var[:, 1:2], eps_col[:, 0:1], ALU.add).then_inc(ln_step, 1)
                nc.gpsimd.tensor_tensor(neg_mean[:], zeros[:, 0:1], mean_var[:, 0:1], ALU.subtract).then_inc(ln_step, 1)
                pool.wait_ge(ln_step, LN_STEPS * n + 2)
                nc.gpsimd.tensor_tensor(rstd[:], var_eps[:], pow_col[:, 0:1], ALU.pow).then_inc(ln_step, 1)
                pool.wait_ge(ln_step, LN_STEPS * n + 3)
                nc.gpsimd.tensor_tensor(shift[:], neg_mean[:], rstd[:], ALU.mult).then_inc(ln_done, 1)
                pool_hit_pos(pool, n - 1)
                if k < TILES - 1:
                    pool_norm_heads(pool, b - 1, k + 1)
                elif not final:
                    pool_norm_heads(pool, b, 0)
                pool_scatter(pool, n - 1)

        def pool_hit_pos(pool, n):
            pool.wait_ge(pos_read, n + 2)
            pool.wait_ge(mask_done, n + 2)
            nc.gpsimd.tensor_tensor(hit_pos[:], hit[:], pos[:].unsqueeze(1).to_broadcast([P, TOPK, EXPERTS]), ALU.mult).then_inc(hit_pos_done, 1)

        def pool_scatter(pool, n):
            pool.wait_ge(slot_done, n + 2)
            pool.sem_inc(held, 1)
            for c in range(TOPK):
                nc.gpsimd.indirect_dma_start(
                    slots, bass.IndirectOffsetOnAxis(ap=slot[:, c : c + 1], axis=0), entry[:, c, :], None,
                    bounds_check=EXPERTS * CAP - 1, oob_is_err=False,
                ).then_inc(scattered, DMA)
            pool.wait_ge(scattered, DMA * TOPK * (n + 2))
            pool.sem_inc(entry_free, 1)

        with nc.Block() as block:

            @block.sync
            def _(sp):
                sp.dma_start(ident[:], ident_in).then_inc(consts_in, DMA)
                sp.dma_start(before_f[:], before_in).then_inc(consts_in, DMA)
                load_qk(sp, 0, 0, 0)
                sp.dma_start(lam_in[:], lambdas.partition_broadcast(P)).then_inc(lam_loaded, DMA)
                load_v(sp, 0, 0, 0)
                sp.dma_start(wo_raw[:], w_out.rearrange("(k p) n -> p k n", p=P)).then_inc(weights_in, DMA)
                sp.dma_start(gate_raw[:], gate_t.rearrange("(k p) n -> p k n", p=P)).then_inc(weights_in, DMA)
                sp.dma_start(subln_col[:], subln).then_inc(weights_in, DMA)
                sp.dma_start(slots, empty_slots).then_inc(pads_out, DMA)
                sp.wait_ge(setup_pool, SETUP_POOL)
                sp.dma_start(x1[TOKENS : TOKENS + CAP, :], zeros[:]).then_inc(pads_out, DMA)
                sp.dma_start(total[TOKENS : TOKENS + CAP, :], zeros[:]).then_inc(pads_out, DMA)
                sp_turns(sp, 0, True, False, True)
                with sp.Fori(1, BATCH) as b:
                    sp_turns(sp, b, True, True, False)
                sp_turns(sp, BATCH, False, True, False)
                sp.wait_ge(qk_in[0], DMA * LOADS_QK * (BATCH * HEADS // 2 + 1))
                sp.wait_ge(v_in[0], DMA * (BATCH * HEADS // 2 + 1))
                sp.wait_ge(pads_out, 3 * DMA)
                for i in range(2):
                    sp.wait_ge(x1_stored[i], 2 * DMA * (TOKENS // P // 2 + 1))
                sp.wait_ge(scattered, DMA * TOPK * (TOKENS // P + 1))

            @block.tensor
            def _(pe):
                pe.sem_inc(at_done, 1)
                pe.sem_inc(y_done, 1)
                pe.sem_inc(gate_done, 1)
                pe.wait_ge(consts_in, 2 * DMA)
                pe.wait_ge(neg_ident_done, 1)
                pe_turns(pe, 0, True, False, True)
                pe.wait_ge(before_done, 1)
                pe.wait_ge(setup_dve, SETUP_DVE)
                with pe.Fori(1, BATCH) as b:
                    pe_turns(pe, b, True, True, False)
                pe_turns(pe, BATCH, False, True, False)
                pe_positions(pe, TOKENS // P - 1)

            @block.scalar
            def _(act):
                act.sem_inc(x1_done, 1)
                act.sem_inc(score_done, 1)
                act.sem_inc(x1_stored[0], 2 * DMA)
                act.sem_inc(x1_stored[1], 2 * DMA)
                act.wait_ge(setup_dve, 2)
                nc.scalar.activation(lam_exp[:], lam_sum[:], ACT.Exp).then_inc(setup_act, 1)
                act_turns(act, 0, True, False, True)
                act.wait_ge(weight_step, 1)
                nc.scalar.copy(wo[0][:], wo_raw[:]).then_inc(setup_act, 1)
                nc.scalar.copy(gate[0][:], gate_raw[:]).then_inc(setup_act, 1)
                with act.Fori(1, BATCH) as b:
                    act_turns(act, b, True, True, False)
                act_turns(act, BATCH, False, True, False)

            @block.vector
            def _(dve):
                dve.sem_inc(sum_done, 2)
                dve.wait_ge(consts_in, 2 * DMA)
                nc.vector.tensor_scalar(neg_ident[:], ident[:], -1.0, None, ALU.mult).then_inc(neg_ident_done, 1)
                nc.vector.tensor_copy(before[:], before_f[:]).then_inc(before_done, 1)
                dve.wait_ge(lam_loaded, DMA)
                nc.vector.tensor_tensor(lam_prod[:], lam_in[:, 0:2, :], lam_in[:, 2:4, :], ALU.mult).then_inc(setup_dve, 1)
                dve.wait_ge(setup_dve, 1)
                nc.vector.tensor_reduce(lam_sum[:], lam_prod[:], AX.X, ALU.add).then_inc(setup_dve, 1)
                dve.wait_ge(setup_act, 1)
                nc.vector.tensor_tensor(lam_diff[:], lam_exp[:, 1:2], lam_exp[:, 0:1], ALU.subtract).then_inc(setup_dve, 1)
                dve.wait_ge(setup_dve, 3)
                nc.vector.tensor_scalar_add(neg_lam[:], lam_diff[:], -LAMBDA_INIT).then_inc(setup_dve, 1)
                nc.vector.memset(ones[:], 1.0).then_inc(setup_dve, 1)
                nc.vector.memset(mask_seen[:], 0.0).then_inc(setup_dve, 1)
                nc.vector.memset(valid[:], 0.0).then_inc(setup_dve, 1)
                nc.vector.memset(room[:], 0.0).then_inc(setup_dve, 1)
                dve.wait_ge(setup_pool, SETUP_POOL)
                nc.vector.tensor_copy(iota[:], iota_i[:]).then_inc(setup_dve, 1)
                nc.vector.tensor_copy(token[:], token_i[:]).then_inc(setup_dve, 1)
                dve.wait_ge(setup_dve, SETUP_DVE)
                dve_turns(dve, 0, True, False, True)
                with dve.Fori(1, BATCH) as b:
                    dve_turns(dve, b, True, True, False)
                dve_turns(dve, BATCH, False, True, False)
                n = TOKENS // P - 1
                for piece in range(4):
                    if piece == 2:
                        read_positions(dve, n)
                    for place in range(6):
                        dve_route(dve, n, piece, place)

            @block.gpsimd
            def _(pool):
                pool.sem_inc(normed_done, NORMED_CREDIT)
                pool.sem_inc(entry_free, 1)
                nc.gpsimd.memset(zeros[:], 0.0).then_inc(setup_pool, 1)
                nc.gpsimd.memset(pow_col[:], -0.5).then_inc(setup_pool, 1)
                nc.gpsimd.memset(eps_col[:], EPS).then_inc(setup_pool, 1)
                nc.gpsimd.memset(score_exp[:], 1.0).then_inc(setup_pool, 1)
                nc.gpsimd.memset(score_sum[:], 1.0).then_inc(setup_pool, 1)
                nc.gpsimd.iota(iota_i[:], [[1, EXPERTS]], base=0, channel_multiplier=0).then_inc(setup_pool, 1)
                nc.gpsimd.iota(token_i[:], [[0, 1]], base=-P, channel_multiplier=1).then_inc(setup_pool, 1)
                nc.gpsimd.memset(square_junk[:], 0.0).then_inc(setup_pool, 1)
                pool.wait_ge(setup_pool, SETUP_POOL)
                pool.wait_ge(pads_out, 3 * DMA)
                pool.wait_ge(weights_in, 3 * DMA)
                nc.gpsimd.tensor_tensor(wo_raw[:], wo_raw[:], subln_col[:].unsqueeze(2).to_broadcast([P, KD, DIM]), ALU.mult).then_inc(weight_step, 1)
                pool_norm_heads(pool, 0, 0)
                pool.wait_ge(setup_act, 3)
                nc.gpsimd.tensor_tensor(wo[1][:], wo_raw[:], wo[0][:].bitcast(F32), ALU.subtract).then_inc(weight_step, 1)
                nc.gpsimd.tensor_tensor(gate[1][:], gate_raw[:], gate[0][:].bitcast(F32), ALU.subtract).then_inc(weight_step, 1)
                with pool.Fori(1, BATCH) as b:
                    pool_tiles(pool, b, False)
                pool_tiles(pool, BATCH, True)
                pool_hit_pos(pool, TOKENS // P - 1)
                pool_scatter(pool, TOKENS // P - 1)


def experts(nc, x1, slots, w13_t, w2_t, sw13_t, sw2_t, ident_in, total):
    FULL = SHARED // P
    REST = SHARED - FULL * P
    UNITS = FULL + 1
    GROUPS = TOKENS // CHUNK
    PER = EXPERTS // GROUPS
    TT = CHUNK // P
    HT = -(-INTER // P)
    LAST = INTER - (HT - 1) * P
    assert REST == HALF
    with Stage(nc, "exp") as st:
        sw13 = [st.sbuf(f"sw13_{part}", [P, KD, 2 * SHARED], F32R) for part in ("hi", "lo")]
        sw2 = [st.sbuf(f"sw2_{part}", [P, UNITS, DIM], F32R) for part in ("hi", "lo")]
        w13_raw = st.sbuf("w13_raw", [P, KD, 2 * INTER])
        w13 = [st.sbuf(f"w13_{part}", [P, KD, 2 * INTER], F32R) for part in ("hi", "lo")]
        w2_raw = st.sbuf("w2_raw", [P, HT, DIM])
        w2 = [st.sbuf(f"w2_{part}", [P, HT, DIM], F32R) for part in ("hi", "lo")]
        ident = st.sbuf("ident", [P, P])
        x_in = st.sbuf("x_in", [P, TT, DIM])
        x_t = [st.sbuf(f"x_t_{part}", [P, KD, CHUNK], F32R) for part in ("hi", "lo")]
        silu = [st.sbuf(f"silu{i}", [P, CHUNK]) for i in range(2)]
        hid = [st.sbuf(f"hid{i}", [P, CHUNK]) for i in range(2)]
        hid_hi = st.sbuf("hid_hi", [P, UNITS, CHUNK], F32R)
        hid_lo = st.sbuf("hid_lo", [P, FULL, CHUNK], F32R)
        z_buf = [st.sbuf(f"z{i}", [P, DIM]) for i in range(TT)]
        table = st.sbuf("table", [EXPERTS, CAP, 2])
        row_of = st.sbuf("row_of", [P, EXPERTS], I32)
        gate_of = st.sbuf("gate_of", [P, EXPERTS])
        rows = [st.sbuf(f"rows{r}", [P, 1], I32) for r in range(PER)]
        gates = [st.sbuf(f"gates{i}", [P, 1]) for i in range(2)]
        xe = [st.sbuf(f"xe{i}", [P, DIM]) for i in range(2)]
        xe_t = [st.sbuf(f"xe_t_{part}", [P, KD, P], F32R) for part in ("hi", "lo")]
        e_silu = st.sbuf("e_silu", [P, INTER])
        e_hid = st.sbuf("e_hid", [P, INTER])
        e_hid_t = [st.sbuf(f"e_hid_t_{part}", [P, HT, P], F32R) for part in ("hi", "lo")]
        ye = [st.sbuf(f"ye{i}", [P, DIM]) for i in range(2)]

        ps_ab = [st.psum(f"ps_ab{i}", [P, 2, CHUNK]) for i in range(2)]
        ps_a, ps_b, ps_et, ps_y = (st.psum(n, [P, 512]) for n in ("ps_a", "ps_b", "ps_et", "ps_y"))

        const_in, table_in, shared_in = st.sem("const_in"), st.sem("table_in"), st.sem("shared_in")
        held = st.sem("held")
        split_hi, split_lo = st.sem("split_hi"), st.sem("split_lo")
        table_t, table_done = st.sem("table_t"), st.sem("table_done")
        w13_in, w2_in = st.sem("w13_in"), st.sem("w2_in")
        gathered = [st.sem(f"gathered{i}") for i in range(2)]
        row_picked, gate_picked = st.sem("row_picked"), st.sem("gate_picked")
        added, ye_free = st.sem("added"), st.sem("ye_free")
        xet_done, xet_hi_done, xet_copied = st.sem("xet_done"), st.sem("xet_hi_done"), st.sem("xet_copied")
        w13_hi_done, w13_lo_done, w2_hi_done, w2_lo_done = (st.sem(n) for n in ("w13_hi_done", "w13_lo_done", "w2_hi_done", "w2_lo_done"))
        eht_hi_done = st.sem("eht_hi_done")
        ab_done, esilu_done, ehid_done = st.sem("ab_done"), st.sem("esilu_done"), st.sem("ehid_done")
        eht_done, eht_copied, ey_done, ye_done = (st.sem(n) for n in ("eht_done", "eht_copied", "ey_done", "ye_done"))
        x_loaded = st.sem("x_loaded")
        xt_done, xt_hi_done, xt_lo_done = st.sem("xt_done"), st.sem("xt_hi_done"), st.sem("xt_lo_done")
        up_done, silu_done, hid_done = st.sem("up_done"), st.sem("silu_done"), st.sem("hid_done")
        hid_hi_done, hid_lo_done = st.sem("hid_hi_done"), st.sem("hid_lo_done")
        z_done, z_read = st.sem("z_done"), st.sem("z_read")
        z_added, z_free = st.sem("z_added"), st.sem("z_free")

        PLAN = [["x", 0, 1], [2, 3, 4], [5, "z0", "z1"], ["z2", "z3:", "z3"]]

        def load_w13(sp, e):
            sp.dma_start(w13_raw[:], w13_t[e].rearrange("(k p) n -> p k n", p=P)).then_inc(w13_in, DMA)

        def load_w2(sp, e):
            sp.dma_start(w2_raw[:, 0 : HT - 1, :], w2_t[e, 0 : (HT - 1) * P, :].rearrange("(k p) n -> p k n", p=P)).then_inc(w2_in, DMA)
            sp.dma_start(w2_raw[0:LAST, HT - 1, :], w2_t[e, (HT - 1) * P : INTER, :]).then_inc(w2_in, DMA)

        def w13_high(act, e):
            act.wait_ge(w13_in, DMA * (e + 1))
            nc.scalar.copy(w13[0][:], w13_raw[:]).then_inc(w13_hi_done, 1)

        def w2_high(act, e):
            act.wait_ge(w2_in, 2 * DMA * (e + 1))
            nc.scalar.copy(w2[0][:, 0 : HT - 1, :], w2_raw[:, 0 : HT - 1, :])
            nc.scalar.copy(w2[0][0:LAST, HT - 1, :], w2_raw[0:LAST, HT - 1, :]).then_inc(w2_hi_done, 1)

        def w13_low(eng, engine, e):
            eng.wait_ge(w13_hi_done, e + 1)
            engine.tensor_tensor(w13[1][:], w13_raw[:], w13[0][:].bitcast(F32), ALU.subtract).then_inc(w13_lo_done, 1)

        def w2_low(dve, e):
            dve.wait_ge(w2_hi_done, e + 1)
            full, rest = (slice(0, P), slice(0, HT - 1)), (slice(0, LAST), HT - 1)
            nc.vector.tensor_tensor(w2[1][full], w2_raw[full], w2[0][full].bitcast(F32), ALU.subtract)
            nc.vector.tensor_tensor(w2[1][rest], w2_raw[rest], w2[0][rest].bitcast(F32), ALU.subtract).then_inc(w2_lo_done, 1)

        def sp_group(sp, g, final):
            for r in range(PER):
                e = PER * g + r
                for u in PLAN[r]:
                    if u == "x" and not final:
                        sp.wait_ge(xt_done, KD * (g + 1))
                        sp.dma_start(x_in[:], x1[bass.ds((g + 1) * CHUNK, CHUNK), :].rearrange("(t p) d -> p t d", p=P)).then_inc(x_loaded, DMA)
                if not (final and r == PER - 1):
                    sp.wait_ge(w2_lo_done, e + 1)
                    load_w2(sp, e + 1)
                if not (final and r >= PER - 2):
                    sp.wait_ge(w13_lo_done, e + 2)
                    load_w13(sp, e + 2)

        def pe_group(pe, g):
            for r in range(PER):
                e, i = PER * g + r, r % 2
                pe.wait_ge(gathered[i], DMA * (PER // 2 * g + r // 2 + 1))
                pe.wait_ge(eht_copied, e + 1)
                for c in range(KD):
                    last = nc.tensor.transpose(ps_et[:, c * P : c * P + P], xe[i][:, c * P : c * P + P], ident[:])
                last.then_inc(xet_done, 1)
                pe_unit(pe, g, PLAN[r][0])
                pe.wait_ge(w13_lo_done, e + 1)
                pe.wait_ge(xet_copied, e + 1)
                pe.wait_ge(ehid_done, e + 1)
                for c in range(KD):
                    for out, cols in ((ps_a, slice(0, INTER)), (ps_b, slice(INTER, 2 * INTER))):
                        last = split_product(
                            nc, out[:, 0:INTER], (xe_t[0][:, c, :], xe_t[1][:, c, :]),
                            (w13[0][:, c, cols], w13[1][:, c, cols]), c == 0, c == KD - 1)
                last.then_inc(ab_done, 1)
                pe_unit(pe, g, PLAN[r][1])
                pe.wait_ge(ehid_done, e + 2)
                for c in range(HT):
                    w = LAST if c == HT - 1 else P
                    last = nc.tensor.transpose(ps_et[0:w, c * P : c * P + P], e_hid[:, c * P : c * P + w], ident[:])
                last.then_inc(eht_done, 1)
                pe_unit(pe, g, PLAN[r][2])
                pe.wait_ge(eht_copied, e + 2)
                pe.wait_ge(w2_lo_done, e + 1)
                pe.wait_ge(ye_done, e + 1)
                for c in range(HT):
                    w = LAST if c == HT - 1 else P
                    last = split_product(
                        nc, ps_y[:], (e_hid_t[0][0:w, c, :], e_hid_t[1][0:w, c, :]),
                        (w2[0][0:w, c, :], w2[1][0:w, c, :]), c == 0, c == HT - 1)
                last.then_inc(ey_done, 1)

        def pe_unit(pe, g, u):
            if u == "x":
                pe.wait_ge(x_loaded, DMA * (g + 1))
                pe.wait_ge(z_read, TT * (g + 1))
                for c in range(KD):
                    for t in range(TT):
                        last = nc.tensor.transpose(ps_ab[c // 2][:, c % 2, t * P : t * P + P], x_in[:, t, c * P : c * P + P], ident[:])
                    last.then_inc(xt_done, 1)
            elif isinstance(u, int):
                if u < 2:
                    pe.wait_ge(split_lo, 4)
                    pe.wait_ge(xt_lo_done, KD * (g + 1))
                else:
                    pe.wait_ge(hid_done, UNITS * g + u + 1)
                tiles = [u, FULL + u] if u < FULL else [2 * FULL]
                for ab, tile in enumerate(tiles):
                    for c in range(KD):
                        cols = slice(tile * P, tile * P + P)
                        last = split_product(nc, ps_ab[u % 2][:, ab, :], (sw13[0][:, c, cols], sw13[1][:, c, cols]), (x_t[0][:, c, :], x_t[1][:, c, :]), c == 0, c == KD - 1)
                last.then_inc(up_done, 1)
            else:
                t = int(u[1])
                pe.wait_ge(hid_lo_done, UNITS * (g + 1))
                out = ps_ab[t // 2][:, t % 2, :]
                toks = slice(t * P, t * P + P)
                half = FULL // 2
                for c in range(half) if u[-1] == ":" else range(half, FULL) if u == "z3" else range(FULL):
                    split_product(nc, out, (hid_hi[:, c, toks], hid_lo[:, c, toks]), (sw2[0][:, c, :], sw2[1][:, c, :]), c == 0, False)
                if u[-1] == ":":
                    return
                nc.tensor.matmul(out, hid_hi[:, FULL, toks], sw2[0][:, FULL, :], start=False, stop=False)
                nc.tensor.matmul(out, hid_hi[:, FULL, toks], sw2[1][:, FULL, :], start=False, stop=True).then_inc(z_done, 1)

        def act_group(act, g, final):
            for r in range(PER):
                e, i = PER * g + r, r % 2
                act.wait_ge(xet_done, e + 2)
                act.wait_ge(ab_done, e + 1)
                nc.scalar.copy(xe_t[0][:], ps_et[:].rearrange("p (c t) -> p c t", t=P)).then_inc(xet_hi_done, 1)
                act_unit(act, g, PLAN[r][0])
                w2_high(act, e)
                act.wait_ge(ab_done, e + 2)
                nc.scalar.activation(e_silu[:], ps_a[:, 0:INTER], ACT.Silu).then_inc(esilu_done, 1)
                if not (final and r == PER - 1):
                    w13_high(act, e + 1)
                act_unit(act, g, PLAN[r][1])
                act.wait_ge(eht_done, e + 2)
                act.wait_ge(ey_done, e + 1)
                nc.scalar.copy(e_hid_t[0][:, 0 : HT - 1, :], ps_et[:, 0 : (HT - 1) * P].rearrange("p (c t) -> p c t", t=P))
                nc.scalar.copy(e_hid_t[0][0:LAST, HT - 1, :], ps_et[0:LAST, (HT - 1) * P : HT * P]).then_inc(eht_hi_done, 1)
                act_unit(act, g, PLAN[r][2])
                act.wait_ge(ey_done, e + 2)
                act.wait_ge(gate_picked, e + 1)
                act.wait_ge(ye_free, e + 1)
                nc.scalar.activation(ye[i][:], ps_y[:], ACT.Copy, scale=gates[i][:]).then_inc(ye_done, 1)

        def act_unit(act, g, u):
            if u == "x":
                act.wait_ge(up_done, UNITS * (g + 1))
                for c in range(KD):
                    act.wait_ge(xt_done, KD * g + c + 1)
                    nc.scalar.copy(x_t[0][:, c, :], ps_ab[c // 2][:, c % 2, :]).then_inc(xt_hi_done, 1)
            elif isinstance(u, int):
                n = UNITS * g + u
                w = P if u < FULL else REST
                act.wait_ge(up_done, n + 1 + UNITS)
                act.wait_ge(hid_done, n + 1)
                nc.scalar.activation(silu[u % 2][0:w, :], ps_ab[u % 2][0:w, 0, :], ACT.Silu).then_inc(silu_done, 1)
                act.wait_ge(hid_done, n + 3)
                if u == 0:
                    act.wait_ge(z_done, TT * (g + 1))
                nc.scalar.copy(hid_hi[0:w, u, :], hid[u % 2][0:w, :]).then_inc(hid_hi_done, 1)

        def dve_group(dve, g, final):
            for r in range(PER):
                e, i = PER * g + r, r % 2
                dve.wait_ge(xet_hi_done, e + 1)
                nc.vector.tensor_tensor(xe_t[1][:], ps_et[:].rearrange("p (c t) -> p c t", t=P), xe_t[0][:].bitcast(F32), ALU.subtract).then_inc(xet_copied, 1)
                dve_unit(dve, g, PLAN[r][0])
                w2_low(dve, e)
                dve.wait_ge(esilu_done, e + 1)
                dve.wait_ge(eht_done, e + 1)
                nc.vector.tensor_tensor(e_hid[:], ps_b[:, 0:INTER], e_silu[:], ALU.mult).then_inc(ehid_done, 1)
                dve_unit(dve, g, PLAN[r][1])
                dve.wait_ge(eht_hi_done, e + 1)
                nc.vector.tensor_tensor(e_hid_t[1][:, 0 : HT - 1, :], ps_et[:, 0 : (HT - 1) * P].rearrange("p (c t) -> p c t", t=P), e_hid_t[0][:, 0 : HT - 1, :].bitcast(F32), ALU.subtract)
                nc.vector.tensor_tensor(e_hid_t[1][0:LAST, HT - 1, :], ps_et[0:LAST, (HT - 1) * P : HT * P], e_hid_t[0][0:LAST, HT - 1, :].bitcast(F32), ALU.subtract).then_inc(eht_copied, 1)
                dve_unit(dve, g, PLAN[r][2])

        def dve_unit(dve, g, u):
            if u == "x":
                for c in range(KD):
                    dve.wait_ge(xt_hi_done, KD * g + c + 1)
                    nc.vector.tensor_tensor(x_t[1][:, c, :], ps_ab[c // 2][:, c % 2, :], x_t[0][:, c, :].bitcast(F32), ALU.subtract).then_inc(xt_lo_done, 1)
            elif isinstance(u, int):
                n = UNITS * g + u
                dve.wait_ge(silu_done, n + 1)
                if u < FULL:
                    nc.vector.tensor_tensor(hid[u % 2][:], ps_ab[u % 2][:, 1, :], silu[u % 2][:], ALU.mult).then_inc(hid_done, 1)
                    low, w = hid_lo[:, u, :], P
                else:
                    nc.vector.tensor_tensor(hid[u % 2][0:REST, :], ps_ab[u % 2][REST:P, 0, :], silu[u % 2][0:REST, :], ALU.mult).then_inc(hid_done, 1)
                    low, w = hid_hi[REST:P, u, :], REST
                dve.wait_ge(hid_hi_done, n + 1)
                nc.vector.tensor_tensor(low, hid[u % 2][0:w, :], hid_hi[0:w, u, :].bitcast(F32), ALU.subtract).then_inc(hid_lo_done, 1)
            elif u[-1] != ":":
                t = int(u[1])
                dve.wait_ge(z_done, TT * g + t + 1 + TT)
                dve.wait_ge(z_free, TT * g + t + 1)
                nc.vector.tensor_copy(z_buf[t][:], ps_ab[t // 2][:, t % 2, :]).then_inc(z_read, 1)

        def pick(pool, e, r):
            i = r % 2
            nc.gpsimd.tensor_copy(rows[r][:], row_of[:, bass.ds(e, 1)]).then_inc(row_picked, 1)
            nc.gpsimd.tensor_copy(gates[i][:], gate_of[:, bass.ds(e, 1)]).then_inc(gate_picked, 1)
            pool.wait_ge(row_picked, e + 1)
            pool.wait_ge(xet_done, e)
            pool.sem_inc(held, 1)
            nc.gpsimd.indirect_dma_start(
                xe[i][:], None, x1, bass.IndirectOffsetOnAxis(ap=rows[r][:, 0:1], axis=0),
                bounds_check=TOKENS + CAP - 1, oob_is_err=False,
            ).then_inc(gathered[i], DMA)

        def z_tiles(r):
            return [int(u[1]) for u in PLAN[r] if isinstance(u, str) and u[0] == "z" and u[-1] != ":"]

        def pool_after(pool, g, r):
            pool.wait_ge(added, DMA * (PER * g + r + 1))
            pool.sem_inc(ye_free, 1)
            for t in z_tiles(r):
                pool.wait_ge(z_read, TT * g + t + 1 + TT)
                pool.sem_inc(held, 1)
                nc.gpsimd.dma_start(total[bass.ds(g * CHUNK + t * P, P), :], z_buf[t][:], accum_op=ALU.add).then_inc(z_added, DMA)

        def pool_z_free(pool, g, r):
            if z_tiles(r):
                pool.wait_ge(z_added, DMA * (TT * g + z_tiles(r)[-1] + 1))
                pool.sem_inc(z_free, len(z_tiles(r)))

        def pool_group(pool, g, first, final):
            for r in range(PER):
                e, i = PER * g + r, r % 2
                before = (g, r - 1) if r else (g - 1, PER - 1)
                if not (final and r == PER - 1):
                    pick(pool, e + 1, (r + 1) % PER)
                if not (first and r == 0):
                    pool_after(pool, *before)
                if not (final and r == PER - 1):
                    w13_low(pool, nc.gpsimd, e + 1)
                if not (first and r == 0):
                    pool_z_free(pool, *before)
                pool.wait_ge(ye_done, e + 2)
                pool.sem_inc(held, 1)
                nc.gpsimd.indirect_dma_start(
                    total, bass.IndirectOffsetOnAxis(ap=rows[r][:, 0:1], axis=0), ye[i][:], None,
                    bounds_check=TOKENS + CAP - 1, compute_op=ALU.add,
                ).then_inc(added, DMA)
            if final:
                pool_after(pool, g, PER - 1)

        with nc.Block() as block:

            @block.sync
            def _(sp):
                sp.dma_start(ident[:], ident_in).then_inc(const_in, DMA)
                sp.dma_start(table[:], slots.rearrange("(e c) w -> e c w", c=CAP)).then_inc(table_in, DMA)
                for i in range(2):
                    if i:
                        sp.wait_ge(split_lo, 1)
                    sp.dma_start(w13_raw[:], sw13_t[:, i * SHARED : (i + 1) * SHARED].rearrange("(k p) n -> p k n", p=P)).then_inc(shared_in, DMA)
                    if i == 0:
                        sp.dma_start(x_in[:], x1[0:CHUNK, :].rearrange("(t p) d -> p t d", p=P)).then_inc(x_loaded, DMA)
                        sp.dma_start(w2_raw[:], sw2_t[0 : 3 * P, :].rearrange("(k p) n -> p k n", p=P)).then_inc(shared_in, DMA)
                    else:
                        sp.wait_ge(split_lo, 2)
                        sp.dma_start(w2_raw[:, 0:2, :], sw2_t[3 * P : 5 * P, :].rearrange("(k p) n -> p k n", p=P)).then_inc(shared_in, DMA)
                        for top in (0, REST):
                            sp.dma_start(w2_raw[top : top + REST, 2, :], sw2_t[FULL * P : SHARED, :]).then_inc(shared_in, DMA)
                sp.wait_ge(split_lo, 3)
                load_w13(sp, 0)
                sp.wait_ge(split_lo, 4)
                load_w2(sp, 0)
                sp.wait_ge(w13_lo_done, 1)
                load_w13(sp, 1)
                with sp.Fori(0, GROUPS - 1) as g:
                    sp_group(sp, g, False)
                sp_group(sp, GROUPS - 1, True)
                sp.wait_ge(z_added, DMA * TT * GROUPS)
                sp.wait_ge(added, DMA * EXPERTS)

            @block.tensor
            def _(pe):
                pe.sem_inc(xet_done, 1)
                pe.sem_inc(ab_done, 1)
                pe.sem_inc(eht_done, 1)
                pe.sem_inc(ey_done, 1)
                pe.sem_inc(up_done, UNITS)
                pe.sem_inc(z_done, TT)
                pe.wait_ge(const_in, DMA)
                pe.wait_ge(table_in, DMA)
                for w in range(2):
                    nc.tensor.transpose(ps_y[:, w * EXPERTS : (w + 1) * EXPERTS], table[:, :, w], ident[0:EXPERTS, 0:EXPERTS]).then_inc(table_t, 1)
                with pe.Fori(0, GROUPS - 1) as g:
                    pe_group(pe, g)
                pe_group(pe, GROUPS - 1)

            @block.scalar
            def _(act):
                act.sem_inc(ye_done, 1)
                for i in range(2):
                    act.wait_ge(shared_in, (2 + 4 * i) * DMA)
                    nc.scalar.copy(sw13[0][:, :, i * SHARED : (i + 1) * SHARED], w13_raw[:]).then_inc(split_hi, 1)
                    nc.scalar.copy(sw2[0][:, 3 * i : 3 * i + 3, :], w2_raw[:]).then_inc(split_hi, 1)
                w13_high(act, 0)
                with act.Fori(0, GROUPS - 1) as g:
                    act_group(act, g, False)
                act_group(act, GROUPS - 1, True)

            @block.vector
            def _(dve):
                dve.sem_inc(ehid_done, 1)
                dve.sem_inc(eht_copied, 1)
                dve.sem_inc(hid_done, 2)
                dve.sem_inc(z_read, TT)
                dve.wait_ge(table_t, 2)
                nc.vector.tensor_copy(row_of[:], ps_y[:, 0:EXPERTS]).then_inc(table_done, 1)
                nc.vector.tensor_copy(gate_of[:], ps_y[:, EXPERTS : 2 * EXPERTS]).then_inc(table_done, 1)
                for i in range(2):
                    dve.wait_ge(split_hi, 2 * i + 1)
                    cols = slice(i * SHARED, (i + 1) * SHARED)
                    nc.vector.tensor_tensor(sw13[1][:, :, cols], w13_raw[:], sw13[0][:, :, cols].bitcast(F32), ALU.subtract).then_inc(split_lo, 1)
                    dve.wait_ge(split_hi, 2 * i + 2)
                    tiles = slice(3 * i, 3 * i + 3)
                    nc.vector.tensor_tensor(sw2[1][:, tiles, :], w2_raw[:], sw2[0][:, tiles, :].bitcast(F32), ALU.subtract).then_inc(split_lo, 1)
                w13_low(dve, nc.vector, 0)
                with dve.Fori(0, GROUPS - 1) as g:
                    dve_group(dve, g, False)
                dve_group(dve, GROUPS - 1, True)

            @block.gpsimd
            def _(pool):
                pool.sem_inc(ye_free, 2)
                pool.sem_inc(z_free, TT)
                pool.wait_ge(table_done, 2)
                nc.gpsimd.tensor_copy(rows[0][:], row_of[:, 0:1]).then_inc(row_picked, 1)
                nc.gpsimd.tensor_copy(gates[0][:], gate_of[:, 0:1]).then_inc(gate_picked, 1)
                pool.wait_ge(row_picked, 1)
                nc.gpsimd.indirect_dma_start(
                    xe[0][:], None, x1, bass.IndirectOffsetOnAxis(ap=rows[0][:, 0:1], axis=0),
                    bounds_check=TOKENS + CAP - 1, oob_is_err=False,
                ).then_inc(gathered[0], DMA)
                pool_group(pool, 0, True, False)
                with pool.Fori(1, GROUPS - 1) as g:
                    pool_group(pool, g, False, False)
                pool_group(pool, GROUPS - 1, False, True)


def finish(nc, total, out):
    TT = 4
    GROUPS = TOKENS // (P * TT)
    BUFS = 4
    total_v, out_v = (t[0:TOKENS, :].rearrange("(g p t) d -> g p t d", p=P, t=TT) for t in (total, out))
    with Stage(nc, "fin") as st:
        a = [st.sbuf(f"a{i}", [P, TT, DIM]) for i in range(BUFS)]
        o = [st.sbuf(f"o{i}", [P, TT, DIM]) for i in range(BUFS)]
        stats = [st.sbuf(f"stats{i}", [P, TT, 6]) for i in range(BUFS)]
        mean_var = [st.sbuf(f"mean_var{i}", [P, TT, 2]) for i in range(BUFS)]
        pow_col = st.sbuf("pow_col", [P, TT])
        eps_col = st.sbuf("eps_col", [P, TT])
        zeros = st.sbuf("zeros", [P, TT])
        var_eps = [st.sbuf(f"var_eps{i}", [P, TT]) for i in range(BUFS)]
        neg_mean = [st.sbuf(f"neg_mean{i}", [P, TT]) for i in range(BUFS)]
        rstd = [st.sbuf(f"rstd{i}", [P, TT]) for i in range(BUFS)]
        shift = [st.sbuf(f"shift{i}", [P, TT]) for i in range(BUFS)]
        loaded = [st.sem(f"loaded{i}") for i in range(BUFS)]
        stored = [st.sem(f"stored{i}") for i in range(BUFS)]
        held = st.sem("held")
        stats_done, mv_done, const_done = st.sem("stats_done"), st.sem("mv_done"), st.sem("const_done")
        pool_step, ready, normed = st.sem("pool_step"), st.sem("ready"), st.sem("normed")
        with nc.Block() as block:

            @block.sync
            def _(sp):
                with sp.Fori(0, GROUPS // BUFS) as gg:
                    for i in range(BUFS):
                        g = BUFS * gg + i
                        sp.wait_ge(normed, g + 1)
                        sp.dma_start(a[i][:], total_v[g]).then_inc(loaded[i], DMA)

            @block.vector
            def _(dve):
                with dve.Fori(0, GROUPS // BUFS) as gg:
                    for i in range(BUFS):
                        g = BUFS * gg + i
                        dve.wait_ge(loaded[i], DMA * (gg + 1))
                        for t in range(TT):
                            last = nc.vector.bn_stats(stats[i][:, t, :], a[i][:, t, :])
                        last.then_inc(stats_done, 1)
                        dve.wait_ge(stats_done, g + 1)
                        dve.sem_inc(held, 1)
                        for t in range(TT):
                            last = nc.vector.bn_aggr(mean_var[i][:, t, :], stats[i][:, t, :])
                        last.then_inc(mv_done, 1)

            @block.gpsimd
            def _(pool):
                nc.gpsimd.memset(pow_col[:], -0.5).then_inc(const_done, 1)
                nc.gpsimd.memset(eps_col[:], EPS).then_inc(const_done, 1)
                nc.gpsimd.memset(zeros[:], 0.0).then_inc(const_done, 1)
                pool.wait_ge(const_done, 3)
                with pool.Fori(0, GROUPS // BUFS) as gg:
                    for i in range(BUFS):
                        g = BUFS * gg + i
                        pool.wait_ge(mv_done, g + 1)
                        pool.wait_ge(normed, g + 1)
                        nc.gpsimd.tensor_tensor(var_eps[i][:], mean_var[i][:, :, 1], eps_col[:], ALU.add).then_inc(pool_step, 1)
                        nc.gpsimd.tensor_tensor(neg_mean[i][:], zeros[:], mean_var[i][:, :, 0], ALU.subtract).then_inc(pool_step, 1)
                        pool.wait_ge(pool_step, 3 * g + 2)
                        nc.gpsimd.tensor_tensor(rstd[i][:], var_eps[i][:], pow_col[:], ALU.pow).then_inc(pool_step, 1)
                        pool.wait_ge(pool_step, 3 * g + 3)
                        nc.gpsimd.tensor_tensor(shift[i][:], neg_mean[i][:], rstd[i][:], ALU.mult).then_inc(ready, 1)

            @block.scalar
            def _(act):
                act.sem_inc(normed, BUFS)
                for i in range(BUFS):
                    act.sem_inc(stored[i], DMA)
                with act.Fori(0, GROUPS // BUFS) as gg:
                    for i in range(BUFS):
                        g = BUFS * gg + i
                        act.wait_ge(ready, g + 1)
                        act.wait_ge(stored[i], DMA * (gg + 1))
                        for t in range(TT):
                            last = nc.scalar.activation(o[i][:, t, :], a[i][:, t, :], ACT.Identity, bias=shift[i][:, t : t + 1], scale=rstd[i][:, t : t + 1])
                        last.then_inc(normed, 1)
                        act.wait_ge(normed, g + 1 + BUFS)
                        act.dma_start(out_v[g], o[i][:]).then_inc(stored[i], DMA)
                for i in range(BUFS):
                    act.wait_ge(stored[i], DMA * (GROUPS // BUFS + 1))


def layer(nc, x, x_t, w_qk, w_v, w_out, lambdas, subln, gate_t, w13_t, w2_t, sw13_t, sw2_t, rope, ident, before, empty_slots, out):
    q_parts = nc.dram_tensor("q_parts", (BATCH, 2, 2, SUBS * FREQ, SEQ), F32).ap()
    k_parts = nc.dram_tensor("k_parts", (BATCH, 2, 2, SUBS * FREQ, SEQ), F32).ap()
    v_parts = nc.dram_tensor("v_parts", (BATCH, HEADS, SEQ, 2 * VD), F32).ap()
    x1 = nc.dram_tensor("x1", (TOKENS + CAP, DIM), F32).ap()
    total = nc.dram_tensor("total", (TOKENS + CAP, DIM), F32).ap()
    slots = nc.dram_tensor("slots", (EXPERTS * CAP, 2), F32).ap()
    project(nc, x_t, w_qk, w_v, (rope[0], rope[2]), (rope[1], rope[3]), q_parts, k_parts, v_parts)
    attend(nc, q_parts, k_parts, v_parts, x, lambdas, subln, w_out, gate_t, ident, before, empty_slots, x1, total, slots)
    experts(nc, x1, slots, w13_t, w2_t, sw13_t, sw2_t, ident, total)
    finish(nc, total, out)


def shape_constants():
    inv = 1.0 / 10000.0 ** (np.arange(0, HALF, 2)[: HALF // 2].astype(np.float64) / HALF)
    angle = np.outer(np.arange(SEQ), inv)
    cos = np.tile(np.cos(angle).astype(np.float32).T, (GROUP, 1))
    sin = np.tile(np.sin(angle).astype(np.float32).T, (GROUP, 1))
    plain, cross = np.stack([cos, sin], 1), np.stack([-sin, cos], 1)
    rope = np.stack([plain * np.float32(SCALE), cross * np.float32(SCALE), plain, cross])
    ident = np.eye(P, dtype=np.float32)
    before = np.triu(np.ones((P, P), np.float32), 1)
    empty = np.zeros((EXPERTS * CAP, 2), np.float32)
    empty[:, 0] = TOKENS + np.tile(np.arange(CAP), EXPERTS)
    return {"rope": np.ascontiguousarray(rope), "ident": ident, "before": before, "empty_slots": empty}


def by_rotation(w):
    w = w.reshape(SUBS // GROUP, GROUP, FREQ, 2, DIM)
    return w.transpose(0, 3, 1, 2, 4).reshape(DIM, DIM).T


def kernel(**inputs):
    import concourse.bacc as bacc
    from concourse.bass_utils import run_bass_kernel_spmd

    a = {name.removeprefix("L0_"): np.asarray(value) for name, value in inputs.items()}
    x = a["attn_x"].reshape(TOKENS, DIM)
    sw1, sw3 = a["ffn_sw1"], a["ffn_sw3"]
    full = SHARED // P * P
    arrays = {
        "x": x,
        "x_t": x.T,
        "w_qk": np.concatenate([by_rotation(a["attn_wq"]), by_rotation(a["attn_wk"])], 1),
        "w_v": a["attn_wv"].T,
        "w_out": a["attn_wout"].T,
        "lambdas": np.stack([a[f"attn_lambda_{n}"] for n in ("q1", "q2", "k1", "k2")]),
        "subln": a["attn_subln_weight"][:, None],
        "gate_t": a["ffn_gate_w"].T,
        "w13_t": np.concatenate([a["ffn_w1"].transpose(0, 2, 1), a["ffn_w3"].transpose(0, 2, 1)], 2),
        "w2_t": a["ffn_w2"].transpose(0, 2, 1),
        "sw13_t": np.concatenate([sw1[:full], sw3[:full], sw1[full:], sw3[full:]]).T,
        "sw2_t": a["ffn_sw2"].T,
        **shape_constants(),
    }
    nc = bacc.Bacc("TRN2", target_bir_lowering=False, num_devices=1)
    args = {}
    for name, value in arrays.items():
        arrays[name] = value = np.ascontiguousarray(value)
        args[name] = nc.dram_tensor(f"in_{name}", value.shape, mybir.dt.from_np(value.dtype), kind="ExternalInput").ap()
    out = nc.dram_tensor("out", (TOKENS, DIM), F32, kind="ExternalOutput").ap()
    layer(nc, out=out, **args)
    result = run_bass_kernel_spmd(nc, [{f"in_{name}": value for name, value in arrays.items()}], core_ids=[0])
    return result.results[0]["out"].reshape(BATCH, SEQ, DIM)
```
